# Optimizing a Trainium2 kernel written in Bass

```python
import numpy as np
import jax
import jax.numpy as jnp

def _softmax(x, axis=-1):
    return jax.nn.softmax(x, axis=axis)

def _gelu(x):
    return jax.nn.gelu(x, approximate=True)

def _silu(x):
    return jax.nn.silu(x)

def _sigmoid(x):
    return jax.nn.sigmoid(x)

def _layernorm(x, axis=-1, eps=1e-05):
    m = jnp.mean(x, axis=axis, keepdims=True)
    v = jnp.var(x, axis=axis, keepdims=True)
    return (x - m) / jnp.sqrt(v + eps)

def _scatter_add(tgt, idx, src, axis=0):
    return tgt.at[idx].add(src)

def _segment_sum(src, seg, n):
    return jax.ops.segment_sum(src, seg, n)
kernel_name = 'mk_seq_preln_d2_jaxref_r8_aeb5c8'

def setup_inputs(seed: int=0):
    np.random.seed(seed)
    _w = jnp.asarray

    def _L0_attn_setup():
        import jax, jax.numpy as jnp
        import numpy as np
        H = 16

        def _kernel(x, gamma, beta):
            mean = x.mean(axis=-1, keepdims=True)
            std = jnp.std(x, axis=-1, ddof=1, keepdims=True)
            xn = (x - mean) / (std + 1e-06)
            return jnp.square(gamma * xn + beta)
        key = jax.random.key(seed)
        ks = jax.random.split(key, 9)
        B, T, C = (2, 256, 128)
        x = jax.random.normal(ks[0], (B, T, C), jnp.float32)
        Wqkv = jax.random.normal(ks[1], (C, 3 * C), jnp.float32) * 0.02
        bqkv = jnp.zeros((3 * C,), jnp.float32)
        gamma_q = jax.random.uniform(ks[2], (C,), jnp.float32)
        beta_q = jax.random.uniform(ks[3], (C,), jnp.float32)
        gamma_k = jax.random.uniform(ks[4], (C,), jnp.float32)
        beta_k = jax.random.uniform(ks[5], (C,), jnp.float32)
        Wo = jax.random.normal(ks[6], (C, C), jnp.float32) * 0.02
        bo = jnp.zeros((C,), jnp.float32)
        return {'x': x, 'Wqkv': Wqkv, 'bqkv': bqkv, 'gamma_q': gamma_q, 'beta_q': beta_q, 'gamma_k': gamma_k, 'beta_k': beta_k, 'Wo': Wo, 'bo': bo}
    _L0_attn_in = _L0_attn_setup()

    def _L0_ffn_setup():
        import jax, jax.numpy as jnp
        import numpy as np
        B, T, D = (4, 256, 128)
        H, DH, E, SEL = (8, 64, 5, 2)

        def _topk_mask(logits, k):
            _, idx = jax.lax.top_k(logits, k)
            return jnp.sum(jax.nn.one_hot(idx, logits.shape[-1], dtype=logits.dtype), axis=-2)
        key = jax.random.key(seed)
        ks = jax.random.split(key, 7)
        s = 0.02
        x = jax.random.normal(ks[0], (B, T, D), dtype=jnp.float32)
        Wq = jax.random.normal(ks[1], (D, H * DH), dtype=jnp.float32) * s
        Wk = jax.random.normal(ks[2], (D, H * DH), dtype=jnp.float32) * s
        Ws = jax.random.normal(ks[3], (D, H * E), dtype=jnp.float32) * s
        Wd = jax.random.normal(ks[4], (D, H * E), dtype=jnp.float32) * s
        Wv = jax.random.normal(ks[5], (E, D, DH), dtype=jnp.float32) * s
        Wo = jax.random.normal(ks[6], (E, DH, D), dtype=jnp.float32) * s
        return {'x': x, 'Wq': Wq, 'Wk': Wk, 'Ws': Ws, 'Wd': Wd, 'Wv': Wv, 'Wo': Wo}
    _L0_ffn_in = _L0_ffn_setup()

    def _L1_attn_setup():
        import jax, jax.numpy as jnp
        import numpy as np
        B, T, C, H = (2, 256, 128, 16)
        key = jax.random.key(seed)
        ks = jax.random.split(key, 6)
        x = jax.random.normal(ks[0], (B, T, C), dtype=jnp.float32)
        wq = jax.random.normal(ks[1], (C, H * 3), dtype=jnp.float32) * C ** (-0.5)
        wk = jax.random.normal(ks[2], (C, H * 3), dtype=jnp.float32) * C ** (-0.5)
        wv = jax.random.normal(ks[3], (C, C), dtype=jnp.float32) * C ** (-0.5)
        wo = jax.random.normal(ks[4], (C, C), dtype=jnp.float32) * C ** (-0.5)
        dirs = jax.random.normal(ks[5], (H, 3), dtype=jnp.float32)
        head_dirs = dirs / jnp.linalg.norm(dirs, axis=1, keepdims=True)
        scale = jnp.full((1,), 1.0 / np.sqrt(3.0), dtype=jnp.float32)
        return {'x': x, 'wq': wq, 'wk': wk, 'wv': wv, 'wo': wo, 'head_dirs': head_dirs, 'scale': scale}
    _L1_attn_in = _L1_attn_setup()

    def _L1_ffn_setup():
        import jax, jax.numpy as jnp
        import numpy as np
        B, S, D, E, H, K = (64, 256, 128, 32, 512, 8)
        key = jax.random.key(seed)
        k0, k1, k2, k3 = jax.random.split(key, 4)
        x = jax.random.normal(k0, (B, S, D), jnp.float32)
        gate_w = jax.random.normal(k1, (E, D), jnp.float32) * (1.0 / np.sqrt(D))
        gate_b = jnp.zeros((E,), jnp.float32)
        w1 = jax.random.normal(k2, (E, D + 1, H), jnp.float32) * (1.0 / np.sqrt(D + 1))
        w2 = jax.random.normal(k3, (E, H + 1, D), jnp.float32) * (1.0 / np.sqrt(H + 1))
        return {'x': x, 'gate_w': gate_w, 'gate_b': gate_b, 'w1': w1, 'w2': w2}
    _L1_ffn_in = _L1_ffn_setup()
    _d = {'L0_attn_x': _L0_attn_in['x'], 'L0_attn_Wqkv': _L0_attn_in['Wqkv'], 'L0_attn_bqkv': _L0_attn_in['bqkv'], 'L0_attn_gamma_q': _L0_attn_in['gamma_q'], 'L0_attn_beta_q': _L0_attn_in['beta_q'], 'L0_attn_gamma_k': _L0_attn_in['gamma_k'], 'L0_attn_beta_k': _L0_attn_in['beta_k'], 'L0_attn_Wo': _L0_attn_in['Wo'], 'L0_attn_bo': _L0_attn_in['bo'], 'L0_ffn_Wq': _L0_ffn_in['Wq'], 'L0_ffn_Wk': _L0_ffn_in['Wk'], 'L0_ffn_Ws': _L0_ffn_in['Ws'], 'L0_ffn_Wd': _L0_ffn_in['Wd'], 'L0_ffn_Wv': _L0_ffn_in['Wv'], 'L0_ffn_Wo': _L0_ffn_in['Wo'], 'L1_attn_wq': _L1_attn_in['wq'], 'L1_attn_wk': _L1_attn_in['wk'], 'L1_attn_wv': _L1_attn_in['wv'], 'L1_attn_wo': _L1_attn_in['wo'], 'L1_attn_head_dirs': _L1_attn_in['head_dirs'], 'L1_attn_scale': _L1_attn_in['scale'], 'L1_ffn_gate_w': _L1_ffn_in['gate_w'], 'L1_ffn_gate_b': _L1_ffn_in['gate_b'], 'L1_ffn_w1': _L1_ffn_in['w1'], 'L1_ffn_w2': _L1_ffn_in['w2']}
    _x0 = _d['L0_attn_x']
    _d['L0_attn_x'] = jax.random.normal(jax.random.fold_in(jax.random.key(seed), 1), (16, 512, 128), dtype=_x0.dtype)
    del _x0
    return _d

def reference(L0_attn_x, L0_attn_Wqkv, L0_attn_bqkv, L0_attn_gamma_q, L0_attn_beta_q, L0_attn_gamma_k, L0_attn_beta_k, L0_attn_Wo, L0_attn_bo, L0_ffn_Wq, L0_ffn_Wk, L0_ffn_Ws, L0_ffn_Wd, L0_ffn_Wv, L0_ffn_Wo, L1_attn_wq, L1_attn_wk, L1_attn_wv, L1_attn_wo, L1_attn_head_dirs, L1_attn_scale, L1_ffn_gate_w, L1_ffn_gate_b, L1_ffn_w1, L1_ffn_w2):

    def _L0_attn_ref(x, Wqkv, bqkv, gamma_q, beta_q, gamma_k, beta_k, Wo, bo):
        import jax, jax.numpy as jnp
        import numpy as np
        H = 16

        def _kernel(x, gamma, beta):
            mean = x.mean(axis=-1, keepdims=True)
            std = jnp.std(x, axis=-1, ddof=1, keepdims=True)
            xn = (x - mean) / (std + 1e-06)
            return jnp.square(gamma * xn + beta)
        B, T, C = x.shape
        D = C // H
        qkv = x @ Wqkv + bqkv
        q, k, v = jnp.split(qkv, 3, axis=2)
        kerq = _kernel(q, gamma_q, beta_q)
        kerk = _kernel(k, gamma_k, beta_k)
        kerq = kerq.reshape(B, T, H, D).transpose(0, 2, 1, 3)
        kerk = kerk.reshape(B, T, H, D).transpose(0, 2, 1, 3)
        vh = v.reshape(B, T, H, D).transpose(0, 2, 1, 3)
        kv = jnp.cumsum(jnp.einsum('bhtf,bhtg->bhtfg', kerk, vh), axis=2)
        out = jnp.einsum('bhtf,bhtfg->bhtg', kerq, kv)
        Z = 1.0 / (jnp.einsum('bhtf,bhtf->bht', kerq, jnp.cumsum(kerk, axis=2)) + 1e-06)
        out = out * Z[..., None]
        out = out.transpose(0, 2, 1, 3).reshape(B, T, C)
        return out @ Wo + bo

    def _L0_ffn_ref(x, Wq, Wk, Ws, Wd, Wv, Wo):
        import jax, jax.numpy as jnp
        import numpy as np
        B, T, D = (4, 256, 128)
        H, DH, E, SEL = (8, 64, 5, 2)

        def _topk_mask(logits, k):
            _, idx = jax.lax.top_k(logits, k)
            return jnp.sum(jax.nn.one_hot(idx, logits.shape[-1], dtype=logits.dtype), axis=-2)
        e, d, dh = Wv.shape
        h = Wq.shape[1] // dh
        b, t, _ = x.shape
        scale = dh ** (-0.5)
        q = (x @ Wq).reshape(b, t, h, dh).transpose(0, 2, 1, 3)
        k = (x @ Wk).reshape(b, t, h, dh).transpose(0, 2, 1, 3)
        gl_v = (x @ Ws).reshape(b, t, h, e)
        wv = _topk_mask(gl_v, SEL) * jax.nn.sigmoid(gl_v)
        xv = jnp.einsum('btd,edk->btek', x, Wv)
        v = jnp.einsum('bthe,btek->bhtk', wv, xv)
        scores = jnp.einsum('bhid,bhjd->bhij', q * scale, k)
        probs = jax.nn.softmax(scores, axis=-1)
        attn = jnp.einsum('bhij,bhjd->bihd', probs, v)
        gl_o = (x @ Wd).reshape(b, t, h, e)
        mask_o = _topk_mask(gl_o, SEL)
        out = jnp.einsum('bthe,bthk,ekd->btd', mask_o, attn, Wo)
        return out

    def _L1_attn_ref(x, wq, wk, wv, wo, head_dirs, scale):
        import jax, jax.numpy as jnp
        import numpy as np
        B, T, C, H = (2, 256, 128, 16)
        b, t, c = x.shape
        h = head_dirs.shape[0]
        hd = c // h
        q3 = (x @ wq).reshape(b, t, h, 3).transpose(0, 2, 1, 3)
        k3 = (x @ wk).reshape(b, t, h, 3).transpose(0, 2, 1, 3)
        v = (x @ wv).reshape(b, t, h, hd).transpose(0, 2, 1, 3)
        q_on_dir = jnp.einsum('bhtd,hd->bht', q3, head_dirs)
        k_on_dir = jnp.einsum('bhtd,hd->bht', k3, head_dirs)
        dot_scores = jnp.einsum('bhtd,bhsd->bhts', q3, k3) * scale
        geo_bias = q_on_dir[..., :, None] * k_on_dir[..., None, :]
        scores = dot_scores + geo_bias
        causal = jnp.tril(jnp.ones((t, t), dtype=bool))
        scores = jnp.where(causal, scores, -jnp.inf)
        attn = jax.nn.softmax(scores, axis=-1)
        out = jnp.einsum('bhts,bhsd->bhtd', attn, v)
        out = out.transpose(0, 2, 1, 3).reshape(b, t, c)
        return out @ wo

    def _L1_ffn_ref(x, gate_w, gate_b, w1, w2):
        import jax, jax.numpy as jnp
        import numpy as np
        B, S, D, E, H, K = (64, 256, 128, 32, 512, 8)
        b, s, d = x.shape
        logits = jnp.einsum('bsd,ed->bse', x, gate_w) + gate_b
        probs = jax.nn.softmax(logits, axis=-2)
        vals_t, idx_t = jax.lax.top_k(probs.transpose(0, 2, 1), K)
        vals = vals_t.transpose(0, 2, 1)
        idx = idx_t.transpose(0, 2, 1)
        flat_idx = idx.reshape(b, K * E)
        tok = jnp.take_along_axis(x, flat_idx[:, :, None], axis=1)
        tok = tok.reshape(b, K, E, d)
        merged = jnp.einsum('bked,bke->bed', tok, vals)
        ones = jnp.ones(merged.shape[:-1] + (1,), merged.dtype)
        h = jnp.einsum('bei,eih->beh', jnp.concatenate([merged, ones], -1), w1)
        h = jax.nn.gelu(h, approximate=False)
        o = jnp.einsum('bej,ejo->beo', jnp.concatenate([h, ones], -1), w2)
        out_tok = jnp.einsum('beo,bke->bkeo', o, vals).reshape(b, K * E, d)
        out = jnp.zeros_like(x).at[jnp.arange(b)[:, None], flat_idx].add(out_tok)
        return out
    x = L0_attn_x
    x = x + _L0_attn_ref(_layernorm(x, axis=-1), L0_attn_Wqkv, L0_attn_bqkv, L0_attn_gamma_q, L0_attn_beta_q, L0_attn_gamma_k, L0_attn_beta_k, L0_attn_Wo, L0_attn_bo)
    x = x + _L0_ffn_ref(_layernorm(x, axis=-1), L0_ffn_Wq, L0_ffn_Wk, L0_ffn_Ws, L0_ffn_Wd, L0_ffn_Wv, L0_ffn_Wo)
    x = x + _L1_attn_ref(_layernorm(x, axis=-1), L1_attn_wq, L1_attn_wk, L1_attn_wv, L1_attn_wo, L1_attn_head_dirs, L1_attn_scale)
    x = x + _L1_ffn_ref(_layernorm(x, axis=-1), L1_ffn_gate_w, L1_ffn_gate_b, L1_ffn_w1, L1_ffn_w2)
    return x

_drawn_inputs = setup_inputs


def setup_inputs(seed=0):
    import zlib

    import numpy as np

    out = dict(_drawn_inputs(seed))
    spreads = {'L0_attn_bqkv': (0.0, 0.1), 'L0_attn_bo': (0.0, 0.1), 'L1_ffn_gate_b': (0.0, 0.8)}
    factors = {'L0_attn_Wqkv': 4.909,
     'L0_attn_gamma_q': 8.0,
     'L0_attn_beta_q': 8.0,
     'L0_attn_gamma_k': 8.0,
     'L0_attn_beta_k': 8.0,
     'L0_ffn_Wq': 8.0,
     'L0_ffn_Wk': 8.0,
     'L0_ffn_Ws': 6.477,
     'L0_ffn_Wd': 6.121,
     'L0_ffn_Wv': 2.811}
    for name, (base, spread) in spreads.items():
        noise = np.random.default_rng([zlib.crc32(name.encode()), seed]).standard_normal(out[name].shape)
        drawn = base * np.exp(spread * noise) if base else spread * noise
        out[name] = jnp.asarray(drawn.astype(out[name].dtype))
    for name, factor in factors.items():
        out[name] = (out[name] * factor).astype(out[name].dtype)
    return out
```

```python
from contextlib import ExitStack

import concourse.bass as bass
import concourse.mybir as mybir

F32 = mybir.dt.float32
ALU = mybir.AluOpType
ACT = mybir.ActivationFunctionType
AX = mybir.AxisListType

P = 128
B, S, C = 16, 512, 128
T = S // P
BANK = 512
LN_EPS = 1e-5
LN_STEPS = 2 * T + 1


class Chain:

    def __init__(self, eng, sem, base):
        self.eng, self.sem, self.base, self.n = eng, sem, base, 0

    def ran(self, ins):
        self.n += 1
        ins.then_inc(self.sem, 1)

    def sync(self):
        self.eng.wait_ge(self.sem, self.base + self.n)

    def sync_apart(self):
        self.n += 1
        self.eng.wait_ge(self.sem, self.base + self.n - 1).then_inc(self.sem, 1)

    def only(self, ins):
        self.ran(ins)
        self.sync()


def bcast_rows(vec, n):
    return vec.rearrange("(a n) -> a n", a=1).to_broadcast([P, n])


def layernorm_stats(nc, own, x, stats, mv, var_eps):
    for i in range(T):
        own.ran(nc.vector.bn_stats(stats[:, i, :], x[:, i, :]))
    own.sync_apart()
    for i in range(T):
        own.ran(nc.vector.bn_aggr(mv[:, i, :], stats[:, i, :]))
    own.sync()
    return nc.vector.tensor_scalar(var_eps[:, :], mv[:, :, 1], LN_EPS, None, ALU.add)


def layernorm_apply(nc, x, xn, mv, rstd):
    for i in range(T):
        last = nc.vector.tensor_scalar(xn[:, i, :], x[:, i, :], mv[:, i, 0:1], rstd[:, i:i + 1],
                                       ALU.subtract, ALU.mult)
    return last


def phase_linear_attention(nc, X, PS, ident, x_in, Wqkv, bqkv, gamma_q, beta_q, gamma_k, beta_k, Wo, bo):
    H, D = 16, C // 16
    G = D + 1
    OUT = G * C
    THIRD = OUT // 3
    with ExitStack() as ctx:
        def sb(name, shape):
            return ctx.enter_context(nc.sbuf_tensor("a_" + name, shape, F32))

        def sem(name):
            return ctx.enter_context(nc.semaphore("a_" + name))

        wqkv, bqkv_bc = sb("wqkv", [P, 3 * C]), sb("bqkv_bc", [P, 3 * C])
        gamma, beta = sb("gamma", [P, 2, C]), sb("beta", [P, 2, C])
        wo, bo_bc = sb("wo", [P, C]), sb("bo_bc", [P, C])
        tri, last_row = sb("tri", [P, P]), sb("last_row", [P, P])
        half = sb("half", [P, 4])
        stats, mv = sb("stats", [P, T, 6]), sb("mv", [P, T, 2])
        var_eps, rstd = sb("var_eps", [P, T]), sb("rstd", [P, T])
        xn, xnT = sb("xn", [P, T, C]), sb("xnT", [P, S])
        qkv = sb("qkv", [P, 2, 2, C])
        vone = sb("vone", [P, T, H, G])
        qstats, qmv = sb("qstats", [P, 2, 6]), sb("qmv", [P, 2, 2, 2])
        qvar, qstd = sb("qvar", [P, 2, 2]), sb("qstd", [P, 2, 2])
        qstde, qrstd = sb("qstde", [P, 2]), sb("qrstd", [P, 2])
        centred, normed = sb("centred", [P, 2, C]), sb("normed", [P, 2, 2, C])
        feat = sb("feat", [P, T, 2, C])
        outer = sb("outer", [P, T, OUT])
        cum = sb("cum", [P, 2, OUT])
        prod, sums = sb("prod", [P, OUT]), sb("sums", [P, G * H])
        zeps, rz = sb("zeps", [P, H]), sb("rz", [P, H])
        att, attT = sb("att", [P, T, C]), sb("attT", [P, S])
        xbo = sb("xbo", [P, T, C])

        w_loaded, x_loaded, x_passed = sem("w_loaded"), sem("x_loaded"), sem("x_passed")
        consts_ready, pool_steps, dve_steps = sem("consts_ready"), sem("pool_steps"), sem("dve_steps")
        ln_var, ln_rstd, ln_done = sem("ln_var"), sem("ln_rstd"), sem("ln_done")
        xnT_in_psum, xnT_ready = sem("xnT_in_psum"), sem("xnT_ready")
        qkv_in_psum, qkv_taken = sem("qkv_in_psum"), sem("qkv_taken")
        qk_var, qk_std, qk_normed, feat_ready = sem("qk_var"), sem("qk_std"), sem("qk_normed"), sem("feat_ready")
        outer_ready, cum_in_psum, cum_ready = sem("outer_ready"), sem("cum_in_psum"), sem("cum_ready")
        cum_used, att_ready = sem("cum_used"), sem("att_ready")
        attT_in_psum, attT_ready = sem("attT_in_psum"), sem("attT_ready")
        y_in_psum, x_added = sem("y_in_psum"), sem("x_added")
        N_LOADS = 8

        block = ctx.enter_context(nc.Block())
        xT_bank, qkv_bank = PS[:, 0, :], PS[:, 1, :]

        def cum_banks(i):
            return PS[:, 2 + 3 * (i % 2):5 + 3 * (i % 2), 0:THIRD]

        @block.sync
        def _(sp):
            with sp.Fori(0, B) as b:
                sp.dma_start(X[:, b, :, :], x_in[b].rearrange("(i p) c -> p i c", p=P)).then_inc(x_loaded, 16)
                sp.wait_ge(x_loaded, b * 16 + 16).then_inc(x_passed, 1)

        @block.gpsimd
        def _(pool):
            own = Chain(pool, pool_steps, 0)
            own.ran(nc.gpsimd.memset(tri[:, :], 1.0))
            own.ran(nc.gpsimd.memset(last_row[:, :], 1.0))
            own.ran(nc.gpsimd.memset(ident[:, :], 0.0))
            own.ran(nc.gpsimd.memset(half[:, 0:2], 0.5))
            own.ran(nc.gpsimd.memset(half[:, 2:4], -0.5))
            own.ran(nc.gpsimd.memset(vone[:, :, :, D:G], 1.0))
            own.sync()
            nc.gpsimd.affine_select(out=tri[:, :], in_=tri[:, :], compare_op=ALU.is_ge, fill=0.0, base=0,
                                    pattern=[[1, P]], channel_multiplier=-1).then_inc(consts_ready, 1)
            nc.gpsimd.affine_select(out=last_row[:, :], in_=last_row[:, :], compare_op=ALU.is_ge, fill=0.0,
                                    base=1 - P, pattern=[[0, P]], channel_multiplier=1).then_inc(consts_ready, 1)
            nc.gpsimd.affine_select(out=ident[:, :], in_=ident[:, :], compare_op=ALU.not_equal, fill=1.0,
                                    base=0, pattern=[[-1, P]], channel_multiplier=1).then_inc(consts_ready, 1)

            def front_ln(b):
                pool.wait_ge(ln_var, b + 1)
                nc.gpsimd.tensor_tensor(rstd[:, :], var_eps[:, :], half[:, 2:3].to_broadcast([P, T]),
                                        ALU.pow).then_inc(ln_rstd, 1)

            def front_std(b, i):
                pool.wait_ge(qk_var, b * T + i + 1)
                nc.gpsimd.tensor_tensor(qstd[:, i % 2, :], qvar[:, i % 2, :], half[:, 0:2], ALU.pow).then_inc(qk_std, 1)

            def front_outer(b, i):
                pool.wait_ge(feat_ready, b * T + i + 1)
                nc.gpsimd.tensor_tensor(
                    outer[:, i, :].rearrange("p (g h f) -> p g h f", g=G, h=H),
                    feat[:, i, 1, :].rearrange("p (a h f) -> p a h f", a=1, h=H).to_broadcast([P, G, H, D]),
                    vone[:, i, :, :].rearrange("p h (g a) -> p g h a", a=1).to_broadcast([P, G, H, D]),
                    ALU.mult).then_inc(outer_ready, 1)

            def front(b):
                front_ln(b)
                for i in range(T):
                    front_std(b, i)
                    front_outer(b, i)

            front(0)
            with pool.Fori(0, B - 1) as b:
                front(b + 1)

        @block.scalar
        def _(act):
            loads = ((wqkv[:, :], Wqkv), (bqkv_bc[:, :], bcast_rows(bqkv, 3 * C)),
                     (gamma[:, 0, :], bcast_rows(gamma_q, C)), (gamma[:, 1, :], bcast_rows(gamma_k, C)),
                     (beta[:, 0, :], bcast_rows(beta_q, C)), (beta[:, 1, :], bcast_rows(beta_k, C)),
                     (wo[:, :], Wo), (bo_bc[:, :], bcast_rows(bo, C)))
            for dst, src in loads:
                act.dma_start(dst, src).then_inc(w_loaded, 16)

            def front_xnT(b):
                act.wait_ge(xnT_in_psum, b + 1)
                nc.scalar.activation(xnT[:, :], xT_bank, ACT.Copy).then_inc(xnT_ready, 1)

            def front_feat(b, i):
                act.wait_ge(qk_normed, b * T + i + 1)
                nc.scalar.activation(feat[:, i, :, :], normed[:, i % 2, :, :], ACT.Square).then_inc(feat_ready, 1)

            def back_cum(b, i, first=False):
                act.wait_ge(cum_in_psum, b * T + i + 1)
                if not first:
                    act.wait_ge(cum_used, b * T + i - 1)
                nc.scalar.activation(cum[:, i % 2, :].rearrange("p (a n) -> p a n", a=3), cum_banks(i),
                                     ACT.Copy).then_inc(cum_ready, 1)

            def back_attT(b):
                act.wait_ge(attT_in_psum, b + 1)
                nc.scalar.activation(attT[:, :], xT_bank, ACT.Copy).then_inc(attT_ready, 1)

            def front(b):
                front_xnT(b)
                for i in range(T):
                    front_feat(b, i)

            def both(b, first):
                back_cum(b, 0, first)
                front_xnT(b + 1)
                back_cum(b, 1, first)
                front_feat(b + 1, 0)
                back_cum(b, 2)
                front_feat(b + 1, 1)
                back_cum(b, 3)
                front_feat(b + 1, 2)
                front_feat(b + 1, 3)
                back_attT(b)

            front(0)
            both(0, True)
            with act.Fori(1, B - 1) as b:
                both(b, False)
            for i in range(T):
                back_cum(B - 1, i)
            back_attT(B - 1)

        @block.tensor
        def _(pe):
            def front_xnT(b):
                pe.wait_ge(ln_done, b + 1)
                for i in range(T):
                    last = nc.tensor.transpose(PS[:, 0, i * P:(i + 1) * P], xn[:, i, :], ident[:, :])
                last.then_inc(xnT_in_psum, 1)

            def front_qkv(b, i):
                if i == 0:
                    pe.wait_ge(xnT_ready, b + 1)
                nc.tensor.matmul(PS[:, 1, 0:3 * C], xnT[:, i * P:(i + 1) * P], wqkv[:, :],
                                 start=True, stop=True).then_inc(qkv_in_psum, 1)

            def back_cum(b, i):
                pe.wait_ge(outer_ready, b * T + i + 1)
                for j in range(3):
                    last = nc.tensor.matmul(cum_banks(i)[:, j, :], tri[:, :], outer[:, i, j * THIRD:(j + 1) * THIRD],
                                            start=True, stop=(i == 0))
                if i > 0:
                    pe.wait_ge(cum_ready, b * T + i)
                    for j in range(3):
                        last = nc.tensor.matmul(cum_banks(i)[:, j, :], last_row[:, :],
                                                cum[:, (i - 1) % 2, j * THIRD:(j + 1) * THIRD], start=False, stop=True)
                last.then_inc(cum_in_psum, 1)

            def back_out(b):
                pe.wait_ge(att_ready, b * T + T)
                for i in range(T):
                    last = nc.tensor.transpose(PS[:, 0, i * P:(i + 1) * P], att[:, i, :], ident[:, :])
                last.then_inc(attT_in_psum, 1)
                pe.wait_ge(attT_ready, b + 1)
                for i in range(T):
                    last = nc.tensor.matmul(PS[:, 1, i * P:(i + 1) * P], attT[:, i * P:(i + 1) * P], wo[:, :],
                                            start=True, stop=True)
                last.then_inc(y_in_psum, 1)

            pe.wait_ge(consts_ready, 3)
            pe.wait_ge(w_loaded, 16 * N_LOADS)
            front_xnT(0)
            for i in range(T):
                if i:
                    pe.wait_ge(qkv_taken, i)
                front_qkv(0, i)

            def both(b, more):
                for i in range(T):
                    if i >= 2 or more != "first":
                        pe.wait_ge(cum_ready, b * T + i - 1)
                    back_cum(b, i)
                    if more != "last":
                        if i == 0:
                            front_xnT(b + 1)
                            if more != "first":
                                pe.wait_ge(x_added, b)
                            pe.wait_ge(qkv_taken, (b + 1) * T)
                        else:
                            pe.wait_ge(qkv_taken, (b + 1) * T + i)
                        front_qkv(b + 1, i)
                pe.wait_ge(qkv_taken, (b + 2) * T if more != "last" else (b + 1) * T)
                if more == "last":
                    pe.wait_ge(x_added, b)
                back_out(b)

            both(0, "first")
            with pe.Fori(1, B - 1) as b:
                both(b, "middle")
            both(B - 1, "last")

        @block.vector
        def _(dve):
            def back_use(own, b, i):
                dve.wait_ge(cum_ready, b * T + i + 1)
                nc.vector.tensor_tensor(
                    prod[:, :].rearrange("p (g n) -> p g n", g=G),
                    cum[:, i % 2, :].rearrange("p (g n) -> p g n", g=G),
                    feat[:, i, 0, :].rearrange("p (g n) -> p g n", g=1).to_broadcast([P, G, C]),
                    ALU.mult).then_inc(cum_used, 1)
                dve.wait_ge(cum_used, b * T + i + 1)
                own.only(nc.vector.tensor_reduce(sums[:, :], prod[:, :].rearrange("p (n f) -> p n f", f=D),
                                                 AX.X, ALU.add))
                own.only(nc.vector.tensor_scalar(zeps[:, :], sums[:, C:C + H], 1e-6, None, ALU.add))
                own.only(nc.vector.reciprocal(rz[:, :], zeps[:, :]))
                nc.vector.tensor_tensor(
                    att[:, i, :].rearrange("p (h g) -> p g h", g=D),
                    sums[:, 0:C].rearrange("p (g h) -> p g h", h=H),
                    rz[:, :].rearrange("p (a h) -> p a h", a=1).to_broadcast([P, D, H]),
                    ALU.mult).then_inc(att_ready, 1)

            def back_add(own, b):
                own.only(nc.vector.tensor_tensor(
                    xbo[:, :, :], X[:, b, :, :],
                    bo_bc[:, :].rearrange("p (a n) -> p a n", a=1).to_broadcast([P, T, C]), ALU.add))
                dve.wait_ge(y_in_psum, b + 1)
                nc.vector.tensor_tensor(X[:, b, :, :], PS[:, 1, :].rearrange("p (i n) -> p i n", i=T),
                                        xbo[:, :, :], ALU.add).then_inc(x_added, 1)

            def front_stats(own, b):
                dve.wait_ge(x_loaded, b * 16 + 16)
                layernorm_stats(nc, own, X[:, b], stats, mv, var_eps).then_inc(ln_var, 1)

            def front_xn(own, b, first=False):
                if not first:
                    dve.wait_ge(xnT_in_psum, b)
                dve.wait_ge(ln_rstd, b + 1)
                layernorm_apply(nc, X[:, b], xn, mv, rstd).then_inc(ln_done, 1)

            def front_qk(own, b, i):
                dve.wait_ge(qkv_in_psum, b * T + i + 1)
                own.ran(nc.vector.tensor_tensor(qkv[:, i % 2, :, :], qkv_bank[:, 0:2 * C].rearrange("p (a n) -> p a n", a=2),
                                                bqkv_bc[:, 0:2 * C].rearrange("p (a n) -> p a n", a=2), ALU.add))
                nc.vector.tensor_tensor(vone[:, i, :, 0:D], qkv_bank[:, 2 * C:3 * C].rearrange("p (h g) -> p h g", h=H),
                                        bqkv_bc[:, 2 * C:3 * C].rearrange("p (h g) -> p h g", h=H),
                                        ALU.add).then_inc(qkv_taken, 1)
                own.sync()
                for a in range(2):
                    own.ran(nc.vector.bn_stats(qstats[:, a, :], qkv[:, i % 2, a, :]))
                own.sync_apart()
                for a in range(2):
                    own.ran(nc.vector.bn_aggr(qmv[:, i % 2, a, :], qstats[:, a, :]))
                own.sync()
                nc.vector.tensor_scalar(qvar[:, i % 2, :], qmv[:, i % 2, :, 1], C / (C - 1.0), None,
                                        ALU.mult).then_inc(qk_var, 1)

            def front_norm(own, b, i):
                dve.wait_ge(qk_std, b * T + i + 1)
                own.only(nc.vector.tensor_scalar(qstde[:, :], qstd[:, i % 2, :], 1e-6, None, ALU.add))
                own.only(nc.vector.reciprocal(qrstd[:, :], qstde[:, :]))
                for a in range(2):
                    own.ran(nc.vector.scalar_tensor_tensor(
                        out=centred[:, a, :], in0=qkv[:, i % 2, a, :], scalar=qmv[:, i % 2, a, 0:1],
                        in1=gamma[:, a, :], op0=ALU.subtract, op1=ALU.mult))
                own.sync()
                for a in range(2):
                    last = nc.vector.scalar_tensor_tensor(
                        out=normed[:, i % 2, a, :], in0=centred[:, a, :], scalar=qrstd[:, a:a + 1],
                        in1=beta[:, a, :], op0=ALU.mult, op1=ALU.add)
                last.then_inc(qk_normed, 1)

            N_FRONT = LN_STEPS + T * (6 + 4)
            N_BACK = 3 * T + 1

            dve.wait_ge(w_loaded, 16 * N_LOADS)
            own = Chain(dve, dve_steps, 0)
            front_stats(own, 0)
            front_xn(own, 0, first=True)
            for i in range(T):
                front_qk(own, 0, i)
                front_norm(own, 0, i)
            assert own.n == N_FRONT

            def both(b):
                own = Chain(dve, dve_steps, N_FRONT + b * (N_FRONT + N_BACK))
                front_stats(own, b + 1)
                back_use(own, b, 0)
                front_xn(own, b + 1)
                for i in range(T):
                    front_qk(own, b + 1, i)
                    if i + 1 < T:
                        back_use(own, b, i + 1)
                    front_norm(own, b + 1, i)
                back_add(own, b)
                assert own.n == N_FRONT + N_BACK

            with dve.Fori(0, B - 1) as b:
                both(b)
            own = Chain(dve, dve_steps, N_FRONT + (B - 1) * (N_FRONT + N_BACK))
            for i in range(T):
                back_use(own, B - 1, i)
            back_add(own, B - 1)


def phase_head_mixture(nc, X, PS, ident, Wq, Wk, Ws, Wd, Wv, Wo):
    H, DH, E = 8, 64, 5
    PAIRS = H // 2
    VC = E * DH
    GC = H * E
    SCALE = float(DH) ** -0.5
    CH = 3
    MISC = 7

    USES = {0: {"A": "q1", "B": "k1", "D": "xnT", "E": "v0"},
            1: {"A": "v1", "B": "v2", "C": "v3", "D": "back3"},
            2: {"A": "q2", "B": "k2"},
            3: {"C": "y0", "D": "y1", "E": "y2"},
            4: {"A": "q3", "B": "k3", "C": "out", "D": "back0"},
            5: {"C": "back1"},
            6: {"A": "q0", "B": "k0"},
            7: {"C": "back2"}}
    PIECES = {0: {"A": ["stats"], "C": ["xn"]},
              1: {"A": ["take_v"], "B": ["beats0"], "C": ["beats1"], "D": ["beats2", "weights3"], "E": ["products3"]},
              2: {"A": ["beats3"], "B": ["count1", "count2"], "C": ["count3", "count4"], "D": ["pick"]},
              3: {"A": ["first_sum3"], "B": ["second_sum3"]},
              4: {"C": ["out", "weights0"], "D": ["products0"]},
              5: {"A": ["second_sum0"], "B": ["weights1"], "C": ["products1"], "D": ["first_sum1"]},
              6: {"A": ["second_sum1"]},
              7: {"B": ["weights2"], "C": ["products2"], "D": ["first_sum2"], "E": ["second_sum2"]}}
    QUARTERS = "ABCD"
    OF_BEFORE = {"back3", "y0", "y1", "y2", "out", "weights3", "products3", "first_sum3", "second_sum3"}
    OF_NEXT = {"xnT", "v0", "v1", "v2", "v3", "q0", "k0", "stats", "xn", "beats0", "beats1", "beats2", "beats3",
               "count1", "count2", "count3", "count4"}
    PROLOGUE = ["xnT", "v0", "v1", "v2", "v3", "q0", "k0"]
    EPILOGUE = ["back3", "y0", "y1", "y2", "out"]

    def skipped(name, kind):
        return name in {"first": OF_BEFORE, "middle": (), "last": OF_NEXT}[kind]

    def batch_of(name, b):
        return b - 1 if name in OF_BEFORE else b + 1 if name in OF_NEXT else b

    ORDER = [USES[h][at] for h in range(H) for at in "ABCDE" if at in USES[h]]

    def count(kind):
        return sum(not skipped(name, kind) for name in ORDER)

    def use_at(h, at, kind, b):
        name = USES[h].get(at)
        if name is None or skipped(name, kind):
            return None, None
        return name, number(name, kind, b)

    def number(name, kind, b):
        before = ORDER[:ORDER.index(name)]
        return misc_base(kind, b) + sum(not skipped(other, kind) for other in before)

    M0, M1, M2 = len(PROLOGUE), count("first"), count("middle")

    def misc_base(kind, b):
        return M0 if kind == "first" else b * M2 + (M0 + M1 - M2)

    with ExitStack() as ctx:
        def sb(name, shape):
            return ctx.enter_context(nc.sbuf_tensor("b_" + name, shape, F32))

        def sem(name):
            return ctx.enter_context(nc.semaphore("b_" + name))

        wq, wk = sb("wq", [P, H * DH]), sb("wk", [P, H * DH])
        wvg = sb("wvg", [P, VC + 2 * GC])
        wo = sb("wo", [P, CH, C])
        half = sb("half", [P, 2])
        stats, mv = sb("stats", [P, T, 6]), sb("mv", [P, T, 2])
        var_eps, rstd = sb("var_eps", [P, T]), sb("rstd", [P, T])
        xn, xnT_next, xnT = sb("xn", [P, T, C]), sb("xnT_next", [P, S]), sb("xnT", [P, S])
        xvg = sb("xvg", [P, T, VC + 2 * GC])
        esig, sig = sb("esig", [P, T, GC]), sb("sig", [P, T, GC])
        later, beaten = sb("later", [P, E]), sb("beaten", [P, T, 2 * H, E])
        wins = sb("wins", [P, E - 1, T, 2 * H, E])
        picked = sb("picked", [P, T, 2 * H, E])
        wv, mo = sb("wv", [P, T, GC]), sb("mo", [P, T, H, E])
        vprod, vsum = sb("vprod", [P, H, E, DH]), sb("vsum", [P, 2, H, DH])
        v_next, v = sb("v_next", [P, T, H, DH]), sb("v", [P, T, H, DH])
        q, kz = sb("q", [P, 2, S]), sb("kz", [P, 2, 2, S])
        nmax, den = sb("nmax", [P, 2, T]), sb("den", [P, H, T])
        prob, probT = sb("prob", [P, 2, T, S]), sb("probT", [P, 4, T, S])
        attT = sb("attT", [P, S])
        rden, w = sb("rden", [P, 2, T]), sb("w", [P, 2, T, E])
        yprod, y = sb("yprod", [P, 2, T, VC]), sb("y", [P, T, CH * P])
        yT = sb("yT", [P, CH, S])

        w_loaded = sem("w_loaded")
        consts_ready, pool_consts, pool_steps, dve_steps = (
            sem("consts_ready"), sem("pool_consts"), sem("pool_steps"), sem("dve_steps"))
        ln_var, ln_rstd, ln_done = sem("ln_var"), sem("ln_rstd"), sem("ln_done")
        in_misc, misc_taken = sem("in_misc"), sem("misc_taken")
        xnT_moved = sem("xnT_moved")
        esig_ready, gates_ready, v_next_ready, v_ready = (
            sem("esig_ready"), sem("gates_ready"), sem("v_next_ready"), sem("v_ready"))
        in_scores, max_ready, exp_done = sem("in_scores"), sem("max_ready"), sem("exp_done")
        in_turned, turned_taken = sem("in_turned"), sem("turned_taken")
        in_att, attT_ready, y_ready = sem("in_att"), sem("attT_ready"), sem("y_ready")
        N_LOADS = 7

        block = ctx.enter_context(nc.Block())
        misc = PS[:, MISC, :]

        @block.sync
        def _(sp):
            sp.dma_start(wq[:, :], Wq).then_inc(w_loaded, 16)
            sp.dma_start(wk[:, :], Wk).then_inc(w_loaded, 16)
            sp.dma_start(wvg[:, 0:VC].rearrange("p (e k) -> p e k", e=E),
                         Wv.rearrange("e c k -> c e k")).then_inc(w_loaded, 16)
            sp.dma_start(wvg[:, VC:VC + GC], Ws).then_inc(w_loaded, 16)
            sp.dma_start(wvg[:, VC + GC:VC + 2 * GC], Wd).then_inc(w_loaded, 16)
            rows = Wo.rearrange("e k d -> (e k) d")
            sp.dma_start(wo[:, 0:2, :], rows[0:2 * P].rearrange("(a p) d -> p a d", p=P)).then_inc(w_loaded, 16)
            sp.wait_ge(pool_consts, 1)
            sp.dma_start(wo[0:VC - 2 * P, 2, :], rows[2 * P:VC]).then_inc(w_loaded, 16)

        @block.gpsimd
        def _(pool):
            nc.gpsimd.memset(wo[:, 2, :], 0.0).then_inc(pool_consts, 1)
            nc.gpsimd.memset(half[:, :], -0.5).then_inc(pool_consts, 1)
            nc.gpsimd.memset(kz[:, :, :, :], 0.0).then_inc(consts_ready, 1)
            nc.gpsimd.memset(y[:, :, :], 0.0).then_inc(consts_ready, 1)
            for j in range(E):
                nc.gpsimd.memset(later[:, j:j + 1], float(E - 1 - j)).then_inc(consts_ready, 1)
            pool.wait_ge(pool_consts, 2)

            def front(b):
                pool.wait_ge(ln_var, b + 1)
                nc.gpsimd.tensor_tensor(rstd[:, :], var_eps[:, :], half[:, 0:1].to_broadcast([P, T]),
                                        ALU.pow).then_inc(ln_rstd, 1)
                own = Chain(pool, pool_steps, b * (4 * T))
                pool.wait_ge(gates_ready, b + 1)
                for i in range(T):
                    own.only(nc.gpsimd.tensor_tensor(
                        vprod[:, :, :, :],
                        xvg[:, i, 0:VC].rearrange("p (a e k) -> p a e k", a=1, e=E).to_broadcast([P, H, E, DH]),
                        wv[:, i, :].rearrange("p (h e a) -> p h e a", h=H, a=1).to_broadcast([P, H, E, DH]),
                        ALU.mult))
                    own.ran(nc.gpsimd.tensor_tensor(vsum[:, 0], vprod[:, :, 0, :], vprod[:, :, 1, :], ALU.add))
                    own.ran(nc.gpsimd.tensor_tensor(vsum[:, 1], vprod[:, :, 2, :], vprod[:, :, 3, :], ALU.add))
                    own.sync()
                    own.only(nc.gpsimd.tensor_tensor(vsum[:, 0], vsum[:, 0], vsum[:, 1], ALU.add))
                    nc.gpsimd.tensor_tensor(v_next[:, i], vsum[:, 0], vprod[:, :, 4, :], ALU.add).then_inc(v_next_ready, 1)
                    pool.wait_ge(v_next_ready, b * T + i + 1)
                assert own.n == 4 * T

            front(0)
            with pool.Fori(0, B - 1) as b:
                front(b + 1)

        @block.scalar
        def _(act):
            def take(k):
                act.wait_ge(in_misc, k + 1)

            def head_exp(b, h, i):
                act.wait_ge(max_ready, (b * H + h) * T + i + 1)
                if i == 0:
                    yield_n = (b * H + h - 1) * T
                    if not (isinstance(b, int) and b == 0 and h < 2):
                        act.wait_ge(in_turned, yield_n)
                nc.scalar.activation(prob[:, h % 2, i, :], PS[:, i, :], ACT.Exp, bias=nmax[:, h % 2, i:i + 1],
                                     accum_out=den[:, h, i:i + 1]).then_inc(exp_done, 1)

            def head_turned(b, h, j):
                act.wait_ge(in_turned, (b * H + h) * T + j + 1)
                if j == 0 and not (isinstance(b, int) and b == 0 and h < 4):
                    act.wait_ge(in_att, b * PAIRS + h // 2 - 1)
                nc.scalar.activation(probT[:, h % 4, j, :], PS[:, 4 + j % 2, :], ACT.Copy).then_inc(turned_taken, 1)

            def pair_att(b, pr):
                act.wait_ge(in_att, b * PAIRS + pr + 1)
                nc.scalar.activation(attT[:, :], PS[:, 6, :], ACT.Copy).then_inc(attT_ready, 1)

            def run_use(name, b, k):
                if name == "xnT":
                    take(k)
                    nc.scalar.activation(xnT_next[:, :], misc, ACT.Copy).then_inc(misc_taken, 1)
                elif name[0] == "v":
                    i = int(name[1])
                    take(k)
                    nc.scalar.activation(xvg[:, i, :], misc[:, 0:VC + 2 * GC], ACT.Copy).then_inc(misc_taken, 1)
                    if i == T - 1:
                        act.wait_ge(misc_taken, k + 1)
                        nc.scalar.activation(esig[:, :, :], xvg[:, :, VC:VC + GC], ACT.Exp,
                                             scale=-1.0).then_inc(esig_ready, 1)
                elif name[0] == "q":
                    pr = int(name[1])
                    take(k)
                    if not (isinstance(b, int) and b == 0 and pr < 2):
                        act.wait_ge(in_scores, (b * PAIRS + pr - 1) * 2 * T)
                    nc.scalar.activation(q[:, pr % 2, :], misc, ACT.Copy, scale=SCALE).then_inc(misc_taken, 1)
                elif name[0] == "k":
                    pr = int(name[1])
                    take(k)
                    nc.scalar.activation(kz[0:DH, pr % 2, 0, :], misc[0:DH], ACT.Copy)
                    nc.scalar.activation(kz[DH:P, pr % 2, 1, :], misc[DH:P], ACT.Copy).then_inc(misc_taken, 1)
                elif name[0] == "y":
                    take(k)
                    nc.scalar.activation(yT[:, int(name[1]), :], misc, ACT.Copy).then_inc(misc_taken, 1)

            act.wait_ge(consts_ready, 2 + E)

            def move_xnT(b):
                nc.scalar.activation(xnT[:, :], xnT_next[:, :], ACT.Copy).then_inc(xnT_moved, 1)

            def batch(b, kind):
                for h in range(H):
                    nb, nh = (b, h + 1) if h + 1 < H else (b + 1, 0)
                    for i, at in enumerate(QUARTERS):
                        head_turned(b, h, i)
                        if h + 1 < H or kind != "last":
                            head_exp(nb, nh, i)
                        name, k = use_at(h, at, kind, b)
                        if name:
                            run_use(name, batch_of(name, b), k)
                    if h == 0 and kind != "first":
                        pair_att(b - 1, PAIRS - 1)
                    if h % 2 == 0 and h:
                        pair_att(b, h // 2 - 1)
                    name, k = use_at(h, "E", kind, b)
                    if name:
                        run_use(name, batch_of(name, b), k)
                    if h == 4 and kind != "last":
                        move_xnT(b + 1)

            for k, name in enumerate(PROLOGUE):
                run_use(name, 0, k)
                if name == "xnT":
                    act.wait_ge(misc_taken, 1)
                    move_xnT(0)
            for i in range(T):
                head_exp(0, 0, i)
            batch(0, "first")
            with act.Fori(1, B - 1) as b:
                batch(b, "middle")
            batch(B - 1, "last")
            pair_att(B - 1, PAIRS - 1)
            for n, name in enumerate(EPILOGUE):
                run_use(name, B - 1, misc_base("last", B - 1) + count("last") + n)

        @block.tensor
        def _(pe):
            def scores(b, h, i, k_use=None):
                if not (isinstance(b, int) and b == 0 and h == 0):
                    pe.wait_ge(exp_done, (b * H + h - 1) * T + i + 1)
                if i == 0 and h % 2 == 0:
                    pe.wait_ge(misc_taken, k_use + 1)
                pr = h // 2
                nc.tensor.matmul(PS[:, i, :], q[:, pr % 2, i * P:(i + 1) * P], kz[:, pr % 2, h % 2, :],
                                 start=True, stop=True).then_inc(in_scores, 1)

            def turn(b, h, j):
                if j == 0:
                    pe.wait_ge(exp_done, (b * H + h) * T + T)
                if not (isinstance(b, int) and b == 0 and h == 0 and j < 2):
                    pe.wait_ge(turned_taken, (b * H + h) * T + j - 1)
                for i in range(T):
                    last = nc.tensor.transpose(PS[:, 4 + j % 2, i * P:(i + 1) * P],
                                               prob[:, h % 2, i, j * P:(j + 1) * P], ident[:, :])
                last.then_inc(in_turned, 1)

            def half_product(b, pr, js):
                if pr == 0 and 0 in js:
                    pe.wait_ge(v_ready, b + 1)
                if 0 in js and not (isinstance(b, int) and b == 0 and pr == 0):
                    pe.wait_ge(attT_ready, b * PAIRS + pr)
                pe.wait_ge(turned_taken, (b * H + 2 * pr + 1) * T + js[-1] + 1)
                for j in js:
                    for hh in range(2):
                        h = 2 * pr + hh
                        last = nc.tensor.matmul(PS[hh * DH:(hh + 1) * DH, 6, :], v[:, j, h, :], probT[:, h % 4, j, :],
                                                start=(j == 0), stop=(j == T - 1), skip_group_check=True)
                if T - 1 in js:
                    last.then_inc(in_att, 1)

            def run_use(name, b, k):
                if not (isinstance(k, int) and k == 0):
                    pe.wait_ge(misc_taken, k)
                if name == "xnT":
                    pe.wait_ge(ln_done, b + 1)
                    for i in range(T):
                        last = nc.tensor.transpose(misc[:, i * P:(i + 1) * P], xn[:, i, :], ident[:, :])
                elif name[0] == "v":
                    i = int(name[1])
                    last = nc.tensor.matmul(misc[:, 0:VC + 2 * GC], xnT_next[:, i * P:(i + 1) * P], wvg[:, :],
                                            start=True, stop=True)
                elif name[0] in "qk":
                    pr = int(name[1])
                    pe.wait_ge(xnT_moved, b + 1)
                    wt = wq if name[0] == "q" else wk
                    last = nc.tensor.matmul(misc, wt[:, pr * P:(pr + 1) * P], xnT[:, :], start=True, stop=True)
                elif name[:4] == "back":
                    pe.wait_ge(attT_ready, b * PAIRS + int(name[4]) + 1)
                    for i in range(T):
                        last = nc.tensor.transpose(misc[:, i * P:(i + 1) * P], attT[:, i * P:(i + 1) * P], ident[:, :])
                elif name[0] == "y":
                    c = int(name[1])
                    if c == 0:
                        pe.wait_ge(y_ready, b + 1)
                    for i in range(T):
                        last = nc.tensor.transpose(misc[:, i * P:(i + 1) * P], y[:, i, c * P:(c + 1) * P], ident[:, :])
                elif name == "out":
                    for i in range(T):
                        for c in range(CH):
                            last = nc.tensor.matmul(misc[:, i * P:(i + 1) * P], yT[:, c, i * P:(i + 1) * P], wo[:, c, :],
                                                    start=(c == 0), stop=(c == CH - 1))
                last.then_inc(in_misc, 1)

            def batch(b, kind):
                k_use = None
                for h in range(H):
                    nb, nh = (b, h + 1) if h + 1 < H else (b + 1, 0)
                    for i, at in enumerate(QUARTERS):
                        if h + 1 < H or kind != "last":
                            scores(nb, nh, i, k_use)
                        turn(b, h, i)
                        name, k = use_at(h, at, kind, b)
                        if name:
                            run_use(name, batch_of(name, b), k)
                            if name[0] == "k":
                                k_use = k
                    if h % 2:
                        half_product(b, h // 2, (0, 1))
                    elif h:
                        half_product(b, h // 2 - 1, (2, 3))
                    elif kind != "first":
                        half_product(b - 1, PAIRS - 1, (2, 3))
                    name, k = use_at(h, "E", kind, b)
                    if name:
                        run_use(name, batch_of(name, b), k)

            pe.wait_ge(w_loaded, 16 * N_LOADS)
            for k, name in enumerate(PROLOGUE):
                run_use(name, 0, k)
            for i in range(T):
                scores(0, 0, i, len(PROLOGUE) - 1)
            batch(0, "first")
            with pe.Fori(1, B - 1) as b:
                batch(b, "middle")
            batch(B - 1, "last")
            half_product(B - 1, PAIRS - 1, (2, 3))
            for n, name in enumerate(EPILOGUE):
                run_use(name, B - 1, misc_base("last", B - 1) + count("last") + n)

        @block.vector
        def _(dve):
            def head_max(b, h, i):
                dve.wait_ge(in_scores, (b * H + h) * T + i + 1)
                nc.vector.tensor_reduce(nmax[:, h % 2, i:i + 1], PS[:, i, :], AX.X, ALU.max,
                                        negate=True).then_inc(max_ready, 1)

            def beats(own, i, taken):
                dve.wait_ge(misc_taken, taken)
                logit = xvg[:, i, VC:VC + 2 * GC].rearrange("p (h e) -> p h e", e=E)
                for d in range(1, E):
                    own.ran(nc.vector.tensor_tensor(wins[:, d - 1, i, :, 0:E - d], logit[:, :, 0:E - d],
                                                    logit[:, :, d:E], ALU.is_ge))
                if i == T - 1:
                    own.ran(nc.vector.tensor_copy(
                        beaten[:, :, :, :].rearrange("p i h e -> p (i h) e"),
                        later[:, :].rearrange("p (a e) -> p a e", a=1).to_broadcast([P, T * 2 * H, E])))

            def count_beaten(own, d):
                if d == 1:
                    own.sync()
                flat = beaten[:, :, :, :].rearrange("p i h e -> p (i h) e")
                won = wins[:, d - 1].rearrange("p i h e -> p (i h) e")[:, :, 0:E - d]
                own.only(nc.vector.tensor_tensor(flat[:, :, d:E], flat[:, :, d:E], won, ALU.add))
                own.only(nc.vector.tensor_tensor(flat[:, :, 0:E - d], flat[:, :, 0:E - d], won, ALU.subtract))

            def keep_mo(own):
                own.only(nc.vector.tensor_copy(mo[:, :, :, :], picked[:, :, H:2 * H, :]))

            def pick(own, b):
                own.ran(nc.vector.tensor_scalar(picked[:, :, :, :], beaten[:, :, :, :], 2.0, None, ALU.is_lt))
                dve.wait_ge(esig_ready, b + 1)
                own.only(nc.vector.tensor_scalar(sig[:, :, :], esig[:, :, :], 1.0, None, ALU.add))
                own.only(nc.vector.reciprocal(sig[:, :, :], sig[:, :, :]))
                nc.vector.tensor_tensor(wv[:, :, :].rearrange("p i (h e) -> p i h e", e=E), picked[:, :, 0:H, :],
                                        sig[:, :, :].rearrange("p i (h e) -> p i h e", e=E),
                                        ALU.mult).then_inc(gates_ready, 1)

            def take_v(b):
                if not (isinstance(b, int) and b == 0):
                    dve.wait_ge(in_att, b * PAIRS)
                dve.wait_ge(v_next_ready, (b + 1) * T)
                nc.vector.tensor_copy(v[:, :, :, :], v_next[:, :, :, :]).then_inc(v_ready, 1)

            def weights(own, b, pr):
                h0 = 2 * pr
                dve.wait_ge(exp_done, (b * H + h0 + 2) * T)
                own.only(nc.vector.reciprocal(rden[:, :, :], den[:, h0:h0 + 2, :]))
                for hh in range(2):
                    own.ran(nc.vector.tensor_tensor(
                        w[:, hh], mo[:, :, h0 + hh, :],
                        rden[:, hh, :].rearrange("p (i a) -> p i a", a=1).to_broadcast([P, T, E]), ALU.mult))

            def products(own, pr, k):
                own.sync()
                dve.wait_ge(in_misc, k + 1)
                att = misc.rearrange("p (i a h k) -> p i a h k", i=T, a=1, h=2)
                for hh in range(2):
                    dst = y[:, :, 0:VC] if pr == 0 and hh == 0 else yprod[:, hh]
                    ins = nc.vector.tensor_tensor(
                        dst.rearrange("p i (e k) -> p i e k", e=E),
                        att[:, :, :, hh, :].to_broadcast([P, T, E, DH]),
                        w[:, hh].rearrange("p i (e a) -> p i e a", a=1).to_broadcast([P, T, E, DH]), ALU.mult)
                    if hh == 0:
                        own.ran(ins)
                    else:
                        ins.then_inc(misc_taken, 1)

            def first_sum(own):
                own.sync()
                own.only(nc.vector.tensor_tensor(y[:, :, 0:VC], y[:, :, 0:VC], yprod[:, 0], ALU.add))

            def second_sum(own, pr, k):
                own.sync()
                dve.wait_ge(misc_taken, k + 1)
                ins = nc.vector.tensor_tensor(y[:, :, 0:VC], y[:, :, 0:VC], yprod[:, 1], ALU.add)
                if pr == PAIRS - 1:
                    ins.then_inc(y_ready, 1)
                else:
                    own.only(ins)

            def add_out(own, b, k):
                dve.wait_ge(in_misc, k + 1)
                nc.vector.tensor_tensor(X[:, b, :, :], misc.rearrange("p (i n) -> p i n", i=T), X[:, b, :, :],
                                        ALU.add).then_inc(misc_taken, 1)

            def front_stats(own, b):
                layernorm_stats(nc, own, X[:, b], stats, mv, var_eps).then_inc(ln_var, 1)

            def front_xn(own, b):
                dve.wait_ge(ln_rstd, b + 1)
                layernorm_apply(nc, X[:, b], xn, mv, rstd).then_inc(ln_done, 1)

            def piece(own, name, b, kind):
                what, n = name.rstrip("01234"), int(name[-1]) if name[-1].isdigit() else None
                at = batch_of(name, b)
                if name == "stats":
                    front_stats(own, at)
                elif name == "xn":
                    front_xn(own, at)
                elif name == "take_v":
                    take_v(at)
                elif name == "out":
                    add_out(own, at, number("out", kind, b))
                elif name == "pick":
                    keep_mo(own)
                    if kind != "last":
                        pick(own, b + 1)
                elif what == "beats":
                    beats(own, n, number("v%d" % n, kind, b) + 1)
                elif what == "count":
                    count_beaten(own, n)
                elif what == "weights":
                    weights(own, at, n)
                elif what == "products":
                    products(own, n, number("back%d" % n, kind, b))
                elif what == "first_sum":
                    first_sum(own)
                elif what == "second_sum":
                    second_sum(own, n, number("back%d" % n, kind, b))

            def batch(b, kind, base):
                own = Chain(dve, dve_steps, base)
                for h in range(H):
                    nb, nh = (b, h + 1) if h + 1 < H else (b + 1, 0)
                    for i, at in enumerate("ABCDE"):
                        if at != "E" and (h + 1 < H or kind != "last"):
                            head_max(nb, nh, i)
                        for name in PIECES[h].get(at, []):
                            if not skipped(name, kind):
                                piece(own, name, b, kind)
                assert own.n == own_steps(kind), (kind, own.n, own_steps(kind))

            COUNTED = {"stats": LN_STEPS, "beats": E - 1, "count": 2, "pick": 1 + 3,
                       "weights": 3, "products": 1, "first_sum": 1, "second_sum": 1}

            def own_steps(kind):
                names = [name for h in PIECES for at in PIECES[h] for name in PIECES[h][at] if not skipped(name, kind)]
                n = sum(COUNTED.get(name.rstrip("01234"), 0) for name in names)
                n += "beats3" in names
                n -= "second_sum3" in names
                return n - (3 if kind == "last" else 0)

            dve.wait_ge(consts_ready, 2 + E)
            own = Chain(dve, dve_steps, 0)
            front_stats(own, 0)
            front_xn(own, 0)
            for i in range(T):
                beats(own, i, PROLOGUE.index("v%d" % i) + 1)
            for d in range(1, E):
                count_beaten(own, d)
            pick(own, 0)
            for i in range(T):
                head_max(0, 0, i)
            n_start = own.n
            batch(0, "first", n_start)
            n_start += own_steps("first")
            n = own_steps("middle")
            with dve.Fori(1, B - 1) as b:
                batch(b, "middle", b * n + (n_start - n))
            n_start += (B - 2) * n
            batch(B - 1, "last", n_start)
            own = Chain(dve, dve_steps, n_start + own_steps("last"))
            base = misc_base("last", B - 1) + count("last")
            weights(own, B - 1, PAIRS - 1)
            products(own, PAIRS - 1, base)
            first_sum(own)
            second_sum(own, PAIRS - 1, base)
            add_out(own, B - 1, base + EPILOGUE.index("out"))


def phase_geometric_attention(nc, X, PS, ident, Wq, Wk, Wv, Wo, head_dirs, scale):
    H, D, HD = 16, 4, C // 16
    TERMS = ((0, 0), (0, 1), (0, 2), (1, 0), (1, 1), (2, 0))
    ROWS = len(TERMS) * D
    GR = 32
    NG = P // GR
    HALF = H // 2
    SL = NG
    VW = 32
    EX = T * (T + 1) // 2 * P
    NEG = -1e30
    S1A, S1B, S1C, S2A, OUTB, MISC = 0, 1, 2, 3, 6, 7
    BF16 = mybir.dt.bfloat16

    def plan(n):
        us = {h: [] for h in range(H)}
        if 0 <= n < B:
            us[1] += ["c1"]
        if 1 <= n <= B:
            us[1] += ["back3"]
            us[2] += ["turn", "out"]
        if n + 2 < B:
            us[1] += ["xnT"]
            us[2] += ["proj"]
            us[3] += ["v0", "v1"]
            us[4] += ["v2", "v3"]
        if 0 <= n < B:
            us[5] += ["back0"]
        if n + 1 < B:
            us[9] += ["c0"]
        if 0 <= n < B:
            us[9] += ["back1"]
            us[13] += ["back2"]
        return us

    START = ["xnT", "proj", "v0", "v1", "v2", "v3"]

    def n_uses(n):
        return sum(len(u) for u in plan(n).values())

    def place_of(k, name):
        return [u for us in plan(k).values() for u in us].index(name)

    def misc_base(n, k):
        if isinstance(n, int):
            return len(START) + sum(n_uses(m) for m in range(-1, n))
        return (n - 1) * n_uses(1) + misc_base(1, 1)

    with ExitStack() as ctx:
        def sb(name, shape, dt=F32):
            return ctx.enter_context(nc.sbuf_tensor("c_" + name, shape, dt))

        def sem(name):
            return ctx.enter_context(nc.semaphore("c_" + name))

        stack = nc.dram_tensor("c_stack", [B, 2, H, ROWS, S], BF16).ap()
        shifts = nc.dram_tensor("c_shifts", [B, 2, 3, HALF, S], BF16).ap()

        wq3, wk3 = sb("wq3", [P, H, 3]), sb("wk3", [P, H, 3])
        dirs, scale_sb = sb("dirs", [P, H, 3]), sb("scale", [P, 1])
        wdir = sb("wdir", [P, 2, H, 3])
        w4 = sb("w4", [P, 2, H, D])
        wv, wo = sb("wv", [P, C]), sb("wo", [P, C])
        half = sb("half", [P, 2])
        ident_bf = sb("ident_bf", [P, P], BF16)
        mask_ts, mask_st = sb("mask_ts", [P, P], BF16), sb("mask_st", [P, P], BF16)
        stats, mv = sb("stats", [P, T, 6]), sb("mv", [P, T, 2])
        var_eps, rstd = sb("var_eps", [P, T]), sb("rstd", [P, T])
        xn, xnT = sb("xn", [P, T, C]), sb("xnT", [P, S])
        parts, rest = sb("parts", [P, 3, S], BF16), sb("rest", [P, S])
        qx, k1, k2 = sb("qx", [P, 2, H, S], BF16), sb("k1", [P, 2, SL, S], BF16), sb("k2", [P, 2, SL, S], BF16)
        v_next, v = sb("v_next", [P, T, H, HD]), sb("v", [P, 2, T, H, VW])
        nmax = sb("nmax", [P, 2, T, HALF])
        cparts, crest = sb("cparts", [P, 3, S], BF16), sb("crest", [P, S])
        ex = sb("ex", [P, HALF, EX])
        oT = sb("oT", [P, S])
        rz = sb("rz", [P, T, NG])
        att, attT = sb("att", [P, T, C]), sb("attT", [P, S])

        w_loaded, w4_ready, consts_ready = sem("w_loaded"), sem("w4_ready"), sem("consts_ready")
        pool_consts, pool_steps, dve_steps = sem("pool_consts"), sem("pool_steps"), sem("dve_steps")
        ln_var, ln_rstd, ln_done = sem("ln_var"), sem("ln_rstd"), sem("ln_done")
        in_misc, misc_taken = sem("in_misc"), sem("misc_taken")
        part1_ready, part2_ready, part3_ready = sem("part1_ready"), sem("part2_ready"), sem("part3_ready")
        stack_written, stack_passed = sem("stack_written"), sem("stack_passed")
        pool_passed = sem("pool_passed")
        k1_loaded = sem("k1_loaded")
        qk_loaded = [sem("qk_loaded0"), sem("qk_loaded1")]
        c_part1, c_part2, c_part3 = sem("c_part1"), sem("c_part2"), sem("c_part3")
        c_written, c_loaded = sem("c_written"), [sem("c_loaded0"), sem("c_loaded1")]
        v_ready = sem("v_ready")
        in_first, max_done = sem("in_first"), sem("max_done")
        in_second, exp_done = sem("in_second"), sem("exp_done")
        in_out, oT_ready, att_ready = sem("in_out"), sem("oT_ready"), sem("att_ready")
        N_LOADS = 6

        block = ctx.enter_context(nc.Block())
        misc = PS[:, MISC, :]

        def steps_of(emit, j_loop):
            emit(-1, -1)
            emit(0, 0)
            with j_loop(0, (B - 4) // 2) as j:
                emit(j * 2 + 1, 1)
                emit(j * 2 + 2, 2)
            for n in range(B - 3, B + 1):
                emit(n, n)

        def batch_of(name, n):
            if name in ("xnT", "proj", "v0", "v1", "v2", "v3"):
                return n + 2
            if name == "c0":
                return n + 1
            if name in ("back3", "turn", "out"):
                return n - 1
            return n

        @block.sync
        def _(sp):
            def write_stack(b):
                sp.wait_ge(part2_ready, b + 1)
                sp.wait_ge(part3_ready, b + 1)
                for qk in range(2):
                    for t, term in enumerate(TERMS):
                        sp.dma_start(stack[b, qk, :, t * D:(t + 1) * D, :],
                                     parts[qk * H * D:(qk + 1) * H * D, term[qk], :]).then_inc(stack_written, 16)
                sp.wait_ge(stack_written, b * (2 * len(TERMS) * 16) + 2 * len(TERMS) * 16).then_inc(stack_passed, 1)

            def load_k1(b, par):
                if not (isinstance(b, int) and b < 2):
                    sp.wait_ge(in_first, (b - 1) * (3 * H))
                for g in range(NG):
                    sp.dma_start(k1[g * GR:g * GR + ROWS, par, :, :],
                                 stack[b, 1, g:H:NG].rearrange("s r n -> r s n")).then_inc(k1_loaded, 16)

            def load_qk(b, par, hf):
                if not (isinstance(b, int) and b < 2):
                    sp.wait_ge(in_second, (b - 2) * (2 * H) + (hf + 1) * H)
                s0, s1 = hf * SL // 2, (hf + 1) * SL // 2
                for g in range(NG):
                    rows = slice(g * GR, g * GR + ROWS)
                    sp.dma_start(qx[rows, par, s0 * NG + g:s1 * NG:NG, :],
                                 stack[b, 0, s0 * NG + g:s1 * NG:NG].rearrange("s r n -> r s n")).then_inc(qk_loaded[hf], 16)
                    sp.dma_start(k2[rows, par, s0:s1, :],
                                 stack[b, 1, s0 * NG + g:s1 * NG:NG].rearrange("s r n -> r s n")).then_inc(qk_loaded[hf], 16)

            def move_c(b, par, hf):
                sp.wait_ge(c_part2, b * 2 + hf + 1)
                sp.wait_ge(c_part3, b * 2 + hf + 1)
                sp.dma_start(shifts[b, hf].rearrange("a h n -> h a n"), cparts[0:HALF, :, :]).then_inc(c_written, 16)
                sp.wait_ge(c_written, b * 32 + (hf + 1) * 16)
                for g in range(NG):
                    sp.dma_start(qx[g * GR + ROWS:g * GR + ROWS + 3, par, hf * HALF + g:(hf + 1) * HALF:NG, :],
                                 shifts[b, hf, :, g:HALF:NG, :]).then_inc(c_loaded[hf], 16)

            for dst, src in ((wq3[:, :, :], Wq.rearrange("c (h d) -> c h d", d=3)),
                             (wk3[:, :, :], Wk.rearrange("c (h d) -> c h d", d=3)),
                             (wv[:, :], Wv), (wo[:, :], Wo),
                             (dirs[:, :, :].rearrange("p h d -> p (h d)"),
                              bcast_rows(head_dirs.rearrange("h d -> (h d)"), H * 3)),
                             (scale_sb[:, :], bcast_rows(scale, 1))):
                sp.dma_start(dst, src).then_inc(w_loaded, 16)
            sp.wait_ge(consts_ready, 8)
            write_stack(0)
            load_k1(0, 0)
            load_qk(0, 0, 0)
            load_qk(0, 0, 1)

            def step(n, k):
                if 0 <= k < B:
                    move_c(n, k % 2, 1)
                if k + 2 < B:
                    write_stack(n + 2)
                    load_k1(n + 2, k % 2)
                    load_qk(n + 2, k % 2, 0)
                if k + 1 < B:
                    move_c(n + 1, (k + 1) % 2, 0)
                if k + 2 < B:
                    load_qk(n + 2, k % 2, 1)

            steps_of(step, sp.Fori)

        @block.gpsimd
        def _(pool):
            own = Chain(pool, pool_consts, 0)
            own.ran(nc.gpsimd.memset(ident_bf[:, :], 0.0))
            own.ran(nc.gpsimd.memset(mask_ts[:, :], 0.0))
            own.ran(nc.gpsimd.memset(mask_st[:, :], 0.0))
            nc.gpsimd.memset(half[:, :], -0.5).then_inc(consts_ready, 1)
            nc.gpsimd.memset(v[:, :, :, :, :], 0.0).then_inc(pool_consts, 1)
            own.n += 1
            own.sync()
            nc.gpsimd.memset(v[:, :, :, :, HD:HD + 1], 1.0).then_inc(consts_ready, 1)
            nc.gpsimd.affine_select(out=ident_bf[:, :], in_=ident_bf[:, :], compare_op=ALU.not_equal, fill=1.0,
                                    base=0, pattern=[[-1, P]], channel_multiplier=1).then_inc(consts_ready, 1)
            nc.gpsimd.affine_select(out=mask_ts[:, :], in_=mask_ts[:, :], compare_op=ALU.is_ge, fill=NEG,
                                    base=0, pattern=[[-1, P]], channel_multiplier=1).then_inc(consts_ready, 1)
            nc.gpsimd.affine_select(out=mask_st[:, :], in_=mask_st[:, :], compare_op=ALU.is_ge, fill=NEG,
                                    base=0, pattern=[[1, P]], channel_multiplier=-1).then_inc(consts_ready, 1)
            pool.wait_ge(consts_ready, 8)

            def ln(b):
                pool.wait_ge(ln_var, b + 1)
                nc.gpsimd.tensor_tensor(rstd[:, :], var_eps[:, :], half[:, 0:1].to_broadcast([P, T]),
                                        ALU.pow).then_inc(ln_rstd, 1)

            def place_v(b, par, v_uses):
                pool.wait_ge(misc_taken, v_uses).then_inc(pool_passed, 1)
                if not (isinstance(b, int) and b < 2):
                    pool.wait_ge(in_out, (b - 1) * NG).then_inc(pool_passed, 1)
                nc.gpsimd.tensor_copy(v[:, par, :, :, 0:HD], v_next[:, :, :, :]).then_inc(v_ready, 1)

            def shift_parts(b, hf, n, k):
                pool.wait_ge(misc_taken, misc_base(n, k) + place_of(k, "c%d" % hf) + 1).then_inc(pool_passed, 1)
                nc.gpsimd.tensor_copy(cparts[0:HALF, 1, :], crest[0:HALF, :]).then_inc(c_part2, 1)
                pool.wait_ge(c_part2, b * 2 + hf + 1)
                nc.gpsimd.tensor_tensor(cparts[0:HALF, 2, :], crest[0:HALF, :], cparts[0:HALF, 1, :],
                                        ALU.subtract).then_inc(c_part3, 1)

            ln(0)
            place_v(0, 0, len(START))

            def step(n, k):
                if k + 2 < B:
                    ln(n + 2)
                if 0 <= k and k + 1 < B:
                    place_v(n + 1, (k + 1) % 2, misc_base(n, k))
                if 0 <= k < B:
                    shift_parts(n, 1, n, k)
                if k + 1 < B:
                    shift_parts(n + 1, 0, n, k)

            steps_of(step, pool.Fori)

        @block.scalar
        def _(act):
            def exps(b, h):
                if h % NG == 0 and not (isinstance(b, int) and b == 0 and h < HALF):
                    act.wait_ge(in_out, b * NG + h // NG - 1)
                e = h % HALF
                act.wait_ge(in_second, (b * H + h) * 2 + 1)
                nc.scalar.activation(ex[:, e, 0:BANK], PS[:, S2A, :], ACT.Exp).then_inc(exp_done, 1)
                act.wait_ge(in_second, (b * H + h) * 2 + 2)
                nc.scalar.activation(ex[:, e, BANK:EX],
                                     PS[:, S2A + 1:S2A + 3, :].rearrange("p a n -> p (a n)")[:, 0:EX - BANK],
                                     ACT.Exp).then_inc(exp_done, 1)

            def take_out(b, gr):
                act.wait_ge(in_out, b * NG + gr + 1)
                nc.scalar.activation(oT[:, :], PS[:, OUTB, :], ACT.Copy).then_inc(oT_ready, 1)

            def run_use(name, b, k, par):
                if name == "xnT":
                    act.wait_ge(in_misc, k + 1)
                    nc.scalar.activation(xnT[:, :], misc, ACT.Copy).then_inc(misc_taken, 1)
                elif name == "proj":
                    act.wait_ge(in_misc, k + 1)
                    if not (isinstance(b, int) and b == 0):
                        act.wait_ge(stack_written, b * (2 * len(TERMS) * 16))
                    nc.scalar.activation(parts[:, 0, :], misc, ACT.Copy).then_inc(part1_ready, 1)
                    act.wait_ge(misc_taken, k + 1)
                    nc.scalar.activation(parts[:, 1, :], rest[:, :], ACT.Copy).then_inc(part2_ready, 1)
                elif name[0] == "v":
                    i = int(name[1])
                    act.wait_ge(in_misc, k + 1)
                    if i == 0 and not (isinstance(b, int) and b == 0):
                        act.wait_ge(v_ready, b)
                    nc.scalar.activation(v_next[:, i, :, :].rearrange("p h g -> p (h g)"), misc[:, 0:C],
                                         ACT.Copy).then_inc(misc_taken, 1)
                elif name == "turn":
                    act.wait_ge(in_misc, k + 1)
                    nc.scalar.activation(attT[:, :], misc, ACT.Copy).then_inc(misc_taken, 1)
                elif name in ("c0", "c1"):
                    hf = int(name[1])
                    act.wait_ge(in_misc, k + 1)
                    n = b * 2 + hf
                    if not (isinstance(b, int) and b == 0 and hf == 0):
                        act.wait_ge(c_written, n * 16)
                    nc.scalar.activation(cparts[0:HALF, 0, :], misc[0:HALF, :], ACT.Copy).then_inc(c_part1, 1)

            act.wait_ge(consts_ready, 8)
            for k, name in enumerate(START):
                run_use(name, 0, k, 0)

            def step(n, k):
                m = misc_base(n, k)
                us = plan(k)
                for h in range(H):
                    if 0 <= k < B:
                        exps(n, h)
                    if h % NG == 0:
                        if h and 0 <= k < B:
                            take_out(n, h // NG - 1)
                        elif h == 0 and 1 <= k <= B:
                            take_out(n - 1, NG - 1)
                    for name in us[h]:
                        run_use(name, batch_of(name, n), m, 0)
                        m = m + 1

            steps_of(step, act.Fori)

        @block.tensor
        def _(pe):
            def first(b, h, par):
                if h == 0:
                    pe.wait_ge(k1_loaded, b * (NG * 16) + NG * 16)
                if h % HALF == 0:
                    pe.wait_ge(qk_loaded[h // HALF], b * (2 * NG * 16) + 2 * NG * 16)
                n4 = (b * H + h) * 4
                started = not (isinstance(b, int) and b == 0 and h == 0)
                q, kk = qx[:, par, h, :], k1[:, par, h // NG, :]

                def tile(bank, c0, i, start, stop):
                    nc.tensor.matmul(PS[:, bank, c0:c0 + (i + 1) * P], q[:, i * P:(i + 1) * P], kk[:, 0:(i + 1) * P],
                                     start=start, stop=False, skip_group_check=True)
                    return nc.tensor.matmul(PS[:, bank, c0 + i * P:c0 + (i + 1) * P], ident_bf[:, :], mask_ts[:, :],
                                            start=False, stop=stop, skip_group_check=True)
                if started:
                    pe.wait_ge(max_done, n4 - 3)
                tile(S1A, 0, 3, True, True).then_inc(in_first, 1)
                if started:
                    pe.wait_ge(max_done, n4 - 1)
                tile(S1B, 0, 2, True, False)
                tile(S1B, 3 * P, 0, False, True).then_inc(in_first, 1)
                if started:
                    pe.wait_ge(max_done, n4)
                tile(S1C, 0, 1, True, True).then_inc(in_first, 1)

            def second(b, h, par):
                if h % HALF == 0:
                    pe.wait_ge(c_loaded[h // HALF], b * (NG * 16) + NG * 16)
                n2 = (b * H + h) * 2
                started = not (isinstance(b, int) and b == 0 and h == 0)
                q, kk = qx[:, par, h, :], k2[:, par, h // NG, :]

                def tile(bank, c0, j, start, stop):
                    nc.tensor.matmul(PS[:, bank, c0:c0 + S - j * P], kk[:, j * P:(j + 1) * P], q[:, j * P:S],
                                     start=start, stop=False, skip_group_check=True)
                    return nc.tensor.matmul(PS[:, bank, c0:c0 + P], ident_bf[:, :], mask_st[:, :],
                                            start=False, stop=stop, skip_group_check=True)
                if started:
                    pe.wait_ge(exp_done, n2 - 1)
                tile(S2A, 0, 0, True, True).then_inc(in_second, 1)
                if started:
                    pe.wait_ge(exp_done, n2)
                tile(S2A + 1, 0, 1, True, False)
                tile(S2A + 1, 3 * P, 3, False, True)
                tile(S2A + 2, 0, 2, True, True).then_inc(in_second, 1)

            EXC = [0, BANK, 2 * BANK, BANK + 3 * P]

            def out_group(b, gr, par):
                pe.wait_ge(exp_done, (b * H + (gr + 1) * NG) * 2)
                if gr == 0:
                    pe.wait_ge(v_ready, b + 1)
                if not (isinstance(b, int) and b == 0 and gr == 0):
                    pe.wait_ge(oT_ready, b * NG + gr)
                for j in range(T):
                    for g in range(NG):
                        h = gr * NG + g
                        last = nc.tensor.matmul(PS[g * VW:(g + 1) * VW, OUTB, j * P:S], v[:, par, j, h, :],
                                                ex[:, h % HALF, EXC[j]:EXC[j] + S - j * P],
                                                start=(j == 0), stop=(j == T - 1), skip_group_check=True)
                last.then_inc(in_out, 1)

            def run_use(name, b, k):
                if not (isinstance(k, int) and k == 0):
                    pe.wait_ge(misc_taken, k)
                if name == "xnT":
                    pe.wait_ge(ln_done, b + 1)
                    for i in range(T):
                        last = nc.tensor.transpose(misc[:, i * P:(i + 1) * P], xn[:, i, :], ident[:, :])
                elif name == "proj":
                    last = nc.tensor.matmul(misc, w4[:, :, :, :].rearrange("p a h d -> p (a h d)"), xnT[:, :],
                                            start=True, stop=True)
                elif name[0] == "v":
                    i = int(name[1])
                    last = nc.tensor.matmul(misc[:, 0:C], xnT[:, i * P:(i + 1) * P], wv[:, :], start=True, stop=True)
                elif name in ("c0", "c1"):
                    hf = int(name[1])
                    pe.wait_ge(max_done, (b * H + (hf + 1) * HALF) * 4)
                    for i in range(T):
                        last = nc.tensor.transpose(misc[0:HALF, i * P:(i + 1) * P], nmax[:, hf, i, :], ident[:, :])
                elif name[:4] == "back":
                    pe.wait_ge(oT_ready, b * NG + int(name[4]) + 1)
                    for i in range(T):
                        last = nc.tensor.transpose(misc[:, i * P:(i + 1) * P], oT[:, i * P:(i + 1) * P], ident[:, :])
                elif name == "turn":
                    for i in range(T):
                        last = nc.tensor.transpose(misc[:, i * P:(i + 1) * P], att[:, i, :], ident[:, :])
                elif name == "out":
                    for i in range(T):
                        last = nc.tensor.matmul(misc[:, i * P:(i + 1) * P], attT[:, i * P:(i + 1) * P], wo[:, :],
                                                start=True, stop=True)
                last.then_inc(in_misc, 1)

            pe.wait_ge(w4_ready, 1)
            pe.wait_ge(consts_ready, 8)
            for k, name in enumerate(START):
                run_use(name, 0, k)

            def step(n, k):
                m = misc_base(n, k)
                us = plan(k)
                for h in range(H):
                    if k + 1 < B:
                        first(n + 1, h, (k + 1) % 2)
                    if 0 <= k < B:
                        second(n, h, k % 2)
                    if h % NG == 0:
                        if h and 0 <= k < B:
                            out_group(n, h // NG - 1, k % 2)
                        elif h == 0 and 1 <= k <= B:
                            out_group(n - 1, NG - 1, (k - 1) % 2)
                    for name in us[h]:
                        run_use(name, batch_of(name, n), m)
                        m = m + 1

            steps_of(step, pe.Fori)

        @block.vector
        def _(dve):
            nc.vector.memset(qx[:, :, :, :], 0.0).then_inc(consts_ready, 1)
            nc.vector.memset(k1[:, :, :, :], 0.0).then_inc(consts_ready, 1)
            nc.vector.memset(k2[:, :, :, :], 1.0).then_inc(consts_ready, 1)
            dve.wait_ge(w_loaded, 16 * N_LOADS)
            own = Chain(dve, dve_steps, 0)
            for a, w3 in enumerate((wq3, wk3)):
                own.ran(nc.vector.tensor_tensor(wdir[:, a], w3[:, :, :], dirs[:, :, :], ALU.mult))
            own.ran(nc.vector.tensor_scalar(w4[:, 0, :, 0:3], wq3[:, :, :], scale_sb[:, 0:1], None, ALU.mult))
            own.ran(nc.vector.tensor_copy(w4[:, 1, :, 0:3], wk3[:, :, :]))
            own.sync()
            nc.vector.tensor_reduce(w4[:, :, :, 3], wdir[:, :, :, :], AX.X, ALU.add).then_inc(w4_ready, 1)

            def maxima(b, h):
                n4, n3, hf, hh = (b * H + h) * 4, (b * H + h) * 3, h // HALF, h % HALF

                def reduce(bank, c0, i):
                    nc.vector.tensor_reduce(nmax[:, hf, i, hh:hh + 1], PS[:, bank, c0:c0 + (i + 1) * P], AX.X, ALU.max,
                                            negate=True).then_inc(max_done, 1)
                dve.wait_ge(in_first, n3 + 1)
                reduce(S1A, 0, 3)
                dve.wait_ge(in_first, n3 + 2)
                reduce(S1B, 0, 2)
                reduce(S1B, 3 * P, 0)
                dve.wait_ge(in_first, n3 + 3)
                reduce(S1C, 0, 1)

            def stats_of(own, b):
                layernorm_stats(nc, own, X[:, b], stats, mv, var_eps).then_inc(ln_var, 1)

            def xn_of(b):
                dve.wait_ge(ln_rstd, b + 1)
                layernorm_apply(nc, X[:, b], xn, mv, rstd).then_inc(ln_done, 1)

            def run_use(own, name, b, k):
                if name == "proj":
                    dve.wait_ge(part1_ready, b + 1)
                    nc.vector.tensor_tensor(rest[:, :], misc, parts[:, 0, :], ALU.subtract).then_inc(misc_taken, 1)
                    dve.wait_ge(part2_ready, b + 1)
                    nc.vector.tensor_tensor(parts[:, 2, :], rest[:, :], parts[:, 1, :],
                                            ALU.subtract).then_inc(part3_ready, 1)
                elif name in ("c0", "c1"):
                    n = b * 2 + int(name[1])
                    dve.wait_ge(c_part1, n + 1)
                    nc.vector.tensor_tensor(crest[0:HALF, :], misc[0:HALF, :], cparts[0:HALF, 0, :],
                                            ALU.subtract).then_inc(misc_taken, 1)
                elif name[:4] == "back":
                    gr = int(name[4])
                    dve.wait_ge(in_misc, k + 1)
                    o = misc.rearrange("p (i g w) -> p i g w", i=T, g=NG)
                    own.only(nc.vector.reciprocal(rz[:, :, :], o[:, :, :, HD]))
                    ins = nc.vector.tensor_tensor(
                        att[:, :, gr * NG * HD:(gr + 1) * NG * HD].rearrange("p i (g w) -> p i g w", g=NG),
                        o[:, :, :, 0:HD],
                        rz[:, :, :].rearrange("p i (g a) -> p i g a", a=1).to_broadcast([P, T, NG, HD]), ALU.mult)
                    ins.then_inc(misc_taken, 1)
                elif name == "out":
                    dve.wait_ge(in_misc, k + 1)
                    nc.vector.tensor_tensor(X[:, b, :, :], misc.rearrange("p (i n) -> p i n", i=T), X[:, b, :, :],
                                            ALU.add).then_inc(misc_taken, 1)

            def n_steps(k):
                names = [u for us in plan(k).values() for u in us]
                return sum(u[:4] == "back" for u in names) + (LN_STEPS if k + 2 < B else 0)

            own = Chain(dve, dve_steps, 4)
            stats_of(own, 0)
            xn_of(0)
            for k, name in enumerate(START):
                run_use(own, name, 0, k)
            n_start = 4 + own.n

            def step(n, k):
                if isinstance(n, int):
                    base = n_start + sum(n_steps(m) for m in range(-1, n))
                else:
                    base = (n - 1) * n_steps(1) + n_start + sum(n_steps(m) for m in range(-1, 1))
                own = Chain(dve, dve_steps, base)
                m = misc_base(n, k)
                us = plan(k)
                for h in range(H):
                    if k + 1 < B:
                        maxima(n + 1, h)
                    if k + 2 < B:
                        if h == 0:
                            stats_of(own, n + 2)
                            xn_of(n + 2)
                    for name in us[h]:
                        run_use(own, name, batch_of(name, n), m)
                        m = m + 1
                assert own.n == n_steps(k), (k, own.n, n_steps(k))

            steps_of(step, dve.Fori)


def phase_expert_choice(nc, X, PS, ident, gate_w, gate_b, w1, w2, out):
    E, HID, TOP = 32, w1.shape[2], 8
    GB = P // E
    NGR = B // GB
    EG = E // GB
    BW = 32
    CH = HID // P
    HALF_S = -0.5
    with ExitStack() as ctx:
        def sb(name, shape):
            return ctx.enter_context(nc.sbuf_tensor("d_" + name, shape, F32))

        def sem(name):
            return ctx.enter_context(nc.semaphore("d_" + name))

        scratch = nc.dram_tensor("d_results", [E, BW, C], F32).ap()
        w1_sb, w2_sb = sb("w1", [P, E, HID]), sb("w2", [P, E, CH * C])
        b1, b2 = sb("b1", [P, HID]), sb("b2", [P, C])
        gw, gwT, gb = sb("gw", [E, C]), sb("gwT", [P, E]), sb("gb", [P, 1])
        half = sb("half", [P, 1])
        NT = GB * T
        stats, mv = sb("stats", [P, NT, 6]), sb("mv", [P, NT, 2])
        var_eps, rstd = sb("var_eps", [P, NT]), sb("rstd", [P, NT])
        xn, xnT = sb("xn", [P, NT, C]), sb("xnT", [P, GB, S])
        logit, nmax, total = sb("logit", [P, S]), sb("nmax", [P, 1]), sb("total", [P, 1])
        expo, rtotal, top = sb("expo", [P, S]), sb("rtotal", [P, 1]), sb("top", [P, TOP])
        picked, chosen = sb("picked", [P, S]), sb("chosen", [P, NGR, S])
        chosenT, merged = sb("chosenT", [P, T, P]), sb("merged", [P, C])
        mT = sb("mT", [P, E, BW])
        hid, hidT = sb("hid", [P, HID]), sb("hidT", [P, CH, P])
        res = sb("res", [P, 2, C])
        spread = xn[:, :, :].rearrange("p (g b) c -> p g b c", g=NGR)

        small_loaded, gw_turned, gwT_ready = sem("small_loaded"), sem("gw_turned"), sem("gwT_ready")
        w1_loaded = [sem("w1_loaded%d" % g) for g in range(EG)]
        w2_loaded = [sem("w2_loaded%d" % g) for g in range(EG)]
        zeroed, dve_steps = sem("zeroed"), sem("dve_steps")
        ln_var, ln_rstd, ln_done = sem("ln_var"), sem("ln_rstd"), sem("ln_done")
        in_xnT, xnT_ready = sem("in_xnT"), sem("xnT_ready")
        in_gate, nmax_ready, exp_ready, picked_ready = (
            sem("in_gate"), sem("nmax_ready"), sem("exp_ready"), sem("picked_ready"))
        chosen_kept = sem("chosen_kept")
        pool_passed = sem("pool_passed")
        in_turned, turned_ready, in_merged, merged_ready = (
            sem("in_turned"), sem("turned_ready"), sem("in_merged"), sem("merged_ready"))
        in_mT, mT_ready = sem("in_mT"), sem("mT_ready")
        in_hid, hid_ready, in_hidT, hidT_ready = sem("in_hid"), sem("hid_ready"), sem("in_hidT"), sem("hidT_ready")
        in_res, res_ready, res_written = sem("in_res"), sem("res_ready"), [sem("res_written0"), sem("res_written1")]
        spread_loaded = sem("spread_loaded")
        in_back, added, stored = sem("in_back"), sem("added"), sem("stored")
        N_SMALL = 3 + GB

        block = ctx.enter_context(nc.Block())

        @block.sync
        def _(sp):
            sp.dma_start(gw[:, :], gate_w).then_inc(small_loaded, 16)
            for g in range(GB):
                sp.dma_start(gb[g * E:(g + 1) * E, :], gate_b.rearrange("(e a) -> e a", a=1)).then_inc(small_loaded, 16)
            sp.wait_ge(zeroed, 2)
            sp.dma_start(b1[0:E, :], w1[:, C, :]).then_inc(small_loaded, 16)
            sp.dma_start(b2[0:E, :], w2[:, HID, :]).then_inc(small_loaded, 16)
            for g in range(EG):
                e = slice(g * GB, (g + 1) * GB)
                sp.dma_start(w1_sb[:, e, :], w1[e, 0:C, :].rearrange("e d h -> d e h")).then_inc(w1_loaded[g], 16)
                sp.dma_start(w2_sb[:, e, :], w2[e, 0:HID, :].rearrange("e (p c) o -> p e (c o)", c=CH)).then_inc(w2_loaded[g], 16)
            for g in range(EG):
                sp.wait_ge(res_ready, g + 1)
                sp.dma_start(scratch[g * GB:(g + 1) * GB].rearrange("e b o -> (e b) o"), res[:, g % 2, :])\
                    .then_inc(res_written[g % 2], 16)
            for half_of in res_written:
                sp.wait_ge(half_of, 16 * EG // 2)
            sp.wait_ge(zeroed, 5)
            for g in range(NGR):
                for b in range(GB):
                    sp.dma_start(spread[b * E:(b + 1) * E, g, b, :], scratch[:, g * GB + b, :]).then_inc(spread_loaded, 16)
            with sp.Fori(0, NGR) as g:
                sp.wait_ge(added, g * T + T)
                for b in range(GB):
                    sp.dma_start(out[g * GB + b].rearrange("(i p) c -> p i c", p=P), X[:, g * GB + b, :, :]).then_inc(stored, 16)
            sp.wait_ge(stored, 16 * B)

        @block.gpsimd
        def _(pool):
            nc.gpsimd.memset(b1[:, :], 0.0).then_inc(zeroed, 1)
            nc.gpsimd.memset(b2[:, :], 0.0).then_inc(zeroed, 1)
            nc.gpsimd.memset(half[:, :], HALF_S).then_inc(zeroed, 1)
            nc.gpsimd.memset(mT[:, :, :], 0.0).then_inc(zeroed, 1)
            pool.wait_ge(zeroed, 4)
            with pool.Fori(0, NGR) as g:
                pool.wait_ge(ln_var, g + 1)
                nc.gpsimd.tensor_tensor(rstd[:, :], var_eps[:, :], half[:, 0:1].to_broadcast([P, NT]),
                                        ALU.pow).then_inc(ln_rstd, 1)
                pool.wait_ge(picked_ready, g + 1).then_inc(pool_passed, 1)
                nc.gpsimd.tensor_copy(chosen[:, g, :], picked[:, :]).then_inc(chosen_kept, 1)
            pool.wait_ge(in_merged, NGR)
            nc.gpsimd.memset(xn[:, :, :], 0.0).then_inc(zeroed, 1)

        @block.scalar
        def _(act):
            act.wait_ge(gw_turned, 1)
            nc.scalar.activation(gwT[:, :], PS[:, 7, 0:E], ACT.Copy).then_inc(gwT_ready, 1)
            with act.Fori(0, NGR) as g:
                for b in range(GB):
                    act.wait_ge(in_xnT, g * GB + b + 1)
                    nc.scalar.activation(xnT[:, b, :], PS[:, b, :], ACT.Copy).then_inc(xnT_ready, 1)
                act.wait_ge(nmax_ready, g + 1)
                nc.scalar.activation(expo[:, :], logit[:, :], ACT.Exp, bias=nmax[:, 0:1],
                                     accum_out=total[:, 0:1]).then_inc(exp_ready, 1)
                act.wait_ge(in_turned, g + 1)
                nc.scalar.activation(chosenT[:, :, :].rearrange("p i n -> p (i n)"), PS[:, 5, :], ACT.Copy).then_inc(turned_ready, 1)
                act.wait_ge(in_merged, g + 1)
                nc.scalar.activation(merged[:, :], PS[:, 6, 0:C], ACT.Copy).then_inc(merged_ready, 1)
            for g in range(EG):
                act.wait_ge(in_hid, g + 1)
                if g:
                    act.wait_ge(in_hidT, g)
                nc.scalar.activation(hid[:, :], PS[:, g % 2, :], ACT.Gelu).then_inc(hid_ready, 1)

        @block.tensor
        def _(pe):
            pe.wait_ge(small_loaded, 16 * N_SMALL)
            nc.tensor.transpose(PS[:, 7, 0:E], gw[:, :], ident[0:E, 0:E]).then_inc(gw_turned, 1)
            pe.wait_ge(gwT_ready, 1)
            with pe.Fori(0, NGR) as g:
                pe.wait_ge(ln_done, g + 1)
                for b in range(GB):
                    for i in range(T):
                        last = nc.tensor.transpose(PS[:, b, i * P:(i + 1) * P], xn[:, b * T + i, :], ident[:, :])
                    last.then_inc(in_xnT, 1)
                pe.wait_ge(xnT_ready, g * GB + GB)
                for b in range(GB):
                    last = nc.tensor.matmul(PS[b * E:(b + 1) * E, 4, :], gwT[:, :], xnT[:, b, :], start=True, stop=True)
                last.then_inc(in_gate, 1)
                pe.wait_ge(picked_ready, g + 1)
                for i in range(T):
                    last = nc.tensor.transpose(PS[:, 5, i * P:(i + 1) * P], picked[:, i * P:(i + 1) * P], ident[:, :])
                last.then_inc(in_turned, 1)
                pe.wait_ge(turned_ready, g + 1)
                for i in range(T):
                    for b in range(GB):
                        last = nc.tensor.matmul(PS[b * E:(b + 1) * E, 6, 0:C], chosenT[:, i, b * E:(b + 1) * E],
                                                xn[:, b * T + i, :], start=(i == 0), stop=(i == T - 1), skip_group_check=True)
                last.then_inc(in_merged, 1)
                pe.wait_ge(merged_ready, g + 1)
                nc.tensor.transpose(PS[:, 7, 0:P], merged[:, :], ident[:, :]).then_inc(in_mT, 1)

            def hidden(g):
                if g == 0:
                    pe.wait_ge(mT_ready, NGR)
                pe.wait_ge(w1_loaded[g], 16)
                if g >= 2:
                    pe.wait_ge(hid_ready, g - 1)
                for e4 in range(GB):
                    nc.tensor.matmul(PS[e4 * BW:(e4 + 1) * BW, g % 2, :], mT[:, g * GB + e4, :], w1_sb[:, g * GB + e4, :],
                                     start=True, stop=False, skip_group_check=True)
                for e4 in range(GB):
                    e = g * GB + e4
                    last = nc.tensor.matmul(PS[e4 * BW:(e4 + 1) * BW, g % 2, :], ident[:, e:e + 1].to_broadcast([P, BW]),
                                            b1[:, :], start=False, stop=True, skip_group_check=True)
                last.then_inc(in_hid, 1)

            def result(g):
                pe.wait_ge(hid_ready, g + 1)
                if g:
                    pe.wait_ge(hidT_ready, g)
                for c in range(CH):
                    last = nc.tensor.transpose(PS[:, 2, c * P:(c + 1) * P], hid[:, c:HID:CH], ident[:, :])
                last.then_inc(in_hidT, 1)
                pe.wait_ge(hidT_ready, g + 1)
                pe.wait_ge(w2_loaded[g], 16)
                if g:
                    pe.wait_ge(res_ready, g)
                for c in range(CH):
                    for e4 in range(GB):
                        nc.tensor.matmul(PS[e4 * BW:(e4 + 1) * BW, 3, 0:C], hidT[:, c, e4 * BW:(e4 + 1) * BW],
                                         w2_sb[:, g * GB + e4, c * C:(c + 1) * C],
                                         start=(c == 0), stop=False, skip_group_check=True)
                for e4 in range(GB):
                    e = g * GB + e4
                    last = nc.tensor.matmul(PS[e4 * BW:(e4 + 1) * BW, 3, 0:C], ident[:, e:e + 1].to_broadcast([P, BW]),
                                            b2[:, :], start=False, stop=True, skip_group_check=True)
                last.then_inc(in_res, 1)

            hidden(0)
            for g in range(EG):
                if g + 1 < EG:
                    hidden(g + 1)
                result(g)

            pe.wait_ge(chosen_kept, NGR)
            pe.wait_ge(spread_loaded, 16 * B)
            for g in range(NGR):
                for i in range(T):
                    n = g * T + i
                    if n >= 4:
                        pe.wait_ge(added, n - 3)
                    nc.tensor.matmul(PS[:, 4 + n % 4, :], chosen[:, g, i * P:(i + 1) * P],
                                     spread[:, g, :, :].rearrange("p b c -> p (b c)"),
                                     start=True, stop=True).then_inc(in_back, 1)

        @block.vector
        def _(dve):
            dve.wait_ge(small_loaded, 16 * N_SMALL)
            dve.wait_ge(zeroed, 4)
            N_OWN = 2 * NT + 8
            with dve.Fori(0, NGR) as g:
                own = Chain(dve, dve_steps, g * N_OWN)
                x = [X[:, g * GB + n // T, n % T, :] for n in range(NT)]
                for n in range(NT):
                    own.ran(nc.vector.bn_stats(stats[:, n, :], x[n]))
                own.sync_apart()
                for n in range(NT):
                    own.ran(nc.vector.bn_aggr(mv[:, n, :], stats[:, n, :]))
                own.sync()
                nc.vector.tensor_scalar(var_eps[:, :], mv[:, :, 1], LN_EPS, None, ALU.add).then_inc(ln_var, 1)
                dve.wait_ge(ln_rstd, g + 1)
                for n in range(NT):
                    last = nc.vector.tensor_scalar(xn[:, n, :], x[n], mv[:, n, 0:1], rstd[:, n:n + 1],
                                                   ALU.subtract, ALU.mult)
                last.then_inc(ln_done, 1)
                dve.wait_ge(in_gate, g + 1)
                own.only(nc.vector.tensor_scalar(logit[:, :], PS[:, 4, :], gb[:, 0:1], None, ALU.add))
                nc.vector.tensor_reduce(nmax[:, 0:1], logit[:, :], AX.X, ALU.max, negate=True).then_inc(nmax_ready, 1)
                dve.wait_ge(exp_ready, g + 1)
                own.only(nc.vector.reciprocal(rtotal[:, :], total[:, :]))
                own.ran(nc.vector.tensor_scalar(expo[:, :], expo[:, :], rtotal[:, 0:1], None, ALU.mult))
                own.sync_apart()
                own.ran(nc.vector.max(top[:, :], expo[:, :]))
                own.sync_apart()
                own.only(nc.vector.match_replace(picked[:, :], top[:, :], expo[:, :], 0.0))
                nc.vector.tensor_tensor(picked[:, :], expo[:, :], picked[:, :], ALU.subtract).then_inc(picked_ready, 1)
                dve.wait_ge(in_mT, g + 1)
                for b in range(GB):
                    last = nc.vector.tensor_copy(mT[:, :, g * GB + b], PS[:, 7, b * E:(b + 1) * E])
                last.then_inc(mT_ready, 1)
                dve.wait_ge(chosen_kept, g + 1)
            for g in range(EG):
                dve.wait_ge(in_hidT, g + 1)
                if g:
                    dve.wait_ge(in_res, g)
                nc.vector.tensor_copy(hidT[:, :, :].rearrange("p c n -> p (c n)"), PS[:, 2, :]).then_inc(hidT_ready, 1)
                dve.wait_ge(in_res, g + 1)
                if g >= 2:
                    dve.wait_ge(res_written[g % 2], 16 * (g // 2))
                nc.vector.tensor_copy(res[:, g % 2, :], PS[:, 3, 0:C]).then_inc(res_ready, 1)
            for g in range(NGR):
                for i in range(T):
                    n = g * T + i
                    dve.wait_ge(in_back, n + 1)
                    xs = X[:, g * GB:(g + 1) * GB, i, :]
                    nc.vector.tensor_tensor(xs, PS[:, 4 + n % 4, :].rearrange("p (b c) -> p b c", b=GB), xs,
                                            ALU.add).then_inc(added, 1)


def program(nc, x, Wqkv, bqkv, gamma_q, beta_q, gamma_k, beta_k, Wo0, Wq, Wk, Ws, Wd, Wv, Wo1,
            wq, wk, wv, wo, head_dirs, scale, gate_w, gate_b, w1, w2, bo, out):
    with (nc.sbuf_tensor("x", [P, B, T, C], F32) as X, nc.sbuf_tensor("ident", [P, P], F32) as ident,
          nc.psum_tensor("banks", [P, 8, BANK], F32) as PS):
        phase_linear_attention(nc, X, PS, ident, x, Wqkv, bqkv, gamma_q, beta_q, gamma_k, beta_k, Wo0, bo)
        phase_head_mixture(nc, X, PS, ident, Wq, Wk, Ws, Wd, Wv, Wo1)
        phase_geometric_attention(nc, X, PS, ident, wq, wk, wv, wo, head_dirs, scale)
        phase_expert_choice(nc, X, PS, ident, gate_w, gate_b, w1, w2, out)


_INS = ["L0_attn_x", "L0_attn_Wqkv", "L0_attn_bqkv", "L0_attn_gamma_q", "L0_attn_beta_q", "L0_attn_gamma_k",
        "L0_attn_beta_k", "L0_attn_Wo", "L0_ffn_Wq", "L0_ffn_Wk", "L0_ffn_Ws", "L0_ffn_Wd", "L0_ffn_Wv",
        "L0_ffn_Wo", "L1_attn_wq", "L1_attn_wk", "L1_attn_wv", "L1_attn_wo", "L1_attn_head_dirs",
        "L1_attn_scale", "L1_ffn_gate_w", "L1_ffn_gate_b", "L1_ffn_w1", "L1_ffn_w2", "L0_attn_bo"]


def kernel(**inputs):
    import numpy as np
    import concourse.bacc as bacc
    from concourse.bass_utils import run_bass_kernel_spmd

    nc = bacc.Bacc("TRN2", target_bir_lowering=False, num_devices=1)
    arrays, args = {}, []
    for name in _INS:
        a = np.ascontiguousarray(inputs[name])
        arrays["in_" + name] = a
        args.append(nc.dram_tensor("in_" + name, a.shape, mybir.dt.from_np(a.dtype), kind="ExternalInput").ap())
    out = nc.dram_tensor("out", (B, S, C), F32, kind="ExternalOutput").ap()
    program(nc, *args, out)
    r = run_bass_kernel_spmd(nc, [arrays], core_ids=[0])
    return r.results[0]["out"]
```

```python
from contextlib import ExitStack

import concourse.bass as bass
import concourse.mybir as mybir

F32 = mybir.dt.float32
ALU = mybir.AluOpType
ACT = mybir.ActivationFunctionType
AX = mybir.AxisListType

P = 128
B, S, C = 16, 512, 128
T = S // P
BANK = 512
LN_EPS = 1e-5
LN_STEPS = 2 * T + 1


class Chain:

    def __init__(self, eng, sem, base):
        self.eng, self.sem, self.base, self.n = eng, sem, base, 0

    def ran(self, ins):
        self.n += 1
        ins.then_inc(self.sem, 1)

    def sync(self):
        self.eng.wait_ge(self.sem, self.base + self.n)

    def sync_apart(self):
        self.n += 1
        self.eng.wait_ge(self.sem, self.base + self.n - 1).then_inc(self.sem, 1)

    def only(self, ins):
        self.ran(ins)
        self.sync()


def bcast_rows(vec, n):
    return vec.rearrange("(a n) -> a n", a=1).to_broadcast([P, n])


def layernorm_stats(nc, own, x, stats, mv, var_eps):
    for i in range(T):
        own.ran(nc.vector.bn_stats(stats[:, i, :], x[:, i, :]))
    own.sync_apart()
    for i in range(T):
        own.ran(nc.vector.bn_aggr(mv[:, i, :], stats[:, i, :]))
    own.sync()
    return nc.vector.tensor_scalar(var_eps[:, :], mv[:, :, 1], LN_EPS, None, ALU.add)


def layernorm_apply(nc, x, xn, mv, rstd):
    for i in range(T):
        last = nc.vector.tensor_scalar(xn[:, i, :], x[:, i, :], mv[:, i, 0:1], rstd[:, i:i + 1],
                                       ALU.subtract, ALU.mult)
    return last


def phase_linear_attention(nc, X, PS, ident, x_in, Wqkv, bqkv, gamma_q, beta_q, gamma_k, beta_k, Wo, bo):
    H, D = 16, C // 16
    G = D + 1
    OUT = G * C
    THIRD = OUT // 3
    with ExitStack() as ctx:
        def sb(name, shape):
            return ctx.enter_context(nc.sbuf_tensor("a_" + name, shape, F32))

        def sem(name):
            return ctx.enter_context(nc.semaphore("a_" + name))

        wqkv, bqkv_bc = sb("wqkv", [P, 3 * C]), sb("bqkv_bc", [P, 3 * C])
        gamma, beta = sb("gamma", [P, 2, C]), sb("beta", [P, 2, C])
        wo, bo_bc = sb("wo", [P, C]), sb("bo_bc", [P, C])
        tri, last_row = sb("tri", [P, P]), sb("last_row", [P, P])
        half = sb("half", [P, 2])
        stats, mv = sb("stats", [P, T, 6]), sb("mv", [P, T, 2])
        var_eps, rstd = sb("var_eps", [P, T]), sb("rstd", [P, T])
        xn, xnT = sb("xn", [P, T, C]), sb("xnT", [P, S])
        qkv, vone = sb("qkv", [P, 2, T, 2, C]), sb("vone", [P, 2, T, H, G])
        feat, outer = sb("feat", [P, 2, T, 2, C]), sb("outer", [P, 2, T, OUT])
        qmv = sb("qmv", [P, 2, T, 2, 2])
        qstats = sb("qstats", [P, T, 2, 6])
        qvar, qstd = sb("qvar", [P, T, 2]), sb("qstd", [P, T, 2])
        qstde, qrstd = sb("qstde", [P, T, 2]), sb("qrstd", [P, T, 2])
        normed, scaled, shifted = sb("normed", [P, T, 2, C]), sb("scaled", [P, 2, 2, C]), sb("shifted", [P, T, 2, C])
        cum = sb("cum", [P, 2, OUT])
        prod, sums = sb("prod", [P, 2, OUT]), sb("sums", [P, T, G * H])
        zeps, rz = sb("zeps", [P, T, H]), sb("rz", [P, T, H])
        att, attT = sb("att", [P, T, C]), sb("attT", [P, S])

        w_loaded, x_loaded, x_passed = sem("w_loaded"), sem("x_loaded"), sem("x_passed")
        consts_ready, pool_steps, dve_steps = sem("consts_ready"), sem("pool_steps"), sem("dve_steps")
        ln_var, ln_rstd, ln_done = sem("ln_var"), sem("ln_rstd"), sem("ln_done")
        xnT_in_psum, xnT_ready = sem("xnT_in_psum"), sem("xnT_ready")
        qkv_in_psum, qkv_taken = sem("qkv_in_psum"), sem("qkv_taken")
        qk_var, qk_std, qk_normed = sem("qk_var"), sem("qk_std"), sem("qk_normed")
        qk_shifted, feat_ready = sem("qk_shifted"), sem("feat_ready")
        outer_ready, cum_in_psum, cum_ready = sem("outer_ready"), sem("cum_in_psum"), sem("cum_ready")
        cum_used, att_ready = sem("cum_used"), sem("att_ready")
        attT_in_psum, attT_ready = sem("attT_in_psum"), sem("attT_ready")
        biased, y_in_psum, x_added = sem("biased"), sem("y_in_psum"), sem("x_added")
        N_LOADS = 8

        block = ctx.enter_context(nc.Block())
        TURN, OUTB = 6, 7

        def cum_banks(i):
            return PS[:, 3 * (i % 2):3 * (i % 2) + 3, 0:THIRD]

        def stages(k):
            return {"A": 0 <= k + 2 < B, "B": 0 <= k + 1 < B, "C": 0 <= k < B, "D": 0 <= k - 1 < B}

        def steps_of(emit, eng):
            for n in (-2, -1, 0):
                emit(n, n)
            with eng.Fori(0, (B - 4) // 2) as j:
                emit(j * 2 + 1, 1)
                emit(j * 2 + 2, 2)
            for n in range(B - 3, B + 1):
                emit(n, n)

        @block.sync
        def _(sp):
            with sp.Fori(0, B) as b:
                sp.dma_start(X[:, b, :, :], x_in[b].rearrange("(i p) c -> p i c", p=P)).then_inc(x_loaded, 16)
                sp.wait_ge(x_loaded, b * 16 + 16).then_inc(x_passed, 1)

        @block.gpsimd
        def _(pool):
            own = Chain(pool, pool_steps, 0)
            own.ran(nc.gpsimd.memset(tri[:, :], 1.0))
            own.ran(nc.gpsimd.memset(last_row[:, :], 1.0))
            own.ran(nc.gpsimd.memset(ident[:, :], 0.0))
            own.ran(nc.gpsimd.memset(half[:, 0:1], 0.5))
            own.ran(nc.gpsimd.memset(half[:, 1:2], -0.5))
            own.ran(nc.gpsimd.memset(vone[:, :, :, :, D:G], 1.0))
            own.sync()
            nc.gpsimd.affine_select(out=tri[:, :], in_=tri[:, :], compare_op=ALU.is_ge, fill=0.0, base=0,
                                    pattern=[[1, P]], channel_multiplier=-1).then_inc(consts_ready, 1)
            nc.gpsimd.affine_select(out=last_row[:, :], in_=last_row[:, :], compare_op=ALU.is_ge, fill=0.0,
                                    base=1 - P, pattern=[[0, P]], channel_multiplier=1).then_inc(consts_ready, 1)
            nc.gpsimd.affine_select(out=ident[:, :], in_=ident[:, :], compare_op=ALU.not_equal, fill=1.0,
                                    base=0, pattern=[[-1, P]], channel_multiplier=1).then_inc(consts_ready, 1)
            pool.wait_ge(w_loaded, 16 * N_LOADS)
            N_CONSTS = own.n

            def rstd_of(b):
                pool.wait_ge(ln_var, b + 1)
                nc.gpsimd.tensor_tensor(rstd[:, :], var_eps[:, :], half[:, 1:2].to_broadcast([P, T]),
                                        ALU.pow).then_inc(ln_rstd, 1)

            def qk_std_of(b):
                pool.wait_ge(qk_var, b + 1)
                nc.gpsimd.tensor_tensor(qstd[:, :, :].rearrange("p i a -> p (i a)"), qvar[:, :, :].rearrange("p i a -> p (i a)"),
                                        half[:, 0:1].to_broadcast([P, 2 * T]), ALU.pow).then_inc(qk_std, 1)

            def affine(own, b, i):
                pool.wait_ge(qk_normed, b * T + i + 1)
                own.only(nc.gpsimd.tensor_tensor(scaled[:, i % 2], normed[:, i], gamma[:, :, :], ALU.mult))
                nc.gpsimd.tensor_tensor(shifted[:, i], scaled[:, i % 2], beta[:, :, :], ALU.add).then_inc(qk_shifted, 1)

            def outer_product(b, i, par, first):
                pool.wait_ge(feat_ready, b * T + i + 1)
                if i == 0 and not first:
                    pool.wait_ge(cum_in_psum, (b - 1) * T)
                nc.gpsimd.tensor_tensor(
                    outer[:, par, i, :].rearrange("p (g h f) -> p g h f", g=G, h=H),
                    feat[:, par, i, 1, :].rearrange("p (a h f) -> p a h f", a=1, h=H).to_broadcast([P, G, H, D]),
                    vone[:, par, i, :, :].rearrange("p h (g a) -> p g h a", a=1).to_broadcast([P, G, H, D]),
                    ALU.mult).then_inc(outer_ready, 1)

            def add_bias(b):
                pool.wait_ge(ln_done, b + 1)
                nc.gpsimd.tensor_tensor(X[:, b, :, :], X[:, b, :, :],
                                        bo_bc[:, :].rearrange("p (a n) -> p a n", a=1).to_broadcast([P, T, C]),
                                        ALU.add).then_inc(biased, 1)

            def step(n, k):
                on, par, first = stages(k), (k + 1) % 2, k + 1 < 2
                own = Chain(pool, pool_steps, (n + 1) * T + N_CONSTS)
                if on["B"]:
                    qk_std_of(n + 1)
                if on["A"]:
                    rstd_of(n + 2)
                if on["B"]:
                    affine(own, n + 1, 0)
                    affine(own, n + 1, 1)
                    outer_product(n + 1, 0, par, first)
                    affine(own, n + 1, 2)
                    outer_product(n + 1, 1, par, first)
                    affine(own, n + 1, 3)
                    outer_product(n + 1, 2, par, first)
                if on["A"]:
                    add_bias(n + 2)
                if on["B"]:
                    outer_product(n + 1, 3, par, first)

            steps_of(step, pool)

        @block.scalar
        def _(act):
            loads = ((wqkv[:, :], Wqkv), (bqkv_bc[:, :], bcast_rows(bqkv, 3 * C)),
                     (gamma[:, 0, :], bcast_rows(gamma_q, C)), (gamma[:, 1, :], bcast_rows(gamma_k, C)),
                     (beta[:, 0, :], bcast_rows(beta_q, C)), (beta[:, 1, :], bcast_rows(beta_k, C)),
                     (wo[:, :], Wo), (bo_bc[:, :], bcast_rows(bo, C)))
            for dst, src in loads:
                act.dma_start(dst, src).then_inc(w_loaded, 16)

            def take_xnT(b):
                act.wait_ge(xnT_in_psum, b + 1)
                nc.scalar.activation(xnT[:, :], PS[:, TURN, :], ACT.Copy).then_inc(xnT_ready, 1)

            def square(b, i, par, first):
                act.wait_ge(qk_shifted, b * T + i + 1)
                if i == 0 and not first:
                    act.wait_ge(cum_used, (b - 1) * T)
                nc.scalar.activation(feat[:, par, i, :, :], shifted[:, i], ACT.Square).then_inc(feat_ready, 1)

            def take_cum(b, i, first):
                act.wait_ge(cum_in_psum, b * T + i + 1)
                if i >= 2 or not first:
                    act.wait_ge(cum_used, b * T + i - 1)
                nc.scalar.activation(cum[:, i % 2, :].rearrange("p (a n) -> p a n", a=3), cum_banks(i),
                                     ACT.Copy).then_inc(cum_ready, 1)

            def take_attT(b):
                act.wait_ge(attT_in_psum, b + 1)
                nc.scalar.activation(attT[:, :], PS[:, TURN, :], ACT.Copy).then_inc(attT_ready, 1)

            def step(n, k):
                on, par, first = stages(k), (k + 1) % 2, k + 1 < 2
                if on["C"]:
                    take_cum(n, 0, k == 0)
                    take_cum(n, 1, k == 0)
                if on["D"]:
                    take_attT(n - 1)
                if on["B"]:
                    square(n + 1, 0, par, first)
                    square(n + 1, 1, par, first)
                if on["A"]:
                    take_xnT(n + 2)
                if on["C"]:
                    take_cum(n, 2, k == 0)
                if on["B"]:
                    square(n + 1, 2, par, first)
                    square(n + 1, 3, par, first)
                if on["C"]:
                    take_cum(n, 3, k == 0)

            steps_of(step, act)

        @block.tensor
        def _(pe):
            def turn_xn(b, after_att):
                pe.wait_ge(ln_done, b + 1)
                if after_att:
                    pe.wait_ge(attT_ready, b - 2)
                elif not (isinstance(b, int) and b == 0):
                    pe.wait_ge(qkv_taken, b * T)
                for i in range(T):
                    last = nc.tensor.transpose(PS[:, TURN, i * P:(i + 1) * P], xn[:, i, :], ident[:, :])
                last.then_inc(xnT_in_psum, 1)

            def project(b, i, after_out):
                if i == 0:
                    pe.wait_ge(xnT_ready, b + 1)
                elif i == 1:
                    if after_out:
                        pe.wait_ge(x_added, b - 2)
                    elif not (isinstance(b, int) and b == 0):
                        pe.wait_ge(qkv_taken, b * T)
                else:
                    pe.wait_ge(qkv_taken, b * T + i - 1)
                nc.tensor.matmul(PS[:, (TURN, OUTB)[i % 2], 0:3 * C], xnT[:, i * P:(i + 1) * P], wqkv[:, :],
                                 start=True, stop=True).then_inc(qkv_in_psum, 1)

            def tile_sums(b, i, par, first):
                if i >= 2 or not first:
                    pe.wait_ge(cum_ready, b * T + i - 1)
                pe.wait_ge(outer_ready, b * T + i + 1)
                for j in range(3):
                    last = nc.tensor.matmul(cum_banks(i)[:, j, :], tri[:, :], outer[:, par, i, j * THIRD:(j + 1) * THIRD],
                                            start=True, stop=(i == 0), skip_group_check=True)
                if i == 0:
                    last.then_inc(cum_in_psum, 1)

            def carry(b, i):
                pe.wait_ge(cum_ready, b * T + i)
                for j in range(3):
                    last = nc.tensor.matmul(cum_banks(i)[:, j, :], last_row[:, :],
                                            cum[:, (i - 1) % 2, j * THIRD:(j + 1) * THIRD], start=False, stop=True,
                                            skip_group_check=True)
                last.then_inc(cum_in_psum, 1)

            def turn_att(b, projected):
                pe.wait_ge(att_ready, b + 1)
                if projected:
                    pe.wait_ge(qkv_taken, (b + 3) * T)
                for i in range(T):
                    last = nc.tensor.transpose(PS[:, TURN, i * P:(i + 1) * P], att[:, i, :], ident[:, :])
                last.then_inc(attT_in_psum, 1)

            def output(b, projected):
                pe.wait_ge(attT_ready, b + 1)
                if not projected:
                    pe.wait_ge(x_added, b)
                for i in range(T):
                    last = nc.tensor.matmul(PS[:, OUTB, i * P:(i + 1) * P], attT[:, i * P:(i + 1) * P], wo[:, :],
                                            start=True, stop=True)
                last.then_inc(y_in_psum, 1)

            pe.wait_ge(consts_ready, 3)
            pe.wait_ge(w_loaded, 16 * N_LOADS)

            def step(n, k):
                on, par, first = stages(k), k % 2, k == 0
                if on["C"]:
                    tile_sums(n, 0, par, first)
                    tile_sums(n, 1, par, first)
                    carry(n, 1)
                if on["D"]:
                    turn_att(n - 1, 0 <= k + 1 < B)
                if on["C"]:
                    tile_sums(n, 2, par, first)
                if on["A"]:
                    turn_xn(n + 2, on["D"])
                if on["C"]:
                    carry(n, 2)
                if on["D"]:
                    output(n - 1, 0 <= k + 1 < B)
                if on["A"]:
                    project(n + 2, 0, on["D"])
                if on["C"]:
                    tile_sums(n, 3, par, first)
                if on["A"]:
                    project(n + 2, 1, on["D"])
                if on["C"]:
                    carry(n, 3)
                if on["A"]:
                    project(n + 2, 2, on["D"])
                    project(n + 2, 3, on["D"])

            steps_of(step, pe)

        @block.vector
        def _(dve):
            def token_stats(own, b):
                dve.wait_ge(x_loaded, b * 16 + 16)
                layernorm_stats(nc, own, X[:, b], stats, mv, var_eps).then_inc(ln_var, 1)

            def normalise(b):
                if not (isinstance(b, int) and b == 0):
                    dve.wait_ge(xnT_in_psum, b)
                dve.wait_ge(ln_rstd, b + 1)
                layernorm_apply(nc, X[:, b], xn, mv, rstd).then_inc(ln_done, 1)

            def take_qkv(own, b, i, par, first):
                if i == 0 and not first:
                    dve.wait_ge(outer_ready, (b - 1) * T)
                dve.wait_ge(qkv_in_psum, b * T + i + 1)
                bank = PS[:, (TURN, OUTB)[i % 2], :]
                own.ran(nc.vector.tensor_tensor(qkv[:, par, i, :, :], bank[:, 0:2 * C].rearrange("p (a n) -> p a n", a=2),
                                                bqkv_bc[:, 0:2 * C].rearrange("p (a n) -> p a n", a=2), ALU.add))
                nc.vector.tensor_tensor(vone[:, par, i, :, 0:D], bank[:, 2 * C:3 * C].rearrange("p (h g) -> p h g", h=H),
                                        bqkv_bc[:, 2 * C:3 * C].rearrange("p (h g) -> p h g", h=H),
                                        ALU.add).then_inc(qkv_taken, 1)

            def qk_stats(own, par):
                own.sync()
                for i in range(T):
                    for a in range(2):
                        own.ran(nc.vector.bn_stats(qstats[:, i, a, :], qkv[:, par, i, a, :]))
                own.sync_apart()
                for i in range(T):
                    for a in range(2):
                        own.ran(nc.vector.bn_aggr(qmv[:, par, i, a, :], qstats[:, i, a, :]))
                own.sync()
                nc.vector.tensor_scalar(qvar[:, :, :], qmv[:, par, :, :, 1], C / (C - 1.0), None,
                                        ALU.mult).then_inc(qk_var, 1)

            def qk_normalise(own, b, par, first):
                dve.wait_ge(qk_std, b + 1)
                own.only(nc.vector.tensor_scalar(qstde[:, :, :], qstd[:, :, :], 1e-6, None, ALU.add))
                own.only(nc.vector.reciprocal(qrstd[:, :, :], qstde[:, :, :]))
                if not first:
                    dve.wait_ge(qk_shifted, b * T)
                for i in range(T):
                    for a in range(2):
                        last = nc.vector.tensor_scalar(normed[:, i, a, :], qkv[:, par, i, a, :], qmv[:, par, i, a, 0:1],
                                                       qrstd[:, i, a:a + 1], ALU.subtract, ALU.mult)
                    last.then_inc(qk_normed, 1)

            def use_cum(own, b, i, par):
                dve.wait_ge(cum_ready, b * T + i + 1)
                nc.vector.tensor_tensor(
                    prod[:, i % 2, :].rearrange("p (g n) -> p g n", g=G),
                    cum[:, i % 2, :].rearrange("p (g n) -> p g n", g=G),
                    feat[:, par, i, 0, :].rearrange("p (g n) -> p g n", g=1).to_broadcast([P, G, C]),
                    ALU.mult).then_inc(cum_used, 1)
                dve.wait_ge(cum_used, b * T + i + 1)
                own.ran(nc.vector.tensor_reduce(sums[:, i, :], prod[:, i % 2, :].rearrange("p (n f) -> p n f", f=D),
                                                AX.X, ALU.add))

            def divide(own, b, first):
                own.sync()
                own.only(nc.vector.tensor_scalar(zeps[:, :, :], sums[:, :, C:C + H], 1e-6, None, ALU.add))
                own.only(nc.vector.reciprocal(rz[:, :, :], zeps[:, :, :]))
                if not first:
                    dve.wait_ge(attT_in_psum, b)
                nc.vector.tensor_tensor(
                    att[:, :, :].rearrange("p i (h g) -> p i g h", g=D),
                    sums[:, :, 0:C].rearrange("p i (g h) -> p i g h", h=H),
                    rz[:, :, :].rearrange("p i (a h) -> p i a h", a=1).to_broadcast([P, T, D, H]),
                    ALU.mult).then_inc(att_ready, 1)

            def add_output(b):
                dve.wait_ge(biased, b + 1)
                dve.wait_ge(y_in_psum, b + 1)
                nc.vector.tensor_tensor(X[:, b, :, :], PS[:, OUTB, :].rearrange("p (i n) -> p i n", i=T),
                                        X[:, b, :, :], ALU.add).then_inc(x_added, 1)

            dve.wait_ge(w_loaded, 16 * N_LOADS)
            dve.wait_ge(pool_steps, 6)
            N_A, N_B, N_C, N_D = LN_STEPS + T + 4 * T + 1, 2, T - 1, 3

            def own_steps(k):
                on = stages(k)
                return N_A * on["A"] + N_B * on["B"] + N_C * on["C"] + N_D * on["D"]

            def step(n, k):
                on, par = stages(k), k % 2
                base = sum(own_steps(m) for m in range(-2, k))
                own = Chain(dve, dve_steps, base if isinstance(n, int) else (n - k) * own_steps(1) + base)
                if on["A"]:
                    token_stats(own, n + 2)
                if on["D"]:
                    use_cum(own, n - 1, T - 1, 1 - par)
                    divide(own, n - 1, k == 1)
                if on["B"]:
                    qk_normalise(own, n + 1, 1 - par, k + 1 == 0)
                if on["A"]:
                    normalise(n + 2)
                if on["C"]:
                    use_cum(own, n, 0, par)
                    use_cum(own, n, 1, par)
                if on["A"]:
                    take_qkv(own, n + 2, 0, par, k + 2 < 2)
                if on["D"]:
                    add_output(n - 1)
                if on["C"]:
                    use_cum(own, n, 2, par)
                if on["A"]:
                    for i in range(1, T):
                        take_qkv(own, n + 2, i, par, k + 2 < 2)
                    qk_stats(own, par)
                assert own.n == own_steps(k), (k, own.n, own_steps(k))

            steps_of(step, dve)


def phase_head_mixture(nc, X, PS, ident, Wq, Wk, Ws, Wd, Wv, Wo):
    H, DH, E = 8, 64, 5
    PAIRS = H // 2
    VC = E * DH
    GC = H * E
    SCALE = float(DH) ** -0.5
    CH = 3
    MISC = 7

    USES = {0: {"A": "q1", "B": "k1", "D": "xnT", "E": "v0"},
            1: {"A": "v1", "B": "v2", "C": "v3", "D": "back3"},
            2: {"A": "q2", "B": "k2"},
            3: {"C": "y0", "D": "y1", "E": "y2"},
            4: {"A": "q3", "B": "k3", "C": "out", "D": "back0"},
            5: {"C": "back1"},
            6: {"A": "q0", "B": "k0"},
            7: {"C": "back2"}}
    PIECES = {0: {"A": ["stats"], "C": ["xn"]},
              1: {"A": ["take_v"], "B": ["beats0"], "C": ["beats1"], "D": ["beats2", "weights3"], "E": ["products3"]},
              2: {"A": ["beats3"], "B": ["count1", "count2"], "C": ["count3", "count4"], "D": ["pick"]},
              3: {"A": ["first_sum3"], "B": ["second_sum3"]},
              4: {"C": ["out", "weights0"], "D": ["products0"]},
              5: {"A": ["second_sum0"], "B": ["weights1"], "C": ["products1"], "D": ["first_sum1"]},
              6: {"A": ["second_sum1"]},
              7: {"B": ["weights2"], "C": ["products2"], "D": ["first_sum2"], "E": ["second_sum2"]}}
    QUARTERS = "ABCD"
    OF_BEFORE = {"back3", "y0", "y1", "y2", "out", "weights3", "products3", "first_sum3", "second_sum3"}
    OF_NEXT = {"xnT", "v0", "v1", "v2", "v3", "q0", "k0", "stats", "xn", "beats0", "beats1", "beats2", "beats3",
               "count1", "count2", "count3", "count4"}
    PROLOGUE = ["xnT", "v0", "v1", "v2", "v3", "q0", "k0"]
    EPILOGUE = ["back3", "y0", "y1", "y2", "out"]

    def skipped(name, kind):
        return name in {"first": OF_BEFORE, "middle": (), "last": OF_NEXT}[kind]

    def batch_of(name, b):
        return b - 1 if name in OF_BEFORE else b + 1 if name in OF_NEXT else b

    ORDER = [USES[h][at] for h in range(H) for at in "ABCDE" if at in USES[h]]

    def count(kind):
        return sum(not skipped(name, kind) for name in ORDER)

    def use_at(h, at, kind, b):
        name = USES[h].get(at)
        if name is None or skipped(name, kind):
            return None, None
        return name, number(name, kind, b)

    def number(name, kind, b):
        before = ORDER[:ORDER.index(name)]
        return misc_base(kind, b) + sum(not skipped(other, kind) for other in before)

    M0, M1, M2 = len(PROLOGUE), count("first"), count("middle")

    def misc_base(kind, b):
        return M0 if kind == "first" else b * M2 + (M0 + M1 - M2)

    with ExitStack() as ctx:
        def sb(name, shape):
            return ctx.enter_context(nc.sbuf_tensor("b_" + name, shape, F32))

        def sem(name):
            return ctx.enter_context(nc.semaphore("b_" + name))

        wq, wk = sb("wq", [P, H * DH]), sb("wk", [P, H * DH])
        wvg = sb("wvg", [P, VC + 2 * GC])
        wo = sb("wo", [P, CH, C])
        half = sb("half", [P, 2])
        stats, mv = sb("stats", [P, T, 6]), sb("mv", [P, T, 2])
        var_eps, rstd = sb("var_eps", [P, T]), sb("rstd", [P, T])
        xn, xnT_next, xnT = sb("xn", [P, T, C]), sb("xnT_next", [P, S]), sb("xnT", [P, S])
        xvg = sb("xvg", [P, T, VC + 2 * GC])
        esig, sig = sb("esig", [P, T, GC]), sb("sig", [P, T, GC])
        later, beaten = sb("later", [P, E]), sb("beaten", [P, T, 2 * H, E])
        wins = sb("wins", [P, E - 1, T, 2 * H, E])
        picked = sb("picked", [P, T, 2 * H, E])
        wv, mo = sb("wv", [P, T, GC]), sb("mo", [P, T, H, E])
        vprod, vsum = sb("vprod", [P, H, E, DH]), sb("vsum", [P, 2, H, DH])
        v_next, v = sb("v_next", [P, T, H, DH]), sb("v", [P, T, H, DH])
        q, kz = sb("q", [P, 2, S]), sb("kz", [P, 2, 2, S])
        nmax, den = sb("nmax", [P, 2, T]), sb("den", [P, H, T])
        prob, probT = sb("prob", [P, 2, T, S]), sb("probT", [P, 4, T, S])
        attT = sb("attT", [P, S])
        rden, w = sb("rden", [P, 2, T]), sb("w", [P, 2, T, E])
        yprod, y = sb("yprod", [P, 2, T, VC]), sb("y", [P, T, CH * P])
        yT = sb("yT", [P, CH, S])

        w_loaded = sem("w_loaded")
        consts_ready, pool_consts, pool_steps, dve_steps = (
            sem("consts_ready"), sem("pool_consts"), sem("pool_steps"), sem("dve_steps"))
        ln_var, ln_rstd, ln_done = sem("ln_var"), sem("ln_rstd"), sem("ln_done")
        in_misc, misc_taken = sem("in_misc"), sem("misc_taken")
        xnT_moved = sem("xnT_moved")
        esig_ready, gates_ready, v_next_ready, v_ready = (
            sem("esig_ready"), sem("gates_ready"), sem("v_next_ready"), sem("v_ready"))
        in_scores, max_ready, exp_done = sem("in_scores"), sem("max_ready"), sem("exp_done")
        in_turned, turned_taken = sem("in_turned"), sem("turned_taken")
        in_att, attT_ready, y_ready = sem("in_att"), sem("attT_ready"), sem("y_ready")
        N_LOADS = 7

        block = ctx.enter_context(nc.Block())
        misc = PS[:, MISC, :]

        @block.sync
        def _(sp):
            sp.dma_start(wq[:, :], Wq).then_inc(w_loaded, 16)
            sp.dma_start(wk[:, :], Wk).then_inc(w_loaded, 16)
            sp.dma_start(wvg[:, 0:VC].rearrange("p (e k) -> p e k", e=E),
                         Wv.rearrange("e c k -> c e k")).then_inc(w_loaded, 16)
            sp.dma_start(wvg[:, VC:VC + GC], Ws).then_inc(w_loaded, 16)
            sp.dma_start(wvg[:, VC + GC:VC + 2 * GC], Wd).then_inc(w_loaded, 16)
            rows = Wo.rearrange("e k d -> (e k) d")
            sp.dma_start(wo[:, 0:2, :], rows[0:2 * P].rearrange("(a p) d -> p a d", p=P)).then_inc(w_loaded, 16)
            sp.wait_ge(pool_consts, 1)
            sp.dma_start(wo[0:VC - 2 * P, 2, :], rows[2 * P:VC]).then_inc(w_loaded, 16)

        @block.gpsimd
        def _(pool):
            nc.gpsimd.memset(wo[:, 2, :], 0.0).then_inc(pool_consts, 1)
            nc.gpsimd.memset(half[:, :], -0.5).then_inc(pool_consts, 1)
            nc.gpsimd.memset(kz[:, :, :, :], 0.0).then_inc(consts_ready, 1)
            nc.gpsimd.memset(y[:, :, :], 0.0).then_inc(consts_ready, 1)
            for j in range(E):
                nc.gpsimd.memset(later[:, j:j + 1], float(E - 1 - j)).then_inc(consts_ready, 1)
            pool.wait_ge(pool_consts, 2)

            def front(b):
                pool.wait_ge(ln_var, b + 1)
                nc.gpsimd.tensor_tensor(rstd[:, :], var_eps[:, :], half[:, 0:1].to_broadcast([P, T]),
                                        ALU.pow).then_inc(ln_rstd, 1)
                own = Chain(pool, pool_steps, b * (4 * T))
                pool.wait_ge(gates_ready, b + 1)
                for i in range(T):
                    own.only(nc.gpsimd.tensor_tensor(
                        vprod[:, :, :, :],
                        xvg[:, i, 0:VC].rearrange("p (a e k) -> p a e k", a=1, e=E).to_broadcast([P, H, E, DH]),
                        wv[:, i, :].rearrange("p (h e a) -> p h e a", h=H, a=1).to_broadcast([P, H, E, DH]),
                        ALU.mult))
                    own.ran(nc.gpsimd.tensor_tensor(vsum[:, 0], vprod[:, :, 0, :], vprod[:, :, 1, :], ALU.add))
                    own.ran(nc.gpsimd.tensor_tensor(vsum[:, 1], vprod[:, :, 2, :], vprod[:, :, 3, :], ALU.add))
                    own.sync()
                    own.only(nc.gpsimd.tensor_tensor(vsum[:, 0], vsum[:, 0], vsum[:, 1], ALU.add))
                    nc.gpsimd.tensor_tensor(v_next[:, i], vsum[:, 0], vprod[:, :, 4, :], ALU.add).then_inc(v_next_ready, 1)
                    pool.wait_ge(v_next_ready, b * T + i + 1)
                assert own.n == 4 * T

            front(0)
            with pool.Fori(0, B - 1) as b:
                front(b + 1)

        @block.scalar
        def _(act):
            def take(k):
                act.wait_ge(in_misc, k + 1)

            def head_exp(b, h, i):
                act.wait_ge(max_ready, (b * H + h) * T + i + 1)
                if i == 0:
                    yield_n = (b * H + h - 1) * T
                    if not (isinstance(b, int) and b == 0 and h < 2):
                        act.wait_ge(in_turned, yield_n)
                nc.scalar.activation(prob[:, h % 2, i, :], PS[:, i, :], ACT.Exp, bias=nmax[:, h % 2, i:i + 1],
                                     accum_out=den[:, h, i:i + 1]).then_inc(exp_done, 1)

            def head_turned(b, h, j):
                act.wait_ge(in_turned, (b * H + h) * T + j + 1)
                if j == 0 and not (isinstance(b, int) and b == 0 and h < 4):
                    act.wait_ge(in_att, b * PAIRS + h // 2 - 1)
                nc.scalar.activation(probT[:, h % 4, j, :], PS[:, 4 + j % 2, :], ACT.Copy).then_inc(turned_taken, 1)

            def pair_att(b, pr):
                act.wait_ge(in_att, b * PAIRS + pr + 1)
                nc.scalar.activation(attT[:, :], PS[:, 6, :], ACT.Copy).then_inc(attT_ready, 1)

            def run_use(name, b, k):
                if name == "xnT":
                    take(k)
                    nc.scalar.activation(xnT_next[:, :], misc, ACT.Copy).then_inc(misc_taken, 1)
                elif name[0] == "v":
                    i = int(name[1])
                    take(k)
                    nc.scalar.activation(xvg[:, i, :], misc[:, 0:VC + 2 * GC], ACT.Copy).then_inc(misc_taken, 1)
                    if i == T - 1:
                        act.wait_ge(misc_taken, k + 1)
                        nc.scalar.activation(esig[:, :, :], xvg[:, :, VC:VC + GC], ACT.Exp,
                                             scale=-1.0).then_inc(esig_ready, 1)
                elif name[0] == "q":
                    pr = int(name[1])
                    take(k)
                    if not (isinstance(b, int) and b == 0 and pr < 2):
                        act.wait_ge(in_scores, (b * PAIRS + pr - 1) * 2 * T)
                    nc.scalar.activation(q[:, pr % 2, :], misc, ACT.Copy, scale=SCALE).then_inc(misc_taken, 1)
                elif name[0] == "k":
                    pr = int(name[1])
                    take(k)
                    nc.scalar.activation(kz[0:DH, pr % 2, 0, :], misc[0:DH], ACT.Copy)
                    nc.scalar.activation(kz[DH:P, pr % 2, 1, :], misc[DH:P], ACT.Copy).then_inc(misc_taken, 1)
                elif name[0] == "y":
                    take(k)
                    nc.scalar.activation(yT[:, int(name[1]), :], misc, ACT.Copy).then_inc(misc_taken, 1)

            act.wait_ge(consts_ready, 2 + E)

            def move_xnT(b):
                nc.scalar.activation(xnT[:, :], xnT_next[:, :], ACT.Copy).then_inc(xnT_moved, 1)

            def batch(b, kind):
                for h in range(H):
                    nb, nh = (b, h + 1) if h + 1 < H else (b + 1, 0)
                    for i, at in enumerate(QUARTERS):
                        head_turned(b, h, i)
                        if h + 1 < H or kind != "last":
                            head_exp(nb, nh, i)
                        name, k = use_at(h, at, kind, b)
                        if name:
                            run_use(name, batch_of(name, b), k)
                    if h == 0 and kind != "first":
                        pair_att(b - 1, PAIRS - 1)
                    if h % 2 == 0 and h:
                        pair_att(b, h // 2 - 1)
                    name, k = use_at(h, "E", kind, b)
                    if name:
                        run_use(name, batch_of(name, b), k)
                    if h == 4 and kind != "last":
                        move_xnT(b + 1)

            for k, name in enumerate(PROLOGUE):
                run_use(name, 0, k)
                if name == "xnT":
                    act.wait_ge(misc_taken, 1)
                    move_xnT(0)
            for i in range(T):
                head_exp(0, 0, i)
            batch(0, "first")
            with act.Fori(1, B - 1) as b:
                batch(b, "middle")
            batch(B - 1, "last")
            pair_att(B - 1, PAIRS - 1)
            for n, name in enumerate(EPILOGUE):
                run_use(name, B - 1, misc_base("last", B - 1) + count("last") + n)

        @block.tensor
        def _(pe):
            def scores(b, h, i, k_use=None):
                if not (isinstance(b, int) and b == 0 and h == 0):
                    pe.wait_ge(exp_done, (b * H + h - 1) * T + i + 1)
                if i == 0 and h % 2 == 0:
                    pe.wait_ge(misc_taken, k_use + 1)
                pr = h // 2
                nc.tensor.matmul(PS[:, i, :], q[:, pr % 2, i * P:(i + 1) * P], kz[:, pr % 2, h % 2, :],
                                 start=True, stop=True).then_inc(in_scores, 1)

            def turn(b, h, j):
                if j == 0:
                    pe.wait_ge(exp_done, (b * H + h) * T + T)
                if not (isinstance(b, int) and b == 0 and h == 0 and j < 2):
                    pe.wait_ge(turned_taken, (b * H + h) * T + j - 1)
                for i in range(T):
                    last = nc.tensor.transpose(PS[:, 4 + j % 2, i * P:(i + 1) * P],
                                               prob[:, h % 2, i, j * P:(j + 1) * P], ident[:, :])
                last.then_inc(in_turned, 1)

            def half_product(b, pr, js):
                if pr == 0 and 0 in js:
                    pe.wait_ge(v_ready, b + 1)
                if 0 in js and not (isinstance(b, int) and b == 0 and pr == 0):
                    pe.wait_ge(attT_ready, b * PAIRS + pr)
                pe.wait_ge(turned_taken, (b * H + 2 * pr + 1) * T + js[-1] + 1)
                for j in js:
                    for hh in range(2):
                        h = 2 * pr + hh
                        last = nc.tensor.matmul(PS[hh * DH:(hh + 1) * DH, 6, :], v[:, j, h, :], probT[:, h % 4, j, :],
                                                start=(j == 0), stop=(j == T - 1), skip_group_check=True)
                if T - 1 in js:
                    last.then_inc(in_att, 1)

            def run_use(name, b, k):
                if not (isinstance(k, int) and k == 0):
                    pe.wait_ge(misc_taken, k)
                if name == "xnT":
                    pe.wait_ge(ln_done, b + 1)
                    for i in range(T):
                        last = nc.tensor.transpose(misc[:, i * P:(i + 1) * P], xn[:, i, :], ident[:, :])
                elif name[0] == "v":
                    i = int(name[1])
                    last = nc.tensor.matmul(misc[:, 0:VC + 2 * GC], xnT_next[:, i * P:(i + 1) * P], wvg[:, :],
                                            start=True, stop=True)
                elif name[0] in "qk":
                    pr = int(name[1])
                    pe.wait_ge(xnT_moved, b + 1)
                    wt = wq if name[0] == "q" else wk
                    last = nc.tensor.matmul(misc, wt[:, pr * P:(pr + 1) * P], xnT[:, :], start=True, stop=True)
                elif name[:4] == "back":
                    pe.wait_ge(attT_ready, b * PAIRS + int(name[4]) + 1)
                    for i in range(T):
                        last = nc.tensor.transpose(misc[:, i * P:(i + 1) * P], attT[:, i * P:(i + 1) * P], ident[:, :])
                elif name[0] == "y":
                    c = int(name[1])
                    if c == 0:
                        pe.wait_ge(y_ready, b + 1)
                    for i in range(T):
                        last = nc.tensor.transpose(misc[:, i * P:(i + 1) * P], y[:, i, c * P:(c + 1) * P], ident[:, :])
                elif name == "out":
                    for i in range(T):
                        for c in range(CH):
                            last = nc.tensor.matmul(misc[:, i * P:(i + 1) * P], yT[:, c, i * P:(i + 1) * P], wo[:, c, :],
                                                    start=(c == 0), stop=(c == CH - 1))
                last.then_inc(in_misc, 1)

            def batch(b, kind):
                k_use = None
                for h in range(H):
                    nb, nh = (b, h + 1) if h + 1 < H else (b + 1, 0)
                    for i, at in enumerate(QUARTERS):
                        if h + 1 < H or kind != "last":
                            scores(nb, nh, i, k_use)
                        turn(b, h, i)
                        name, k = use_at(h, at, kind, b)
                        if name:
                            run_use(name, batch_of(name, b), k)
                            if name[0] == "k":
                                k_use = k
                    if h % 2:
                        half_product(b, h // 2, (0, 1))
                    elif h:
                        half_product(b, h // 2 - 1, (2, 3))
                    elif kind != "first":
                        half_product(b - 1, PAIRS - 1, (2, 3))
                    name, k = use_at(h, "E", kind, b)
                    if name:
                        run_use(name, batch_of(name, b), k)

            pe.wait_ge(w_loaded, 16 * N_LOADS)
            for k, name in enumerate(PROLOGUE):
                run_use(name, 0, k)
            for i in range(T):
                scores(0, 0, i, len(PROLOGUE) - 1)
            batch(0, "first")
            with pe.Fori(1, B - 1) as b:
                batch(b, "middle")
            batch(B - 1, "last")
            half_product(B - 1, PAIRS - 1, (2, 3))
            for n, name in enumerate(EPILOGUE):
                run_use(name, B - 1, misc_base("last", B - 1) + count("last") + n)

        @block.vector
        def _(dve):
            def head_max(b, h, i):
                dve.wait_ge(in_scores, (b * H + h) * T + i + 1)
                nc.vector.tensor_reduce(nmax[:, h % 2, i:i + 1], PS[:, i, :], AX.X, ALU.max,
                                        negate=True).then_inc(max_ready, 1)

            def beats(own, i, taken):
                dve.wait_ge(misc_taken, taken)
                logit = xvg[:, i, VC:VC + 2 * GC].rearrange("p (h e) -> p h e", e=E)
                for d in range(1, E):
                    own.ran(nc.vector.tensor_tensor(wins[:, d - 1, i, :, 0:E - d], logit[:, :, 0:E - d],
                                                    logit[:, :, d:E], ALU.is_ge))
                if i == T - 1:
                    own.ran(nc.vector.tensor_copy(
                        beaten[:, :, :, :].rearrange("p i h e -> p (i h) e"),
                        later[:, :].rearrange("p (a e) -> p a e", a=1).to_broadcast([P, T * 2 * H, E])))

            def count_beaten(own, d):
                if d == 1:
                    own.sync()
                flat = beaten[:, :, :, :].rearrange("p i h e -> p (i h) e")
                won = wins[:, d - 1].rearrange("p i h e -> p (i h) e")[:, :, 0:E - d]
                own.only(nc.vector.tensor_tensor(flat[:, :, d:E], flat[:, :, d:E], won, ALU.add))
                own.only(nc.vector.tensor_tensor(flat[:, :, 0:E - d], flat[:, :, 0:E - d], won, ALU.subtract))

            def keep_mo(own):
                own.only(nc.vector.tensor_copy(mo[:, :, :, :], picked[:, :, H:2 * H, :]))

            def pick(own, b):
                own.ran(nc.vector.tensor_scalar(picked[:, :, :, :], beaten[:, :, :, :], 2.0, None, ALU.is_lt))
                dve.wait_ge(esig_ready, b + 1)
                own.only(nc.vector.tensor_scalar(sig[:, :, :], esig[:, :, :], 1.0, None, ALU.add))
                own.only(nc.vector.reciprocal(sig[:, :, :], sig[:, :, :]))
                nc.vector.tensor_tensor(wv[:, :, :].rearrange("p i (h e) -> p i h e", e=E), picked[:, :, 0:H, :],
                                        sig[:, :, :].rearrange("p i (h e) -> p i h e", e=E),
                                        ALU.mult).then_inc(gates_ready, 1)

            def take_v(b):
                if not (isinstance(b, int) and b == 0):
                    dve.wait_ge(in_att, b * PAIRS)
                dve.wait_ge(v_next_ready, (b + 1) * T)
                nc.vector.tensor_copy(v[:, :, :, :], v_next[:, :, :, :]).then_inc(v_ready, 1)

            def weights(own, b, pr):
                h0 = 2 * pr
                dve.wait_ge(exp_done, (b * H + h0 + 2) * T)
                own.only(nc.vector.reciprocal(rden[:, :, :], den[:, h0:h0 + 2, :]))
                for hh in range(2):
                    own.ran(nc.vector.tensor_tensor(
                        w[:, hh], mo[:, :, h0 + hh, :],
                        rden[:, hh, :].rearrange("p (i a) -> p i a", a=1).to_broadcast([P, T, E]), ALU.mult))

            def products(own, pr, k):
                own.sync()
                dve.wait_ge(in_misc, k + 1)
                att = misc.rearrange("p (i a h k) -> p i a h k", i=T, a=1, h=2)
                for hh in range(2):
                    dst = y[:, :, 0:VC] if pr == 0 and hh == 0 else yprod[:, hh]
                    ins = nc.vector.tensor_tensor(
                        dst.rearrange("p i (e k) -> p i e k", e=E),
                        att[:, :, :, hh, :].to_broadcast([P, T, E, DH]),
                        w[:, hh].rearrange("p i (e a) -> p i e a", a=1).to_broadcast([P, T, E, DH]), ALU.mult)
                    if hh == 0:
                        own.ran(ins)
                    else:
                        ins.then_inc(misc_taken, 1)

            def first_sum(own):
                own.sync()
                own.only(nc.vector.tensor_tensor(y[:, :, 0:VC], y[:, :, 0:VC], yprod[:, 0], ALU.add))

            def second_sum(own, pr, k):
                own.sync()
                dve.wait_ge(misc_taken, k + 1)
                ins = nc.vector.tensor_tensor(y[:, :, 0:VC], y[:, :, 0:VC], yprod[:, 1], ALU.add)
                if pr == PAIRS - 1:
                    ins.then_inc(y_ready, 1)
                else:
                    own.only(ins)

            def add_out(own, b, k):
                dve.wait_ge(in_misc, k + 1)
                nc.vector.tensor_tensor(X[:, b, :, :], misc.rearrange("p (i n) -> p i n", i=T), X[:, b, :, :],
                                        ALU.add).then_inc(misc_taken, 1)

            def front_stats(own, b):
                layernorm_stats(nc, own, X[:, b], stats, mv, var_eps).then_inc(ln_var, 1)

            def front_xn(own, b):
                dve.wait_ge(ln_rstd, b + 1)
                layernorm_apply(nc, X[:, b], xn, mv, rstd).then_inc(ln_done, 1)

            def piece(own, name, b, kind):
                what, n = name.rstrip("01234"), int(name[-1]) if name[-1].isdigit() else None
                at = batch_of(name, b)
                if name == "stats":
                    front_stats(own, at)
                elif name == "xn":
                    front_xn(own, at)
                elif name == "take_v":
                    take_v(at)
                elif name == "out":
                    add_out(own, at, number("out", kind, b))
                elif name == "pick":
                    keep_mo(own)
                    if kind != "last":
                        pick(own, b + 1)
                elif what == "beats":
                    beats(own, n, number("v%d" % n, kind, b) + 1)
                elif what == "count":
                    count_beaten(own, n)
                elif what == "weights":
                    weights(own, at, n)
                elif what == "products":
                    products(own, n, number("back%d" % n, kind, b))
                elif what == "first_sum":
                    first_sum(own)
                elif what == "second_sum":
                    second_sum(own, n, number("back%d" % n, kind, b))

            def batch(b, kind, base):
                own = Chain(dve, dve_steps, base)
                for h in range(H):
                    nb, nh = (b, h + 1) if h + 1 < H else (b + 1, 0)
                    for i, at in enumerate("ABCDE"):
                        if at != "E" and (h + 1 < H or kind != "last"):
                            head_max(nb, nh, i)
                        for name in PIECES[h].get(at, []):
                            if not skipped(name, kind):
                                piece(own, name, b, kind)
                assert own.n == own_steps(kind), (kind, own.n, own_steps(kind))

            COUNTED = {"stats": LN_STEPS, "beats": E - 1, "count": 2, "pick": 1 + 3,
                       "weights": 3, "products": 1, "first_sum": 1, "second_sum": 1}

            def own_steps(kind):
                names = [name for h in PIECES for at in PIECES[h] for name in PIECES[h][at] if not skipped(name, kind)]
                n = sum(COUNTED.get(name.rstrip("01234"), 0) for name in names)
                n += "beats3" in names
                n -= "second_sum3" in names
                return n - (3 if kind == "last" else 0)

            dve.wait_ge(consts_ready, 2 + E)
            own = Chain(dve, dve_steps, 0)
            front_stats(own, 0)
            front_xn(own, 0)
            for i in range(T):
                beats(own, i, PROLOGUE.index("v%d" % i) + 1)
            for d in range(1, E):
                count_beaten(own, d)
            pick(own, 0)
            for i in range(T):
                head_max(0, 0, i)
            n_start = own.n
            batch(0, "first", n_start)
            n_start += own_steps("first")
            n = own_steps("middle")
            with dve.Fori(1, B - 1) as b:
                batch(b, "middle", b * n + (n_start - n))
            n_start += (B - 2) * n
            batch(B - 1, "last", n_start)
            own = Chain(dve, dve_steps, n_start + own_steps("last"))
            base = misc_base("last", B - 1) + count("last")
            weights(own, B - 1, PAIRS - 1)
            products(own, PAIRS - 1, base)
            first_sum(own)
            second_sum(own, PAIRS - 1, base)
            add_out(own, B - 1, base + EPILOGUE.index("out"))


def phase_geometric_attention(nc, X, PS, ident, Wq, Wk, Wv, Wo, head_dirs, scale):
    H, D, HD = 16, 4, C // 16
    TERMS = ((0, 0), (0, 1), (0, 2), (1, 0), (1, 1), (2, 0))
    ROWS = len(TERMS) * D
    GR = 32
    NG = P // GR
    HALF = H // 2
    SL = NG
    VW = 32
    EX = T * (T + 1) // 2 * P
    NEG = -1e30
    S1A, S1B, S1C, S2A, OUTB, MISC = 0, 1, 2, 3, 6, 7
    BF16 = mybir.dt.bfloat16

    def plan(n):
        us = {h: [] for h in range(H)}

        def put(**slots):
            for name, h in slots.items():
                us[h].append(name)
        if 0 <= n < B:
            put(c1=1, back0=10, back1=14)
        if 1 <= n <= B:
            put(back2=2, back3=5, turn=7, out=8)
        if n + 1 < B:
            put(c0=9)
        if n + 2 < B:
            put(xnT=3, proj=4, v0=6, v1=11, v2=12, v3=13)
        return us

    START = ["xnT", "proj", "v0", "v1", "v2", "v3"]

    def n_uses(n):
        return sum(len(u) for u in plan(n).values())

    def place_of(k, name):
        return [u for us in plan(k).values() for u in us].index(name)

    def misc_base(n, k):
        if isinstance(n, int):
            return len(START) + sum(n_uses(m) for m in range(-1, n))
        return (n - 1) * n_uses(1) + misc_base(1, 1)

    with ExitStack() as ctx:
        def sb(name, shape, dt=F32):
            return ctx.enter_context(nc.sbuf_tensor("c_" + name, shape, dt))

        def sem(name):
            return ctx.enter_context(nc.semaphore("c_" + name))

        stack = nc.dram_tensor("c_stack", [B, 2, H, ROWS, S], BF16).ap()
        shifts = nc.dram_tensor("c_shifts", [B, 2, 3, HALF, S], BF16).ap()

        wq3, wk3 = sb("wq3", [P, H, 3]), sb("wk3", [P, H, 3])
        dirs, scale_sb = sb("dirs", [P, H, 3]), sb("scale", [P, 1])
        wdir = sb("wdir", [P, 2, H, 3])
        w4 = sb("w4", [P, 2, H, D])
        wv, wo = sb("wv", [P, C]), sb("wo", [P, C])
        half = sb("half", [P, 2])
        ident_bf = sb("ident_bf", [P, P], BF16)
        mask_ts, mask_st = sb("mask_ts", [P, P], BF16), sb("mask_st", [P, P], BF16)
        stats, mv = sb("stats", [P, T, 6]), sb("mv", [P, T, 2])
        var_eps, rstd = sb("var_eps", [P, T]), sb("rstd", [P, T])
        xn, xnT = sb("xn", [P, T, C]), sb("xnT", [P, S])
        parts, rest = sb("parts", [P, 3, S], BF16), sb("rest", [P, S])
        qx, k1, k2 = sb("qx", [P, 2, H, S], BF16), sb("k1", [P, 2, SL, S], BF16), sb("k2", [P, 2, SL, S], BF16)
        v_next, v = sb("v_next", [P, T, H, HD]), sb("v", [P, 2, T, H, VW])
        nmax = sb("nmax", [P, 2, T, HALF])
        cparts, crest = sb("cparts", [P, 3, S], BF16), sb("crest", [P, S])
        ex = sb("ex", [P, HALF, EX])
        oT = sb("oT", [P, S])
        rz = sb("rz", [P, T, NG])
        att, attT = sb("att", [P, T, C]), sb("attT", [P, S])

        w_loaded, w4_ready, consts_ready = sem("w_loaded"), sem("w4_ready"), sem("consts_ready")
        pool_consts, pool_steps, dve_steps = sem("pool_consts"), sem("pool_steps"), sem("dve_steps")
        ln_var, ln_rstd, ln_done = sem("ln_var"), sem("ln_rstd"), sem("ln_done")
        in_misc, misc_taken = sem("in_misc"), sem("misc_taken")
        part1_ready, part2_ready, part3_ready = sem("part1_ready"), sem("part2_ready"), sem("part3_ready")
        stack_written, stack_passed = sem("stack_written"), sem("stack_passed")
        pool_passed = sem("pool_passed")
        k1_loaded = sem("k1_loaded")
        qk_loaded = [sem("qk_loaded0"), sem("qk_loaded1")]
        c_part1, c_part2, c_part3 = sem("c_part1"), sem("c_part2"), sem("c_part3")
        c_written, c_loaded = sem("c_written"), [sem("c_loaded0"), sem("c_loaded1")]
        v_ready = sem("v_ready")
        in_first, max_done = sem("in_first"), sem("max_done")
        in_second, exp_done = sem("in_second"), sem("exp_done")
        in_out, oT_ready, att_ready = sem("in_out"), sem("oT_ready"), sem("att_ready")
        N_LOADS = 6

        block = ctx.enter_context(nc.Block())
        misc = PS[:, MISC, :]

        def steps_of(emit, j_loop):
            emit(-1, -1)
            emit(0, 0)
            with j_loop(0, (B - 4) // 2) as j:
                emit(j * 2 + 1, 1)
                emit(j * 2 + 2, 2)
            for n in range(B - 3, B + 1):
                emit(n, n)

        def batch_of(name, n):
            if name in ("xnT", "proj", "v0", "v1", "v2", "v3"):
                return n + 2
            if name == "c0":
                return n + 1
            if name in ("back2", "back3", "turn", "out"):
                return n - 1
            return n

        @block.sync
        def _(sp):
            def write_stack(b):
                sp.wait_ge(part2_ready, b + 1)
                sp.wait_ge(part3_ready, b + 1)
                for qk in range(2):
                    for t, term in enumerate(TERMS):
                        sp.dma_start(stack[b, qk, :, t * D:(t + 1) * D, :],
                                     parts[qk * H * D:(qk + 1) * H * D, term[qk], :]).then_inc(stack_written, 16)
                sp.wait_ge(stack_written, b * (2 * len(TERMS) * 16) + 2 * len(TERMS) * 16).then_inc(stack_passed, 1)

            def load_k1(b, par):
                if not (isinstance(b, int) and b < 2):
                    sp.wait_ge(in_first, (b - 1) * (3 * H))
                for g in range(NG):
                    sp.dma_start(k1[g * GR:g * GR + ROWS, par, :, :],
                                 stack[b, 1, g:H:NG].rearrange("s r n -> r s n")).then_inc(k1_loaded, 16)

            def load_qk(b, par, hf):
                if not (isinstance(b, int) and b < 2):
                    sp.wait_ge(in_second, (b - 2) * (2 * H) + (hf + 1) * H)
                s0, s1 = hf * SL // 2, (hf + 1) * SL // 2
                for g in range(NG):
                    rows = slice(g * GR, g * GR + ROWS)
                    sp.dma_start(qx[rows, par, s0 * NG + g:s1 * NG:NG, :],
                                 stack[b, 0, s0 * NG + g:s1 * NG:NG].rearrange("s r n -> r s n")).then_inc(qk_loaded[hf], 16)
                    sp.dma_start(k2[rows, par, s0:s1, :],
                                 stack[b, 1, s0 * NG + g:s1 * NG:NG].rearrange("s r n -> r s n")).then_inc(qk_loaded[hf], 16)

            def move_c(b, par, hf):
                sp.wait_ge(c_part2, b * 2 + hf + 1)
                sp.wait_ge(c_part3, b * 2 + hf + 1)
                sp.dma_start(shifts[b, hf].rearrange("a h n -> h a n"), cparts[0:HALF, :, :]).then_inc(c_written, 16)
                sp.wait_ge(c_written, b * 32 + (hf + 1) * 16)
                for g in range(NG):
                    sp.dma_start(qx[g * GR + ROWS:g * GR + ROWS + 3, par, hf * HALF + g:(hf + 1) * HALF:NG, :],
                                 shifts[b, hf, :, g:HALF:NG, :]).then_inc(c_loaded[hf], 16)

            for dst, src in ((wq3[:, :, :], Wq.rearrange("c (h d) -> c h d", d=3)),
                             (wk3[:, :, :], Wk.rearrange("c (h d) -> c h d", d=3)),
                             (wv[:, :], Wv), (wo[:, :], Wo),
                             (dirs[:, :, :].rearrange("p h d -> p (h d)"),
                              bcast_rows(head_dirs.rearrange("h d -> (h d)"), H * 3)),
                             (scale_sb[:, :], bcast_rows(scale, 1))):
                sp.dma_start(dst, src).then_inc(w_loaded, 16)
            sp.wait_ge(consts_ready, 8)
            write_stack(0)
            load_k1(0, 0)
            load_qk(0, 0, 0)
            load_qk(0, 0, 1)

            def step(n, k):
                if 0 <= k < B:
                    move_c(n, k % 2, 1)
                if k + 2 < B:
                    write_stack(n + 2)
                    load_k1(n + 2, k % 2)
                    load_qk(n + 2, k % 2, 0)
                if k + 1 < B:
                    move_c(n + 1, (k + 1) % 2, 0)
                if k + 2 < B:
                    load_qk(n + 2, k % 2, 1)

            steps_of(step, sp.Fori)

        @block.gpsimd
        def _(pool):
            own = Chain(pool, pool_consts, 0)
            own.ran(nc.gpsimd.memset(ident_bf[:, :], 0.0))
            own.ran(nc.gpsimd.memset(mask_ts[:, :], 0.0))
            own.ran(nc.gpsimd.memset(mask_st[:, :], 0.0))
            nc.gpsimd.memset(half[:, :], -0.5).then_inc(consts_ready, 1)
            nc.gpsimd.memset(v[:, :, :, :, :], 0.0).then_inc(pool_consts, 1)
            own.n += 1
            own.sync()
            nc.gpsimd.memset(v[:, :, :, :, HD:HD + 1], 1.0).then_inc(consts_ready, 1)
            nc.gpsimd.affine_select(out=ident_bf[:, :], in_=ident_bf[:, :], compare_op=ALU.not_equal, fill=1.0,
                                    base=0, pattern=[[-1, P]], channel_multiplier=1).then_inc(consts_ready, 1)
            nc.gpsimd.affine_select(out=mask_ts[:, :], in_=mask_ts[:, :], compare_op=ALU.is_ge, fill=NEG,
                                    base=0, pattern=[[-1, P]], channel_multiplier=1).then_inc(consts_ready, 1)
            nc.gpsimd.affine_select(out=mask_st[:, :], in_=mask_st[:, :], compare_op=ALU.is_ge, fill=NEG,
                                    base=0, pattern=[[1, P]], channel_multiplier=-1).then_inc(consts_ready, 1)
            pool.wait_ge(consts_ready, 8)

            def ln(b):
                pool.wait_ge(ln_var, b + 1)
                nc.gpsimd.tensor_tensor(rstd[:, :], var_eps[:, :], half[:, 0:1].to_broadcast([P, T]),
                                        ALU.pow).then_inc(ln_rstd, 1)

            def place_v(b, par, v_uses):
                pool.wait_ge(misc_taken, v_uses).then_inc(pool_passed, 1)
                if not (isinstance(b, int) and b < 2):
                    pool.wait_ge(in_out, (b - 1) * NG).then_inc(pool_passed, 1)
                nc.gpsimd.tensor_copy(v[:, par, :, :, 0:HD], v_next[:, :, :, :]).then_inc(v_ready, 1)

            def shift_parts(b, hf, n, k):
                pool.wait_ge(misc_taken, misc_base(n, k) + place_of(k, "c%d" % hf) + 1).then_inc(pool_passed, 1)
                nc.gpsimd.tensor_copy(cparts[0:HALF, 1, :], crest[0:HALF, :]).then_inc(c_part2, 1)
                pool.wait_ge(c_part2, b * 2 + hf + 1)
                nc.gpsimd.tensor_tensor(cparts[0:HALF, 2, :], crest[0:HALF, :], cparts[0:HALF, 1, :],
                                        ALU.subtract).then_inc(c_part3, 1)

            ln(0)
            place_v(0, 0, len(START))

            def step(n, k):
                if k + 2 < B:
                    ln(n + 2)
                if 0 <= k < B:
                    shift_parts(n, 1, n, k)
                if 0 <= k and k + 1 < B:
                    place_v(n + 1, (k + 1) % 2, misc_base(n, k))
                if k + 1 < B:
                    shift_parts(n + 1, 0, n, k)

            steps_of(step, pool.Fori)

        @block.scalar
        def _(act):
            def exps(b, h):
                if h % NG == 0 and not (isinstance(b, int) and b == 0 and h < HALF):
                    act.wait_ge(in_out, b * NG + h // NG - 1)
                e = h % HALF
                act.wait_ge(in_second, (b * H + h) * 2 + 1)
                nc.scalar.activation(ex[:, e, 0:BANK], PS[:, S2A, :], ACT.Exp).then_inc(exp_done, 1)
                act.wait_ge(in_second, (b * H + h) * 2 + 2)
                nc.scalar.activation(ex[:, e, BANK:EX],
                                     PS[:, S2A + 1:S2A + 3, :].rearrange("p a n -> p (a n)")[:, 0:EX - BANK],
                                     ACT.Exp).then_inc(exp_done, 1)

            def take_out(b, gr):
                act.wait_ge(in_out, b * NG + gr + 1)
                nc.scalar.activation(oT[:, :], PS[:, OUTB, :], ACT.Copy).then_inc(oT_ready, 1)

            def run_use(name, b, k, par):
                if name == "xnT":
                    act.wait_ge(in_misc, k + 1)
                    nc.scalar.activation(xnT[:, :], misc, ACT.Copy).then_inc(misc_taken, 1)
                elif name == "proj":
                    act.wait_ge(in_misc, k + 1)
                    if not (isinstance(b, int) and b == 0):
                        act.wait_ge(stack_written, b * (2 * len(TERMS) * 16))
                    nc.scalar.activation(parts[:, 0, :], misc, ACT.Copy).then_inc(part1_ready, 1)
                    act.wait_ge(misc_taken, k + 1)
                    nc.scalar.activation(parts[:, 1, :], rest[:, :], ACT.Copy).then_inc(part2_ready, 1)
                elif name[0] == "v":
                    i = int(name[1])
                    act.wait_ge(in_misc, k + 1)
                    if i == 0 and not (isinstance(b, int) and b == 0):
                        act.wait_ge(v_ready, b)
                    nc.scalar.activation(v_next[:, i, :, :].rearrange("p h g -> p (h g)"), misc[:, 0:C],
                                         ACT.Copy).then_inc(misc_taken, 1)
                elif name == "turn":
                    act.wait_ge(in_misc, k + 1)
                    nc.scalar.activation(attT[:, :], misc, ACT.Copy).then_inc(misc_taken, 1)
                elif name in ("c0", "c1"):
                    hf = int(name[1])
                    act.wait_ge(in_misc, k + 1)
                    n = b * 2 + hf
                    if not (isinstance(b, int) and b == 0 and hf == 0):
                        act.wait_ge(c_written, n * 16)
                    nc.scalar.activation(cparts[0:HALF, 0, :], misc[0:HALF, :], ACT.Copy).then_inc(c_part1, 1)

            act.wait_ge(consts_ready, 8)
            for k, name in enumerate(START):
                run_use(name, 0, k, 0)

            def step(n, k):
                m = misc_base(n, k)
                us = plan(k)
                for h in range(H):
                    if 0 <= k < B:
                        exps(n, h)
                    if h % NG == NG - 1:
                        if h >= NG and 0 <= k < B:
                            take_out(n, h // NG - 1)
                        elif h < NG and 1 <= k <= B:
                            take_out(n - 1, NG - 1)
                    for name in us[h]:
                        run_use(name, batch_of(name, n), m, 0)
                        m = m + 1

            steps_of(step, act.Fori)

        @block.tensor
        def _(pe):
            def first(b, h, par):
                if h == 0:
                    pe.wait_ge(k1_loaded, b * (NG * 16) + NG * 16)
                if h % HALF == 0:
                    pe.wait_ge(qk_loaded[h // HALF], b * (2 * NG * 16) + 2 * NG * 16)
                n4 = (b * H + h) * 4
                started = not (isinstance(b, int) and b == 0 and h == 0)
                q, kk = qx[:, par, h, :], k1[:, par, h // NG, :]

                def tile(bank, c0, i, start, stop):
                    nc.tensor.matmul(PS[:, bank, c0:c0 + (i + 1) * P], q[:, i * P:(i + 1) * P], kk[:, 0:(i + 1) * P],
                                     start=start, stop=False, skip_group_check=True)
                    return nc.tensor.matmul(PS[:, bank, c0 + i * P:c0 + (i + 1) * P], ident_bf[:, :], mask_ts[:, :],
                                            start=False, stop=stop, skip_group_check=True)
                if started:
                    pe.wait_ge(max_done, n4 - 3)
                tile(S1A, 0, 3, True, True).then_inc(in_first, 1)
                if started:
                    pe.wait_ge(max_done, n4 - 1)
                tile(S1B, 0, 2, True, False)
                tile(S1B, 3 * P, 0, False, True).then_inc(in_first, 1)
                if started:
                    pe.wait_ge(max_done, n4)
                tile(S1C, 0, 1, True, True).then_inc(in_first, 1)

            def second(b, h, par):
                if h % HALF == 0:
                    pe.wait_ge(c_loaded[h // HALF], b * (NG * 16) + NG * 16)
                n2 = (b * H + h) * 2
                started = not (isinstance(b, int) and b == 0 and h == 0)
                q, kk = qx[:, par, h, :], k2[:, par, h // NG, :]

                def tile(bank, c0, j, start, stop):
                    nc.tensor.matmul(PS[:, bank, c0:c0 + S - j * P], kk[:, j * P:(j + 1) * P], q[:, j * P:S],
                                     start=start, stop=False, skip_group_check=True)
                    return nc.tensor.matmul(PS[:, bank, c0:c0 + P], ident_bf[:, :], mask_st[:, :],
                                            start=False, stop=stop, skip_group_check=True)
                if started:
                    pe.wait_ge(exp_done, n2 - 1)
                tile(S2A, 0, 0, True, True).then_inc(in_second, 1)
                if started:
                    pe.wait_ge(exp_done, n2)
                tile(S2A + 1, 0, 1, True, False)
                tile(S2A + 1, 3 * P, 3, False, True)
                tile(S2A + 2, 0, 2, True, True).then_inc(in_second, 1)

            EXC = [0, BANK, 2 * BANK, BANK + 3 * P]

            def out_part(b, gr, j, par):
                if j == 0:
                    pe.wait_ge(exp_done, (b * H + (gr + 1) * NG) * 2)
                    if gr == 0:
                        pe.wait_ge(v_ready, b + 1)
                    if not (isinstance(b, int) and b == 0 and gr == 0):
                        pe.wait_ge(oT_ready, b * NG + gr)
                for g in range(NG):
                    h = gr * NG + g
                    last = nc.tensor.matmul(PS[g * VW:(g + 1) * VW, OUTB, j * P:S], v[:, par, j, h, :],
                                            ex[:, h % HALF, EXC[j]:EXC[j] + S - j * P],
                                            start=(j == 0), stop=(j == T - 1), skip_group_check=True)
                if j == T - 1:
                    last.then_inc(in_out, 1)

            def run_use(name, b, k):
                if not (isinstance(k, int) and k == 0):
                    pe.wait_ge(misc_taken, k)
                if name == "xnT":
                    pe.wait_ge(ln_done, b + 1)
                    for i in range(T):
                        last = nc.tensor.transpose(misc[:, i * P:(i + 1) * P], xn[:, i, :], ident[:, :])
                elif name == "proj":
                    last = nc.tensor.matmul(misc, w4[:, :, :, :].rearrange("p a h d -> p (a h d)"), xnT[:, :],
                                            start=True, stop=True)
                elif name[0] == "v":
                    i = int(name[1])
                    last = nc.tensor.matmul(misc[:, 0:C], xnT[:, i * P:(i + 1) * P], wv[:, :], start=True, stop=True)
                elif name in ("c0", "c1"):
                    hf = int(name[1])
                    pe.wait_ge(max_done, (b * H + (hf + 1) * HALF) * 4)
                    for i in range(T):
                        last = nc.tensor.transpose(misc[0:HALF, i * P:(i + 1) * P], nmax[:, hf, i, :], ident[:, :])
                elif name[:4] == "back":
                    pe.wait_ge(oT_ready, b * NG + int(name[4]) + 1)
                    for i in range(T):
                        last = nc.tensor.transpose(misc[:, i * P:(i + 1) * P], oT[:, i * P:(i + 1) * P], ident[:, :])
                elif name == "turn":
                    for i in range(T):
                        last = nc.tensor.transpose(misc[:, i * P:(i + 1) * P], att[:, i, :], ident[:, :])
                elif name == "out":
                    for i in range(T):
                        last = nc.tensor.matmul(misc[:, i * P:(i + 1) * P], attT[:, i * P:(i + 1) * P], wo[:, :],
                                                start=True, stop=True)
                last.then_inc(in_misc, 1)

            pe.wait_ge(w4_ready, 1)
            pe.wait_ge(consts_ready, 8)
            for k, name in enumerate(START):
                run_use(name, 0, k)

            def step(n, k):
                m = misc_base(n, k)
                us = plan(k)
                for h in range(H):
                    if k + 1 < B:
                        first(n + 1, h, (k + 1) % 2)
                    if 0 <= k < B:
                        second(n, h, k % 2)
                    if h >= NG and 0 <= k < B:
                        out_part(n, h // NG - 1, h % NG, k % 2)
                    elif h < NG and 1 <= k <= B:
                        out_part(n - 1, NG - 1, h % NG, (k - 1) % 2)
                    for name in us[h]:
                        run_use(name, batch_of(name, n), m)
                        m = m + 1

            steps_of(step, pe.Fori)

        @block.vector
        def _(dve):
            nc.vector.memset(qx[:, :, :, :], 0.0).then_inc(consts_ready, 1)
            nc.vector.memset(k1[:, :, :, :], 0.0).then_inc(consts_ready, 1)
            nc.vector.memset(k2[:, :, :, :], 1.0).then_inc(consts_ready, 1)
            dve.wait_ge(w_loaded, 16 * N_LOADS)
            own = Chain(dve, dve_steps, 0)
            for a, w3 in enumerate((wq3, wk3)):
                own.ran(nc.vector.tensor_tensor(wdir[:, a], w3[:, :, :], dirs[:, :, :], ALU.mult))
            own.ran(nc.vector.tensor_scalar(w4[:, 0, :, 0:3], wq3[:, :, :], scale_sb[:, 0:1], None, ALU.mult))
            own.ran(nc.vector.tensor_copy(w4[:, 1, :, 0:3], wk3[:, :, :]))
            own.sync()
            nc.vector.tensor_reduce(w4[:, :, :, 3], wdir[:, :, :, :], AX.X, ALU.add).then_inc(w4_ready, 1)

            def maxima(b, h):
                n4, n3, hf, hh = (b * H + h) * 4, (b * H + h) * 3, h // HALF, h % HALF

                def reduce(bank, c0, i):
                    nc.vector.tensor_reduce(nmax[:, hf, i, hh:hh + 1], PS[:, bank, c0:c0 + (i + 1) * P], AX.X, ALU.max,
                                            negate=True).then_inc(max_done, 1)
                dve.wait_ge(in_first, n3 + 1)
                reduce(S1A, 0, 3)
                dve.wait_ge(in_first, n3 + 2)
                reduce(S1B, 0, 2)
                reduce(S1B, 3 * P, 0)
                dve.wait_ge(in_first, n3 + 3)
                reduce(S1C, 0, 1)

            def stats_of(own, b):
                layernorm_stats(nc, own, X[:, b], stats, mv, var_eps).then_inc(ln_var, 1)

            def xn_of(b):
                dve.wait_ge(ln_rstd, b + 1)
                layernorm_apply(nc, X[:, b], xn, mv, rstd).then_inc(ln_done, 1)

            def run_use(own, name, b, k):
                if name == "proj":
                    dve.wait_ge(part1_ready, b + 1)
                    nc.vector.tensor_tensor(rest[:, :], misc, parts[:, 0, :], ALU.subtract).then_inc(misc_taken, 1)
                    dve.wait_ge(part2_ready, b + 1)
                    nc.vector.tensor_tensor(parts[:, 2, :], rest[:, :], parts[:, 1, :],
                                            ALU.subtract).then_inc(part3_ready, 1)
                elif name in ("c0", "c1"):
                    n = b * 2 + int(name[1])
                    dve.wait_ge(c_part1, n + 1)
                    nc.vector.tensor_tensor(crest[0:HALF, :], misc[0:HALF, :], cparts[0:HALF, 0, :],
                                            ALU.subtract).then_inc(misc_taken, 1)
                elif name[:4] == "back":
                    gr = int(name[4])
                    dve.wait_ge(in_misc, k + 1)
                    o = misc.rearrange("p (i g w) -> p i g w", i=T, g=NG)
                    own.only(nc.vector.reciprocal(rz[:, :, :], o[:, :, :, HD]))
                    ins = nc.vector.tensor_tensor(
                        att[:, :, gr * NG * HD:(gr + 1) * NG * HD].rearrange("p i (g w) -> p i g w", g=NG),
                        o[:, :, :, 0:HD],
                        rz[:, :, :].rearrange("p i (g a) -> p i g a", a=1).to_broadcast([P, T, NG, HD]), ALU.mult)
                    ins.then_inc(misc_taken, 1)
                elif name == "out":
                    dve.wait_ge(in_misc, k + 1)
                    nc.vector.tensor_tensor(X[:, b, :, :], misc.rearrange("p (i n) -> p i n", i=T), X[:, b, :, :],
                                            ALU.add).then_inc(misc_taken, 1)

            def n_steps(k):
                names = [u for us in plan(k).values() for u in us]
                return sum(u[:4] == "back" for u in names) + (LN_STEPS if k + 2 < B else 0)

            own = Chain(dve, dve_steps, 4)
            stats_of(own, 0)
            xn_of(0)
            for k, name in enumerate(START):
                run_use(own, name, 0, k)
            n_start = 4 + own.n

            def step(n, k):
                if isinstance(n, int):
                    base = n_start + sum(n_steps(m) for m in range(-1, n))
                else:
                    base = (n - 1) * n_steps(1) + n_start + sum(n_steps(m) for m in range(-1, 1))
                own = Chain(dve, dve_steps, base)
                m = misc_base(n, k)
                us = plan(k)
                for h in range(H):
                    if k + 1 < B:
                        maxima(n + 1, h)
                    if k + 2 < B:
                        if h == 0:
                            stats_of(own, n + 2)
                            xn_of(n + 2)
                    for name in us[h]:
                        run_use(own, name, batch_of(name, n), m)
                        m = m + 1
                assert own.n == n_steps(k), (k, own.n, n_steps(k))

            steps_of(step, dve.Fori)


def phase_expert_choice(nc, X, PS, ident, gate_w, gate_b, w1, w2, out):
    E, HID, TOP = 32, w1.shape[2], 8
    GB = P // E
    NGR = B // GB
    EG = E // GB
    BW = 32
    CH = HID // P
    HALF_S = -0.5
    with ExitStack() as ctx:
        def sb(name, shape):
            return ctx.enter_context(nc.sbuf_tensor("d_" + name, shape, F32))

        def sem(name):
            return ctx.enter_context(nc.semaphore("d_" + name))

        scratch = nc.dram_tensor("d_results", [E, BW, C], F32).ap()
        w1_sb, w2_sb = sb("w1", [P, E, HID]), sb("w2", [P, E, CH * C])
        b1, b2 = sb("b1", [P, HID]), sb("b2", [P, C])
        gw, gwT, gb = sb("gw", [E, C]), sb("gwT", [P, E]), sb("gb", [P, 1])
        half = sb("half", [P, 1])
        NT = GB * T
        stats, mv = sb("stats", [P, NT, 6]), sb("mv", [P, NT, 2])
        var_eps, rstd = sb("var_eps", [P, NT]), sb("rstd", [P, NT])
        xn, xnT = sb("xn", [P, NT, C]), sb("xnT", [P, GB, S])
        logit, nmax, total = sb("logit", [P, S]), sb("nmax", [P, 1]), sb("total", [P, 1])
        expo, rtotal, top = sb("expo", [P, S]), sb("rtotal", [P, 1]), sb("top", [P, TOP])
        picked, chosen = sb("picked", [P, S]), sb("chosen", [P, NGR, S])
        chosenT, merged = sb("chosenT", [P, T, P]), sb("merged", [P, C])
        mT = sb("mT", [P, E, BW])
        hid, hidT = sb("hid", [P, HID]), sb("hidT", [P, CH, P])
        res = sb("res", [P, 2, C])
        spread = xn[:, :, :].rearrange("p (g b) c -> p g b c", g=NGR)

        small_loaded, gw_turned, gwT_ready = sem("small_loaded"), sem("gw_turned"), sem("gwT_ready")
        w1_loaded = [sem("w1_loaded%d" % g) for g in range(EG)]
        w2_loaded = [sem("w2_loaded%d" % g) for g in range(EG)]
        zeroed, dve_steps = sem("zeroed"), sem("dve_steps")
        ln_var, ln_rstd, ln_done = sem("ln_var"), sem("ln_rstd"), sem("ln_done")
        in_xnT, xnT_ready = sem("in_xnT"), sem("xnT_ready")
        in_gate, nmax_ready, exp_ready, picked_ready = (
            sem("in_gate"), sem("nmax_ready"), sem("exp_ready"), sem("picked_ready"))
        chosen_kept = sem("chosen_kept")
        pool_passed = sem("pool_passed")
        in_turned, turned_ready, in_merged, merged_ready = (
            sem("in_turned"), sem("turned_ready"), sem("in_merged"), sem("merged_ready"))
        in_mT, mT_ready = sem("in_mT"), sem("mT_ready")
        in_hid, hid_ready, in_hidT, hidT_ready = sem("in_hid"), sem("hid_ready"), sem("in_hidT"), sem("hidT_ready")
        in_res, res_ready, res_written = sem("in_res"), sem("res_ready"), [sem("res_written0"), sem("res_written1")]
        spread_loaded = sem("spread_loaded")
        in_back, added, stored = sem("in_back"), sem("added"), sem("stored")
        N_SMALL = 3 + GB

        block = ctx.enter_context(nc.Block())

        @block.sync
        def _(sp):
            sp.dma_start(gw[:, :], gate_w).then_inc(small_loaded, 16)
            for g in range(GB):
                sp.dma_start(gb[g * E:(g + 1) * E, :], gate_b.rearrange("(e a) -> e a", a=1)).then_inc(small_loaded, 16)
            sp.wait_ge(zeroed, 2)
            sp.dma_start(b1[0:E, :], w1[:, C, :]).then_inc(small_loaded, 16)
            sp.dma_start(b2[0:E, :], w2[:, HID, :]).then_inc(small_loaded, 16)
            for g in range(EG):
                e = slice(g * GB, (g + 1) * GB)
                sp.dma_start(w1_sb[:, e, :], w1[e, 0:C, :].rearrange("e d h -> d e h")).then_inc(w1_loaded[g], 16)
                sp.dma_start(w2_sb[:, e, :], w2[e, 0:HID, :].rearrange("e (p c) o -> p e (c o)", c=CH)).then_inc(w2_loaded[g], 16)
            for g in range(EG):
                sp.wait_ge(res_ready, g + 1)
                sp.dma_start(scratch[g * GB:(g + 1) * GB].rearrange("e b o -> (e b) o"), res[:, g % 2, :])\
                    .then_inc(res_written[g % 2], 16)
            for half_of in res_written:
                sp.wait_ge(half_of, 16 * EG // 2)
            sp.wait_ge(zeroed, 5)
            for g in range(NGR):
                for b in range(GB):
                    sp.dma_start(spread[b * E:(b + 1) * E, g, b, :], scratch[:, g * GB + b, :]).then_inc(spread_loaded, 16)
            with sp.Fori(0, NGR) as g:
                sp.wait_ge(added, g * T + T)
                for b in range(GB):
                    sp.dma_start(out[g * GB + b].rearrange("(i p) c -> p i c", p=P), X[:, g * GB + b, :, :]).then_inc(stored, 16)
            sp.wait_ge(stored, 16 * B)

        @block.gpsimd
        def _(pool):
            nc.gpsimd.memset(b1[:, :], 0.0).then_inc(zeroed, 1)
            nc.gpsimd.memset(b2[:, :], 0.0).then_inc(zeroed, 1)
            nc.gpsimd.memset(half[:, :], HALF_S).then_inc(zeroed, 1)
            nc.gpsimd.memset(mT[:, :, :], 0.0).then_inc(zeroed, 1)
            pool.wait_ge(zeroed, 4)
            with pool.Fori(0, NGR) as g:
                pool.wait_ge(ln_var, g + 1)
                nc.gpsimd.tensor_tensor(rstd[:, :], var_eps[:, :], half[:, 0:1].to_broadcast([P, NT]),
                                        ALU.pow).then_inc(ln_rstd, 1)
                pool.wait_ge(picked_ready, g + 1).then_inc(pool_passed, 1)
                nc.gpsimd.tensor_copy(chosen[:, g, :], picked[:, :]).then_inc(chosen_kept, 1)
            pool.wait_ge(in_merged, NGR)
            nc.gpsimd.memset(xn[:, :, :], 0.0).then_inc(zeroed, 1)

        @block.scalar
        def _(act):
            act.wait_ge(gw_turned, 1)
            nc.scalar.activation(gwT[:, :], PS[:, 7, 0:E], ACT.Copy).then_inc(gwT_ready, 1)
            with act.Fori(0, NGR) as g:
                for b in range(GB):
                    act.wait_ge(in_xnT, g * GB + b + 1)
                    nc.scalar.activation(xnT[:, b, :], PS[:, b, :], ACT.Copy).then_inc(xnT_ready, 1)
                act.wait_ge(nmax_ready, g + 1)
                nc.scalar.activation(expo[:, :], logit[:, :], ACT.Exp, bias=nmax[:, 0:1],
                                     accum_out=total[:, 0:1]).then_inc(exp_ready, 1)
                act.wait_ge(in_turned, g + 1)
                nc.scalar.activation(chosenT[:, :, :].rearrange("p i n -> p (i n)"), PS[:, 5, :], ACT.Copy).then_inc(turned_ready, 1)
                act.wait_ge(in_merged, g + 1)
                nc.scalar.activation(merged[:, :], PS[:, 6, 0:C], ACT.Copy).then_inc(merged_ready, 1)
            for g in range(EG):
                act.wait_ge(in_hid, g + 1)
                if g:
                    act.wait_ge(in_hidT, g)
                nc.scalar.activation(hid[:, :], PS[:, g % 2, :], ACT.Gelu).then_inc(hid_ready, 1)

        @block.tensor
        def _(pe):
            pe.wait_ge(small_loaded, 16 * N_SMALL)
            nc.tensor.transpose(PS[:, 7, 0:E], gw[:, :], ident[0:E, 0:E]).then_inc(gw_turned, 1)
            pe.wait_ge(gwT_ready, 1)
            with pe.Fori(0, NGR) as g:
                pe.wait_ge(ln_done, g + 1)
                for b in range(GB):
                    for i in range(T):
                        last = nc.tensor.transpose(PS[:, b, i * P:(i + 1) * P], xn[:, b * T + i, :], ident[:, :])
                    last.then_inc(in_xnT, 1)
                pe.wait_ge(xnT_ready, g * GB + GB)
                for b in range(GB):
                    last = nc.tensor.matmul(PS[b * E:(b + 1) * E, 4, :], gwT[:, :], xnT[:, b, :], start=True, stop=True)
                last.then_inc(in_gate, 1)
                pe.wait_ge(picked_ready, g + 1)
                for i in range(T):
                    last = nc.tensor.transpose(PS[:, 5, i * P:(i + 1) * P], picked[:, i * P:(i + 1) * P], ident[:, :])
                last.then_inc(in_turned, 1)
                pe.wait_ge(turned_ready, g + 1)
                for i in range(T):
                    for b in range(GB):
                        last = nc.tensor.matmul(PS[b * E:(b + 1) * E, 6, 0:C], chosenT[:, i, b * E:(b + 1) * E],
                                                xn[:, b * T + i, :], start=(i == 0), stop=(i == T - 1), skip_group_check=True)
                last.then_inc(in_merged, 1)
                pe.wait_ge(merged_ready, g + 1)
                nc.tensor.transpose(PS[:, 7, 0:P], merged[:, :], ident[:, :]).then_inc(in_mT, 1)

            def hidden(g):
                if g == 0:
                    pe.wait_ge(mT_ready, NGR)
                pe.wait_ge(w1_loaded[g], 16)
                if g >= 2:
                    pe.wait_ge(hid_ready, g - 1)
                for e4 in range(GB):
                    nc.tensor.matmul(PS[e4 * BW:(e4 + 1) * BW, g % 2, :], mT[:, g * GB + e4, :], w1_sb[:, g * GB + e4, :],
                                     start=True, stop=False, skip_group_check=True)
                for e4 in range(GB):
                    e = g * GB + e4
                    last = nc.tensor.matmul(PS[e4 * BW:(e4 + 1) * BW, g % 2, :], ident[:, e:e + 1].to_broadcast([P, BW]),
                                            b1[:, :], start=False, stop=True, skip_group_check=True)
                last.then_inc(in_hid, 1)

            def result(g):
                pe.wait_ge(hid_ready, g + 1)
                if g:
                    pe.wait_ge(hidT_ready, g)
                for c in range(CH):
                    last = nc.tensor.transpose(PS[:, 2, c * P:(c + 1) * P], hid[:, c:HID:CH], ident[:, :])
                last.then_inc(in_hidT, 1)
                pe.wait_ge(hidT_ready, g + 1)
                pe.wait_ge(w2_loaded[g], 16)
                if g:
                    pe.wait_ge(res_ready, g)
                for c in range(CH):
                    for e4 in range(GB):
                        nc.tensor.matmul(PS[e4 * BW:(e4 + 1) * BW, 3, 0:C], hidT[:, c, e4 * BW:(e4 + 1) * BW],
                                         w2_sb[:, g * GB + e4, c * C:(c + 1) * C],
                                         start=(c == 0), stop=False, skip_group_check=True)
                for e4 in range(GB):
                    e = g * GB + e4
                    last = nc.tensor.matmul(PS[e4 * BW:(e4 + 1) * BW, 3, 0:C], ident[:, e:e + 1].to_broadcast([P, BW]),
                                            b2[:, :], start=False, stop=True, skip_group_check=True)
                last.then_inc(in_res, 1)

            hidden(0)
            for g in range(EG):
                if g + 1 < EG:
                    hidden(g + 1)
                result(g)

            pe.wait_ge(chosen_kept, NGR)
            pe.wait_ge(spread_loaded, 16 * B)
            for g in range(NGR):
                for i in range(T):
                    n = g * T + i
                    if n >= 4:
                        pe.wait_ge(added, n - 3)
                    nc.tensor.matmul(PS[:, 4 + n % 4, :], chosen[:, g, i * P:(i + 1) * P],
                                     spread[:, g, :, :].rearrange("p b c -> p (b c)"),
                                     start=True, stop=True).then_inc(in_back, 1)

        @block.vector
        def _(dve):
            dve.wait_ge(small_loaded, 16 * N_SMALL)
            dve.wait_ge(zeroed, 4)
            N_OWN = 2 * NT + 8
            with dve.Fori(0, NGR) as g:
                own = Chain(dve, dve_steps, g * N_OWN)
                x = [X[:, g * GB + n // T, n % T, :] for n in range(NT)]
                for n in range(NT):
                    own.ran(nc.vector.bn_stats(stats[:, n, :], x[n]))
                own.sync_apart()
                for n in range(NT):
                    own.ran(nc.vector.bn_aggr(mv[:, n, :], stats[:, n, :]))
                own.sync()
                nc.vector.tensor_scalar(var_eps[:, :], mv[:, :, 1], LN_EPS, None, ALU.add).then_inc(ln_var, 1)
                dve.wait_ge(ln_rstd, g + 1)
                for n in range(NT):
                    last = nc.vector.tensor_scalar(xn[:, n, :], x[n], mv[:, n, 0:1], rstd[:, n:n + 1],
                                                   ALU.subtract, ALU.mult)
                last.then_inc(ln_done, 1)
                dve.wait_ge(in_gate, g + 1)
                own.only(nc.vector.tensor_scalar(logit[:, :], PS[:, 4, :], gb[:, 0:1], None, ALU.add))
                nc.vector.tensor_reduce(nmax[:, 0:1], logit[:, :], AX.X, ALU.max, negate=True).then_inc(nmax_ready, 1)
                dve.wait_ge(exp_ready, g + 1)
                own.only(nc.vector.reciprocal(rtotal[:, :], total[:, :]))
                own.ran(nc.vector.tensor_scalar(expo[:, :], expo[:, :], rtotal[:, 0:1], None, ALU.mult))
                own.sync_apart()
                own.ran(nc.vector.max(top[:, :], expo[:, :]))
                own.sync_apart()
                own.only(nc.vector.match_replace(picked[:, :], top[:, :], expo[:, :], 0.0))
                nc.vector.tensor_tensor(picked[:, :], expo[:, :], picked[:, :], ALU.subtract).then_inc(picked_ready, 1)
                dve.wait_ge(in_mT, g + 1)
                for b in range(GB):
                    last = nc.vector.tensor_copy(mT[:, :, g * GB + b], PS[:, 7, b * E:(b + 1) * E])
                last.then_inc(mT_ready, 1)
                dve.wait_ge(chosen_kept, g + 1)
            for g in range(EG):
                dve.wait_ge(in_hidT, g + 1)
                if g:
                    dve.wait_ge(in_res, g)
                nc.vector.tensor_copy(hidT[:, :, :].rearrange("p c n -> p (c n)"), PS[:, 2, :]).then_inc(hidT_ready, 1)
                dve.wait_ge(in_res, g + 1)
                if g >= 2:
                    dve.wait_ge(res_written[g % 2], 16 * (g // 2))
                nc.vector.tensor_copy(res[:, g % 2, :], PS[:, 3, 0:C]).then_inc(res_ready, 1)
            for g in range(NGR):
                for i in range(T):
                    n = g * T + i
                    dve.wait_ge(in_back, n + 1)
                    xs = X[:, g * GB:(g + 1) * GB, i, :]
                    nc.vector.tensor_tensor(xs, PS[:, 4 + n % 4, :].rearrange("p (b c) -> p b c", b=GB), xs,
                                            ALU.add).then_inc(added, 1)


def program(nc, x, Wqkv, bqkv, gamma_q, beta_q, gamma_k, beta_k, Wo0, Wq, Wk, Ws, Wd, Wv, Wo1,
            wq, wk, wv, wo, head_dirs, scale, gate_w, gate_b, w1, w2, bo, out):
    with (nc.sbuf_tensor("x", [P, B, T, C], F32) as X, nc.sbuf_tensor("ident", [P, P], F32) as ident,
          nc.psum_tensor("banks", [P, 8, BANK], F32) as PS):
        phase_linear_attention(nc, X, PS, ident, x, Wqkv, bqkv, gamma_q, beta_q, gamma_k, beta_k, Wo0, bo)
        phase_head_mixture(nc, X, PS, ident, Wq, Wk, Ws, Wd, Wv, Wo1)
        phase_geometric_attention(nc, X, PS, ident, wq, wk, wv, wo, head_dirs, scale)
        phase_expert_choice(nc, X, PS, ident, gate_w, gate_b, w1, w2, out)


_INS = ["L0_attn_x", "L0_attn_Wqkv", "L0_attn_bqkv", "L0_attn_gamma_q", "L0_attn_beta_q", "L0_attn_gamma_k",
        "L0_attn_beta_k", "L0_attn_Wo", "L0_ffn_Wq", "L0_ffn_Wk", "L0_ffn_Ws", "L0_ffn_Wd", "L0_ffn_Wv",
        "L0_ffn_Wo", "L1_attn_wq", "L1_attn_wk", "L1_attn_wv", "L1_attn_wo", "L1_attn_head_dirs",
        "L1_attn_scale", "L1_ffn_gate_w", "L1_ffn_gate_b", "L1_ffn_w1", "L1_ffn_w2", "L0_attn_bo"]


def kernel(**inputs):
    import numpy as np
    import concourse.bacc as bacc
    from concourse.bass_utils import run_bass_kernel_spmd

    nc = bacc.Bacc("TRN2", target_bir_lowering=False, num_devices=1)
    arrays, args = {}, []
    for name in _INS:
        a = np.ascontiguousarray(inputs[name])
        arrays["in_" + name] = a
        args.append(nc.dram_tensor("in_" + name, a.shape, mybir.dt.from_np(a.dtype), kind="ExternalInput").ap())
    out = nc.dram_tensor("out", (B, S, C), F32, kind="ExternalOutput").ap()
    program(nc, *args, out)
    r = run_bass_kernel_spmd(nc, [arrays], core_ids=[0])
    return r.results[0]["out"]
```

```python
from contextlib import ExitStack

import concourse.bass as bass
import concourse.mybir as mybir

F32 = mybir.dt.float32
ALU = mybir.AluOpType
ACT = mybir.ActivationFunctionType
AX = mybir.AxisListType

P = 128
B, S, C = 16, 512, 128
T = S // P
BANK = 512
LN_EPS = 1e-5
LN_STEPS = 2 * T + 1


class Chain:

    def __init__(self, eng, sem, base):
        self.eng, self.sem, self.base, self.n = eng, sem, base, 0

    def ran(self, ins):
        self.n += 1
        ins.then_inc(self.sem, 1)

    def sync(self):
        self.eng.wait_ge(self.sem, self.base + self.n)

    def sync_apart(self):
        self.n += 1
        self.eng.wait_ge(self.sem, self.base + self.n - 1).then_inc(self.sem, 1)

    def only(self, ins):
        self.ran(ins)
        self.sync()


def bcast_rows(vec, n):
    return vec.rearrange("(a n) -> a n", a=1).to_broadcast([P, n])


def layernorm_stats(nc, own, x, stats, mv, var_eps):
    for i in range(T):
        own.ran(nc.vector.bn_stats(stats[:, i, :], x[:, i, :]))
    own.sync_apart()
    for i in range(T):
        own.ran(nc.vector.bn_aggr(mv[:, i, :], stats[:, i, :]))
    own.sync()
    return nc.vector.tensor_scalar(var_eps[:, :], mv[:, :, 1], LN_EPS, None, ALU.add)


def layernorm_apply(nc, x, xn, mv, rstd):
    for i in range(T):
        last = nc.vector.tensor_scalar(xn[:, i, :], x[:, i, :], mv[:, i, 0:1], rstd[:, i:i + 1],
                                       ALU.subtract, ALU.mult)
    return last


def phase_linear_attention(nc, X, PS, ident, x_in, Wqkv, bqkv, gamma_q, beta_q, gamma_k, beta_k, Wo, bo):
    H, D = 16, C // 16
    G = D + 1
    OUT = G * C
    THIRD = OUT // 3
    with ExitStack() as ctx:
        def sb(name, shape):
            return ctx.enter_context(nc.sbuf_tensor("a_" + name, shape, F32))

        def sem(name):
            return ctx.enter_context(nc.semaphore("a_" + name))

        wqkv, bqkv_bc = sb("wqkv", [P, 3 * C]), sb("bqkv_bc", [P, 3 * C])
        gamma, beta = sb("gamma", [P, 2, C]), sb("beta", [P, 2, C])
        wo, bo_bc = sb("wo", [P, C]), sb("bo_bc", [P, C])
        tri, last_row = sb("tri", [P, P]), sb("last_row", [P, P])
        half, minus_one = sb("half", [P, 2]), sb("minus_one", [P, 1])
        stats, mv = sb("stats", [P, T, 6]), sb("mv", [P, T, 2])
        var_eps, rstd = sb("var_eps", [P, T]), sb("rstd", [P, T])
        scaled_mean, shift = sb("scaled_mean", [P, T]), sb("shift", [P, T])
        xn, xnT = sb("xn", [P, T, C]), sb("xnT", [P, S])
        qkv, vone = sb("qkv", [P, 2, T, 2, C]), sb("vone", [P, 2, T, H, G])
        feat, outer = sb("feat", [P, 2, T, 2, C]), sb("outer", [P, 2, T, OUT])
        qmv = sb("qmv", [P, 2, T, 2, 2])
        qstats = sb("qstats", [P, T, 2, 6])
        qvar, qstd = sb("qvar", [P, T, 2]), sb("qstd", [P, T, 2])
        qstde, qrstd = sb("qstde", [P, T, 2]), sb("qrstd", [P, T, 2])
        qshift = sb("qshift", [P, T, 2])
        normed, scaled, shifted = sb("normed", [P, T, 2, C]), sb("scaled", [P, 2, 2, C]), sb("shifted", [P, T, 2, C])
        cum = sb("cum", [P, 2, OUT])
        prod, sums = sb("prod", [P, 2, OUT]), sb("sums", [P, T, G * H])
        zeps, rz = sb("zeps", [P, T, H]), sb("rz", [P, T, H])
        att, attT = sb("att", [P, T, C]), sb("attT", [P, S])

        w_loaded, x_loaded, x_passed = sem("w_loaded"), sem("x_loaded"), sem("x_passed")
        consts_ready, pool_steps, dve_steps = sem("consts_ready"), sem("pool_steps"), sem("dve_steps")
        ln_var, ln_shift, ln_done = sem("ln_var"), sem("ln_shift"), sem("ln_done")
        xnT_in_psum, xnT_ready = sem("xnT_in_psum"), sem("xnT_ready")
        qkv_in_psum, qkv_taken = sem("qkv_in_psum"), sem("qkv_taken")
        qk_var, qk_std, qk_shift, qk_normed = sem("qk_var"), sem("qk_std"), sem("qk_shift"), sem("qk_normed")
        qk_shifted, feat_ready = sem("qk_shifted"), sem("feat_ready")
        outer_ready, cum_in_psum, cum_ready = sem("outer_ready"), sem("cum_in_psum"), sem("cum_ready")
        cum_used, att_ready = sem("cum_used"), sem("att_ready")
        attT_in_psum, attT_ready = sem("attT_in_psum"), sem("attT_ready")
        biased, y_in_psum, x_added = sem("biased"), sem("y_in_psum"), sem("x_added")
        N_LOADS = 8

        block = ctx.enter_context(nc.Block())
        TURN, OUTB = 6, 7

        def cum_banks(i):
            return PS[:, 3 * (i % 2):3 * (i % 2) + 3, 0:THIRD]

        def stages(k):
            return {"S": 0 < k + 3 < B, "A": 0 <= k + 2 < B, "B": 0 <= k + 1 < B, "C": 0 <= k < B, "D": 0 <= k - 1 < B}

        def steps_of(emit, eng):
            for n in (-2, -1, 0):
                emit(n, n)
            with eng.Fori(0, (B - 4) // 2) as j:
                emit(j * 2 + 1, 1)
                emit(j * 2 + 2, 2)
            for n in range(B - 3, B + 1):
                emit(n, n)

        @block.sync
        def _(sp):
            with sp.Fori(0, B) as b:
                sp.dma_start(X[:, b, :, :], x_in[b].rearrange("(i p) c -> p i c", p=P)).then_inc(x_loaded, 16)
                sp.wait_ge(x_loaded, b * 16 + 16).then_inc(x_passed, 1)

        @block.gpsimd
        def _(pool):
            own = Chain(pool, pool_steps, 0)
            own.ran(nc.gpsimd.memset(tri[:, :], 1.0))
            own.ran(nc.gpsimd.memset(last_row[:, :], 1.0))
            own.ran(nc.gpsimd.memset(ident[:, :], 0.0))
            own.ran(nc.gpsimd.memset(half[:, 0:1], 0.5))
            own.ran(nc.gpsimd.memset(half[:, 1:2], -0.5))
            own.ran(nc.gpsimd.memset(minus_one[:, :], -1.0))
            own.ran(nc.gpsimd.memset(vone[:, :, :, :, D:G], 1.0))
            own.sync()
            nc.gpsimd.affine_select(out=tri[:, :], in_=tri[:, :], compare_op=ALU.is_ge, fill=0.0, base=0,
                                    pattern=[[1, P]], channel_multiplier=-1).then_inc(consts_ready, 1)
            nc.gpsimd.affine_select(out=last_row[:, :], in_=last_row[:, :], compare_op=ALU.is_ge, fill=0.0,
                                    base=1 - P, pattern=[[0, P]], channel_multiplier=1).then_inc(consts_ready, 1)
            nc.gpsimd.affine_select(out=ident[:, :], in_=ident[:, :], compare_op=ALU.not_equal, fill=1.0,
                                    base=0, pattern=[[-1, P]], channel_multiplier=1).then_inc(consts_ready, 1)
            N_CONSTS = own.n

            def shift_of(own, b):
                pool.wait_ge(ln_var, b + 1)
                own.only(nc.gpsimd.tensor_tensor(rstd[:, :], var_eps[:, :], half[:, 1:2].to_broadcast([P, T]), ALU.pow))
                own.only(nc.gpsimd.tensor_tensor(scaled_mean[:, :], mv[:, :, 0], rstd[:, :], ALU.mult))
                nc.gpsimd.tensor_tensor(shift[:, :], scaled_mean[:, :], minus_one[:, 0:1].to_broadcast([P, T]),
                                        ALU.mult).then_inc(ln_shift, 1)

            def qk_std_of(b):
                pool.wait_ge(qk_var, b + 1)
                nc.gpsimd.tensor_tensor(qstd[:, :, :].rearrange("p i a -> p (i a)"), qvar[:, :, :].rearrange("p i a -> p (i a)"),
                                        half[:, 0:1].to_broadcast([P, 2 * T]), ALU.pow).then_inc(qk_std, 1)

            def affine(own, b, i):
                pool.wait_ge(qk_normed, b * T + i + 1)
                own.only(nc.gpsimd.tensor_tensor(scaled[:, i % 2], normed[:, i], gamma[:, :, :], ALU.mult))
                nc.gpsimd.tensor_tensor(shifted[:, i], scaled[:, i % 2], beta[:, :, :], ALU.add).then_inc(qk_shifted, 1)

            def outer_product(b, i, par, first):
                pool.wait_ge(feat_ready, b * T + i + 1)
                if i == 0 and not first:
                    pool.wait_ge(cum_in_psum, (b - 1) * T)
                nc.gpsimd.tensor_tensor(
                    outer[:, par, i, :].rearrange("p (g h f) -> p g h f", g=G, h=H),
                    feat[:, par, i, 1, :].rearrange("p (a h f) -> p a h f", a=1, h=H).to_broadcast([P, G, H, D]),
                    vone[:, par, i, :, :].rearrange("p h (g a) -> p g h a", a=1).to_broadcast([P, G, H, D]),
                    ALU.mult).then_inc(outer_ready, 1)

            def add_bias(b):
                pool.wait_ge(ln_done, b + 1)
                nc.gpsimd.tensor_tensor(X[:, b, :, :], X[:, b, :, :],
                                        bo_bc[:, :].rearrange("p (a n) -> p a n", a=1).to_broadcast([P, T, C]),
                                        ALU.add).then_inc(biased, 1)

            def step(n, k):
                on, par, first = stages(k), (k + 1) % 2, k + 1 < 2
                if isinstance(n, int):
                    base = max(n + 1, 0) * T + min(n + 3, B) * 2 + N_CONSTS
                else:
                    base = n * (T + 2) + (T + 3 * 2 + N_CONSTS)
                own = Chain(pool, pool_steps, base)
                if on["B"]:
                    qk_std_of(n + 1)
                if on["B"]:
                    affine(own, n + 1, 0)
                    affine(own, n + 1, 1)
                    outer_product(n + 1, 0, par, first)
                    affine(own, n + 1, 2)
                    outer_product(n + 1, 1, par, first)
                    affine(own, n + 1, 3)
                    outer_product(n + 1, 2, par, first)
                if on["A"]:
                    add_bias(n + 2)
                if on["B"]:
                    outer_product(n + 1, 3, par, first)
                if on["S"]:
                    shift_of(own, n + 3)

            shift_of(Chain(pool, pool_steps, N_CONSTS), 0)
            pool.wait_ge(w_loaded, 16 * N_LOADS)
            steps_of(step, pool)

        @block.scalar
        def _(act):
            loads = ((wqkv[:, :], Wqkv), (bqkv_bc[:, :], bcast_rows(bqkv, 3 * C)),
                     (gamma[:, 0, :], bcast_rows(gamma_q, C)), (gamma[:, 1, :], bcast_rows(gamma_k, C)),
                     (beta[:, 0, :], bcast_rows(beta_q, C)), (beta[:, 1, :], bcast_rows(beta_k, C)),
                     (wo[:, :], Wo), (bo_bc[:, :], bcast_rows(bo, C)))
            for dst, src in loads:
                act.dma_start(dst, src).then_inc(w_loaded, 16)

            def normalise(b):
                act.wait_ge(ln_shift, b + 1)
                for i in range(T):
                    last = nc.scalar.activation(xn[:, i, :], X[:, b, i, :], ACT.Identity, bias=shift[:, i:i + 1],
                                                scale=rstd[:, i:i + 1])
                last.then_inc(ln_done, 1)

            def qk_normalise(b, i, par):
                act.wait_ge(qk_shift, b + 1)
                for a in range(2):
                    last = nc.scalar.activation(normed[:, i, a, :], qkv[:, par, i, a, :], ACT.Identity,
                                                bias=qshift[:, i, a:a + 1], scale=qrstd[:, i, a:a + 1])
                last.then_inc(qk_normed, 1)

            def take_xnT(b):
                act.wait_ge(xnT_in_psum, b + 1)
                nc.scalar.activation(xnT[:, :], PS[:, TURN, :], ACT.Copy).then_inc(xnT_ready, 1)

            def square(b, i, par, first):
                act.wait_ge(qk_shifted, b * T + i + 1)
                if i == 0 and not first:
                    act.wait_ge(cum_used, (b - 1) * T)
                nc.scalar.activation(feat[:, par, i, :, :], shifted[:, i], ACT.Square).then_inc(feat_ready, 1)

            def take_cum(b, i, first):
                act.wait_ge(cum_in_psum, b * T + i + 1)
                if i >= 2 or not first:
                    act.wait_ge(cum_used, b * T + i - 1)
                nc.scalar.activation(cum[:, i % 2, :].rearrange("p (a n) -> p a n", a=3), cum_banks(i),
                                     ACT.Copy).then_inc(cum_ready, 1)

            def take_attT(b):
                act.wait_ge(attT_in_psum, b + 1)
                nc.scalar.activation(attT[:, :], PS[:, TURN, :], ACT.Copy).then_inc(attT_ready, 1)

            def step(n, k):
                on, par, first = stages(k), (k + 1) % 2, k + 1 < 2
                if on["C"]:
                    take_cum(n, 0, k == 0)
                if on["A"]:
                    normalise(n + 2)
                if on["B"]:
                    qk_normalise(n + 1, 0, par)
                    qk_normalise(n + 1, 1, par)
                if on["C"]:
                    take_cum(n, 1, k == 0)
                if on["B"]:
                    qk_normalise(n + 1, 2, par)
                    qk_normalise(n + 1, 3, par)
                    square(n + 1, 0, par, first)
                    square(n + 1, 1, par, first)
                if on["C"]:
                    take_cum(n, 2, k == 0)
                if on["D"]:
                    take_attT(n - 1)
                if on["A"]:
                    take_xnT(n + 2)
                if on["B"]:
                    square(n + 1, 2, par, first)
                    square(n + 1, 3, par, first)
                if on["C"]:
                    take_cum(n, 3, k == 0)

            steps_of(step, act)

        @block.tensor
        def _(pe):
            def turn_xn(b, after_att):
                pe.wait_ge(ln_done, b + 1)
                if after_att:
                    pe.wait_ge(attT_ready, b - 2)
                elif not (isinstance(b, int) and b == 0):
                    pe.wait_ge(qkv_taken, b * T)
                for i in range(T):
                    last = nc.tensor.transpose(PS[:, TURN, i * P:(i + 1) * P], xn[:, i, :], ident[:, :])
                last.then_inc(xnT_in_psum, 1)

            def project(b, i, after_out):
                if i == 0:
                    pe.wait_ge(xnT_ready, b + 1)
                elif i == 1:
                    if after_out:
                        pe.wait_ge(x_added, b - 2)
                    elif not (isinstance(b, int) and b == 0):
                        pe.wait_ge(qkv_taken, b * T)
                else:
                    pe.wait_ge(qkv_taken, b * T + i - 1)
                nc.tensor.matmul(PS[:, (TURN, OUTB)[i % 2], 0:3 * C], xnT[:, i * P:(i + 1) * P], wqkv[:, :],
                                 start=True, stop=True).then_inc(qkv_in_psum, 1)

            def tile_sums(b, i, par, first):
                if i >= 2 or not first:
                    pe.wait_ge(cum_ready, b * T + i - 1)
                pe.wait_ge(outer_ready, b * T + i + 1)
                for j in range(3):
                    last = nc.tensor.matmul(cum_banks(i)[:, j, :], tri[:, :], outer[:, par, i, j * THIRD:(j + 1) * THIRD],
                                            start=True, stop=(i == 0), skip_group_check=True)
                if i == 0:
                    last.then_inc(cum_in_psum, 1)

            def carry(b, i):
                pe.wait_ge(cum_ready, b * T + i)
                for j in range(3):
                    last = nc.tensor.matmul(cum_banks(i)[:, j, :], last_row[:, :],
                                            cum[:, (i - 1) % 2, j * THIRD:(j + 1) * THIRD], start=False, stop=True,
                                            skip_group_check=True)
                last.then_inc(cum_in_psum, 1)

            def turn_att(b, projected):
                pe.wait_ge(att_ready, b + 1)
                if projected:
                    pe.wait_ge(qkv_taken, (b + 3) * T)
                for i in range(T):
                    last = nc.tensor.transpose(PS[:, TURN, i * P:(i + 1) * P], att[:, i, :], ident[:, :])
                last.then_inc(attT_in_psum, 1)

            def output(b, projected):
                pe.wait_ge(attT_ready, b + 1)
                if not projected:
                    pe.wait_ge(x_added, b)
                for i in range(T):
                    last = nc.tensor.matmul(PS[:, OUTB, i * P:(i + 1) * P], attT[:, i * P:(i + 1) * P], wo[:, :],
                                            start=True, stop=True)
                last.then_inc(y_in_psum, 1)

            pe.wait_ge(consts_ready, 3)
            pe.wait_ge(w_loaded, 16 * N_LOADS)

            def step(n, k):
                on, par, first = stages(k), k % 2, k == 0
                if on["C"]:
                    tile_sums(n, 0, par, first)
                    tile_sums(n, 1, par, first)
                    carry(n, 1)
                    tile_sums(n, 2, par, first)
                    carry(n, 2)
                if on["D"]:
                    turn_att(n - 1, 0 <= k + 1 < B)
                if on["A"]:
                    turn_xn(n + 2, on["D"])
                if on["D"]:
                    output(n - 1, 0 <= k + 1 < B)
                if on["A"]:
                    project(n + 2, 0, on["D"])
                if on["C"]:
                    tile_sums(n, 3, par, first)
                if on["A"]:
                    project(n + 2, 1, on["D"])
                if on["C"]:
                    carry(n, 3)
                if on["A"]:
                    project(n + 2, 2, on["D"])
                    project(n + 2, 3, on["D"])

            steps_of(step, pe)

        @block.vector
        def _(dve):
            def token_stats(own, b):
                dve.wait_ge(x_loaded, b * 16 + 16)
                if not (isinstance(b, int) and b == 0):
                    dve.wait_ge(ln_shift, b)
                layernorm_stats(nc, own, X[:, b], stats, mv, var_eps).then_inc(ln_var, 1)

            def take_qkv(own, b, i, par, first):
                if i == 0 and not first:
                    dve.wait_ge(outer_ready, (b - 1) * T)
                dve.wait_ge(qkv_in_psum, b * T + i + 1)
                bank = PS[:, (TURN, OUTB)[i % 2], :]
                own.ran(nc.vector.tensor_tensor(qkv[:, par, i, :, :], bank[:, 0:2 * C].rearrange("p (a n) -> p a n", a=2),
                                                bqkv_bc[:, 0:2 * C].rearrange("p (a n) -> p a n", a=2), ALU.add))
                nc.vector.tensor_tensor(vone[:, par, i, :, 0:D], bank[:, 2 * C:3 * C].rearrange("p (h g) -> p h g", h=H),
                                        bqkv_bc[:, 2 * C:3 * C].rearrange("p (h g) -> p h g", h=H),
                                        ALU.add).then_inc(qkv_taken, 1)

            def qk_stats(own, par):
                own.sync()
                for i in range(T):
                    for a in range(2):
                        own.ran(nc.vector.bn_stats(qstats[:, i, a, :], qkv[:, par, i, a, :]))
                own.sync_apart()
                for i in range(T):
                    for a in range(2):
                        own.ran(nc.vector.bn_aggr(qmv[:, par, i, a, :], qstats[:, i, a, :]))
                own.sync()
                nc.vector.tensor_scalar(qvar[:, :, :], qmv[:, par, :, :, 1], C / (C - 1.0), None,
                                        ALU.mult).then_inc(qk_var, 1)

            def qk_shift_of(own, b, par, first):
                dve.wait_ge(qk_std, b + 1)
                if not first:
                    dve.wait_ge(qk_normed, b * T)
                own.only(nc.vector.tensor_scalar(qstde[:, :, :], qstd[:, :, :], 1e-6, None, ALU.add))
                own.only(nc.vector.reciprocal(qrstd[:, :, :], qstde[:, :, :]))
                nc.vector.scalar_tensor_tensor(out=qshift[:, :, :], in0=qmv[:, par, :, :, 0], scalar=-1.0,
                                               in1=qrstd[:, :, :], op0=ALU.mult, op1=ALU.mult).then_inc(qk_shift, 1)

            def use_cum(own, b, i, par):
                dve.wait_ge(cum_ready, b * T + i + 1)
                nc.vector.tensor_tensor(
                    prod[:, i % 2, :].rearrange("p (g n) -> p g n", g=G),
                    cum[:, i % 2, :].rearrange("p (g n) -> p g n", g=G),
                    feat[:, par, i, 0, :].rearrange("p (g n) -> p g n", g=1).to_broadcast([P, G, C]),
                    ALU.mult).then_inc(cum_used, 1)
                dve.wait_ge(cum_used, b * T + i + 1)
                own.ran(nc.vector.tensor_reduce(sums[:, i, :], prod[:, i % 2, :].rearrange("p (n f) -> p n f", f=D),
                                                AX.X, ALU.add))

            def divide(own, b, first):
                own.sync()
                own.only(nc.vector.tensor_scalar(zeps[:, :, :], sums[:, :, C:C + H], 1e-6, None, ALU.add))
                own.only(nc.vector.reciprocal(rz[:, :, :], zeps[:, :, :]))
                if not first:
                    dve.wait_ge(attT_in_psum, b)
                nc.vector.tensor_tensor(
                    att[:, :, :].rearrange("p i (h g) -> p i g h", g=D),
                    sums[:, :, 0:C].rearrange("p i (g h) -> p i g h", h=H),
                    rz[:, :, :].rearrange("p i (a h) -> p i a h", a=1).to_broadcast([P, T, D, H]),
                    ALU.mult).then_inc(att_ready, 1)

            def add_output(b):
                dve.wait_ge(biased, b + 1)
                dve.wait_ge(y_in_psum, b + 1)
                nc.vector.tensor_tensor(X[:, b, :, :], PS[:, OUTB, :].rearrange("p (i n) -> p i n", i=T),
                                        X[:, b, :, :], ALU.add).then_inc(x_added, 1)

            N_S, N_A, N_B, N_C, N_D = LN_STEPS, T + 4 * T + 1, 2, T - 1, 3

            def own_steps(k):
                on = stages(k)
                return N_S * on["S"] + N_A * on["A"] + N_B * on["B"] + N_C * on["C"] + N_D * on["D"]

            def step(n, k):
                on, par = stages(k), k % 2
                base = N_S + sum(own_steps(m) for m in range(-2, k))
                own = Chain(dve, dve_steps, base if isinstance(n, int) else (n - k) * own_steps(1) + base)
                if on["D"]:
                    use_cum(own, n - 1, T - 1, 1 - par)
                if on["B"]:
                    qk_shift_of(own, n + 1, 1 - par, k + 1 == 0)
                if on["D"]:
                    divide(own, n - 1, k == 1)
                if on["C"]:
                    use_cum(own, n, 0, par)
                    use_cum(own, n, 1, par)
                if on["D"]:
                    add_output(n - 1)
                if on["C"]:
                    use_cum(own, n, 2, par)
                if on["A"]:
                    take_qkv(own, n + 2, 0, par, k + 2 < 2)
                    take_qkv(own, n + 2, 1, par, k + 2 < 2)
                if on["S"]:
                    token_stats(own, n + 3)
                if on["A"]:
                    take_qkv(own, n + 2, 2, par, k + 2 < 2)
                    take_qkv(own, n + 2, 3, par, k + 2 < 2)
                    qk_stats(own, par)
                assert own.n == own_steps(k), (k, own.n, own_steps(k))

            token_stats(Chain(dve, dve_steps, 0), 0)
            dve.wait_ge(w_loaded, 16 * N_LOADS)
            dve.wait_ge(pool_steps, 7)
            steps_of(step, dve)


def phase_head_mixture(nc, X, PS, ident, Wq, Wk, Ws, Wd, Wv, Wo):
    H, DH, E = 8, 64, 5
    PAIRS = H // 2
    VC = E * DH
    GC = H * E
    SCALE = float(DH) ** -0.5
    CH = 3
    MISC = 7

    USES = {0: {"A": "q1", "B": "k1", "D": "xnT", "E": "v0"},
            1: {"A": "v1", "B": "v2", "C": "v3", "D": "back3"},
            2: {"A": "q2", "B": "k2"},
            3: {"A": "q3", "B": "k3", "D": "y0", "E": "y1"},
            4: {"A": "y2", "B": "out", "D": "back0"},
            5: {"C": "back1"},
            6: {"A": "q0", "B": "k0"},
            7: {"C": "back2"}}
    PIECES = {0: {"A": ["stats"], "C": ["xn"]},
              1: {"A": ["take_v"], "B": ["beats0"], "C": ["beats1"], "D": ["beats2", "weights3"], "E": ["products3"]},
              2: {"A": ["beats3"], "B": ["count1", "count2"], "C": ["count3", "count4"], "D": ["pick"]},
              3: {"A": ["first_sum3"], "B": ["second_sum3"]},
              4: {"B": ["out"], "C": ["weights0"], "D": ["products0"]},
              5: {"A": ["second_sum0"], "B": ["weights1"], "C": ["products1"], "D": ["first_sum1"]},
              6: {"A": ["second_sum1"]},
              7: {"B": ["weights2"], "C": ["products2"], "D": ["first_sum2"], "E": ["second_sum2"]}}
    QUARTERS = "ABCD"
    POOL_TILES, DVE_TILES = (0, 1), (2, 3)
    FEWER = T - len(POOL_TILES)
    OF_BEFORE = {"back3", "y0", "y1", "y2", "out", "weights3", "products3", "first_sum3", "second_sum3"}
    OF_NEXT = {"xnT", "v0", "v1", "v2", "v3", "q0", "k0", "stats", "xn", "beats0", "beats1", "beats2", "beats3",
               "count1", "count2", "count3", "count4"}
    PROLOGUE = ["xnT", "v0", "v1", "v2", "v3", "q0", "k0"]
    EPILOGUE = ["back3", "y0", "y1", "y2", "out"]

    def skipped(name, kind):
        if name == "stats" and kind == "first":
            return True
        return name in {"first": OF_BEFORE, "middle": (), "last": OF_NEXT}[kind]

    def batch_of(name, b):
        return b - 1 if name in OF_BEFORE else b + 1 if name in OF_NEXT else b

    ORDER = [USES[h][at] for h in range(H) for at in "ABCDE" if at in USES[h]]

    def count(kind):
        return sum(not skipped(name, kind) for name in ORDER)

    def use_at(h, at, kind, b):
        name = USES[h].get(at)
        if name is None or skipped(name, kind):
            return None, None
        return name, number(name, kind, b)

    def number(name, kind, b):
        before = ORDER[:ORDER.index(name)]
        return misc_base(kind, b) + sum(not skipped(other, kind) for other in before)

    M0, M1, M2 = len(PROLOGUE), count("first"), count("middle")

    def misc_base(kind, b):
        return M0 if kind == "first" else b * M2 + (M0 + M1 - M2)

    with ExitStack() as ctx:
        def sb(name, shape):
            return ctx.enter_context(nc.sbuf_tensor("b_" + name, shape, F32))

        def sem(name):
            return ctx.enter_context(nc.semaphore("b_" + name))

        wq, wk = sb("wq", [P, H * DH]), sb("wk", [P, H * DH])
        wvg = sb("wvg", [P, VC + 2 * GC])
        wo = sb("wo", [P, CH, C])
        half = sb("half", [P, 2])
        stats, mv = sb("stats", [P, T, 6]), sb("mv", [P, T, 2])
        var_eps, rstd = sb("var_eps", [P, T]), sb("rstd", [P, T])
        xn, xnT_next, xnT = sb("xn", [P, T, C]), sb("xnT_next", [P, S]), sb("xnT", [P, S])
        xvg = sb("xvg", [P, T, VC + 2 * GC])
        esig, sig = sb("esig", [P, T, GC]), sb("sig", [P, T, GC])
        later, beaten = sb("later", [P, E]), sb("beaten", [P, T, 2 * H, E])
        wins = sb("wins", [P, E - 1, T, 2 * H, E])
        picked = sb("picked", [P, T, 2 * H, E])
        wv, mo = sb("wv", [P, T, GC]), sb("mo", [P, T, H, E])
        vprod, vsum = sb("vprod", [P, H, E, DH]), sb("vsum", [P, 2, H, DH])
        v_next, v = sb("v_next", [P, T, H, DH]), sb("v", [P, T, H, DH])
        q, kz = sb("q", [P, 2, S]), sb("kz", [P, 2, 2, S])
        nmax, den = sb("nmax", [P, 2, T]), sb("den", [P, H, T])
        prob, probT = sb("prob", [P, 2, T, S]), sb("probT", [P, 4, T, S])
        attT = sb("attT", [P, S])
        rden, w = sb("rden", [P, 2, T]), sb("w", [P, 2, T, E])
        yprod, y = sb("yprod", [P, 2, T, VC]), sb("y", [P, T, CH * P])
        yT = sb("yT", [P, CH, S])

        w_loaded = sem("w_loaded")
        consts_ready, pool_consts, pool_steps, dve_steps = (
            sem("consts_ready"), sem("pool_consts"), sem("pool_steps"), sem("dve_steps"))
        ln_var, ln_rstd, ln_done = sem("ln_var"), sem("ln_rstd"), sem("ln_done")
        in_misc, misc_taken = sem("in_misc"), sem("misc_taken")
        xnT_moved = sem("xnT_moved")
        esig_ready, gates_ready, v_next_ready, v_ready = (
            sem("esig_ready"), sem("gates_ready"), sem("v_next_ready"), sem("v_ready"))
        first_v_ready = sem("first_v_ready")
        in_scores, max_ready, exp_done = sem("in_scores"), sem("max_ready"), sem("exp_done")
        in_turned, turned_taken = sem("in_turned"), sem("turned_taken")
        in_att, attT_ready, y_ready = sem("in_att"), sem("attT_ready"), sem("y_ready")
        N_LOADS = 7

        block = ctx.enter_context(nc.Block())
        misc = PS[:, MISC, :]

        @block.sync
        def _(sp):
            sp.dma_start(wq[:, :], Wq).then_inc(w_loaded, 16)
            sp.dma_start(wk[:, :], Wk).then_inc(w_loaded, 16)
            sp.dma_start(wvg[:, 0:VC].rearrange("p (e k) -> p e k", e=E),
                         Wv.rearrange("e c k -> c e k")).then_inc(w_loaded, 16)
            sp.dma_start(wvg[:, VC:VC + GC], Ws).then_inc(w_loaded, 16)
            sp.dma_start(wvg[:, VC + GC:VC + 2 * GC], Wd).then_inc(w_loaded, 16)
            rows = Wo.rearrange("e k d -> (e k) d")
            sp.dma_start(wo[:, 0:2, :], rows[0:2 * P].rearrange("(a p) d -> p a d", p=P)).then_inc(w_loaded, 16)
            sp.wait_ge(pool_consts, 1)
            sp.dma_start(wo[0:VC - 2 * P, 2, :], rows[2 * P:VC]).then_inc(w_loaded, 16)

        @block.gpsimd
        def _(pool):
            nc.gpsimd.memset(wo[:, 2, :], 0.0).then_inc(pool_consts, 1)
            nc.gpsimd.memset(half[:, :], -0.5).then_inc(pool_consts, 1)
            nc.gpsimd.memset(kz[:, :, :, :], 0.0).then_inc(consts_ready, 1)
            nc.gpsimd.memset(y[:, :, :], 0.0).then_inc(consts_ready, 1)
            for j in range(E):
                nc.gpsimd.memset(later[:, j:j + 1], float(E - 1 - j)).then_inc(consts_ready, 1)
            pool.wait_ge(pool_consts, 2)

            def rstd_of(b):
                pool.wait_ge(ln_var, b + 1)
                if not (isinstance(b, int) and b == 0):
                    pool.wait_ge(ln_done, b)
                nc.gpsimd.tensor_tensor(rstd[:, :], var_eps[:, :], half[:, 0:1].to_broadcast([P, T]),
                                        ALU.pow).then_inc(ln_rstd, 1)

            def values(own, b, tiles):
                for i in tiles:
                    own.only(nc.gpsimd.tensor_tensor(
                        vprod[:, :, :, :],
                        xvg[:, i, 0:VC].rearrange("p (a e k) -> p a e k", a=1, e=E).to_broadcast([P, H, E, DH]),
                        wv[:, i, :].rearrange("p (h e a) -> p h e a", h=H, a=1).to_broadcast([P, H, E, DH]),
                        ALU.mult))
                    own.ran(nc.gpsimd.tensor_tensor(vsum[:, 0], vprod[:, :, 0, :], vprod[:, :, 1, :], ALU.add))
                    own.ran(nc.gpsimd.tensor_tensor(vsum[:, 1], vprod[:, :, 2, :], vprod[:, :, 3, :], ALU.add))
                    own.sync()
                    own.only(nc.gpsimd.tensor_tensor(vsum[:, 0], vsum[:, 0], vsum[:, 1], ALU.add))
                    nc.gpsimd.tensor_tensor(v_next[:, i], vsum[:, 0], vprod[:, :, 4, :], ALU.add).then_inc(v_next_ready, 1)
                    pool.wait_ge(v_next_ready, i + 1 if isinstance(b, int) and b == 0 else b * T - FEWER + i + 1)

            rstd_of(0)
            rstd_of(1)
            own = Chain(pool, pool_steps, 0)
            pool.wait_ge(gates_ready, 1)
            values(own, 0, POOL_TILES)
            n_start = own.n
            with pool.Fori(0, B - 2) as b:
                own = Chain(pool, pool_steps, b * (4 * T) + n_start)
                pool.wait_ge(gates_ready, b + 2)
                values(own, b + 1, range(T))
                rstd_of(b + 2)
            own = Chain(pool, pool_steps, (B - 2) * (4 * T) + n_start)
            pool.wait_ge(gates_ready, B)
            values(own, B - 1, range(T))

        @block.scalar
        def _(act):
            def take(k):
                act.wait_ge(in_misc, k + 1)

            def head_exp(b, h, i):
                act.wait_ge(max_ready, (b * H + h) * T + i + 1)
                if i == 0:
                    if not (isinstance(b, int) and b == 0 and h < 2):
                        act.wait_ge(in_turned, (b * H + h - 1) * T)
                nc.scalar.activation(prob[:, h % 2, i, :], PS[:, i, :], ACT.Exp, bias=nmax[:, h % 2, i:i + 1],
                                     accum_out=den[:, h, i:i + 1]).then_inc(exp_done, 1)

            def head_turned(b, h, j):
                act.wait_ge(in_turned, (b * H + h) * T + j + 1)
                if j == 0 and not (isinstance(b, int) and b == 0 and h < 4):
                    act.wait_ge(in_att, b * PAIRS + h // 2 - 1)
                nc.scalar.activation(probT[:, h % 4, j, :], PS[:, 4 + j % 2, :], ACT.Copy).then_inc(turned_taken, 1)

            def pair_att(b, pr):
                act.wait_ge(in_att, b * PAIRS + pr + 1)
                nc.scalar.activation(attT[:, :], PS[:, 6, :], ACT.Copy).then_inc(attT_ready, 1)

            def run_use(name, b, k):
                if name == "xnT":
                    take(k)
                    nc.scalar.activation(xnT_next[:, :], misc, ACT.Copy).then_inc(misc_taken, 1)
                elif name[0] == "v":
                    i = int(name[1])
                    take(k)
                    if isinstance(b, int) and b == 1 and i in POOL_TILES:
                        act.wait_ge(v_next_ready, i + 1)
                    elif isinstance(b, int) and b == 1:
                        act.wait_ge(first_v_ready, i - DVE_TILES[0] + 1)
                    nc.scalar.activation(xvg[:, i, :], misc[:, 0:VC + 2 * GC], ACT.Copy).then_inc(misc_taken, 1)
                    if i == T - 1:
                        act.wait_ge(misc_taken, k + 1)
                        nc.scalar.activation(esig[:, :, :], xvg[:, :, VC:VC + GC], ACT.Exp,
                                             scale=-1.0).then_inc(esig_ready, 1)
                elif name[0] == "q":
                    pr = int(name[1])
                    take(k)
                    if not (isinstance(b, int) and b == 0 and pr < 2):
                        act.wait_ge(in_scores, (b * PAIRS + pr - 1) * 2 * T)
                    nc.scalar.activation(q[:, pr % 2, :], misc, ACT.Copy, scale=SCALE).then_inc(misc_taken, 1)
                elif name[0] == "k":
                    pr = int(name[1])
                    take(k)
                    nc.scalar.activation(kz[0:DH, pr % 2, 0, :], misc[0:DH], ACT.Copy)
                    nc.scalar.activation(kz[DH:P, pr % 2, 1, :], misc[DH:P], ACT.Copy).then_inc(misc_taken, 1)
                elif name[0] == "y":
                    take(k)
                    nc.scalar.activation(yT[:, int(name[1]), :], misc, ACT.Copy).then_inc(misc_taken, 1)

            act.wait_ge(consts_ready, 2 + E)

            def move_xnT(b):
                nc.scalar.activation(xnT[:, :], xnT_next[:, :], ACT.Copy).then_inc(xnT_moved, 1)

            def batch(b, kind):
                for h in range(H):
                    nb, nh = (b, h + 1) if h + 1 < H else (b + 1, 0)
                    for i, at in enumerate(QUARTERS):
                        head_turned(b, h, i)
                        name, k = use_at(h, at, kind, b)
                        if name:
                            run_use(name, batch_of(name, b), k)
                        if h + 1 < H or kind != "last":
                            head_exp(nb, nh, i)
                    if h == 0 and kind != "first":
                        pair_att(b - 1, PAIRS - 1)
                    if h % 2 == 0 and h:
                        pair_att(b, h // 2 - 1)
                    name, k = use_at(h, "E", kind, b)
                    if name:
                        run_use(name, batch_of(name, b), k)
                    if h == 4 and kind != "last":
                        move_xnT(b + 1)

            for k, name in enumerate(PROLOGUE):
                run_use(name, 0, k)
                if name == "xnT":
                    act.wait_ge(misc_taken, 1)
                    move_xnT(0)
            for i in range(T):
                head_exp(0, 0, i)
            batch(0, "first")
            with act.Fori(1, B - 1) as b:
                batch(b, "middle")
            batch(B - 1, "last")
            pair_att(B - 1, PAIRS - 1)
            for n, name in enumerate(EPILOGUE):
                run_use(name, B - 1, misc_base("last", B - 1) + count("last") + n)

        @block.tensor
        def _(pe):
            def scores(b, h, i, k_use=None):
                if not (isinstance(b, int) and b == 0 and h == 0):
                    pe.wait_ge(exp_done, (b * H + h - 1) * T + i + 1)
                if i == 0 and h % 2 == 0:
                    pe.wait_ge(misc_taken, k_use + 1)
                pr = h // 2
                nc.tensor.matmul(PS[:, i, :], q[:, pr % 2, i * P:(i + 1) * P], kz[:, pr % 2, h % 2, :],
                                 start=True, stop=True).then_inc(in_scores, 1)

            def turn(b, h, j):
                if j == 0:
                    pe.wait_ge(exp_done, (b * H + h) * T + T)
                if not (isinstance(b, int) and b == 0 and h == 0 and j < 2):
                    pe.wait_ge(turned_taken, (b * H + h) * T + j - 1)
                for i in range(T):
                    last = nc.tensor.transpose(PS[:, 4 + j % 2, i * P:(i + 1) * P],
                                               prob[:, h % 2, i, j * P:(j + 1) * P], ident[:, :])
                last.then_inc(in_turned, 1)

            def half_product(b, pr, js):
                if pr == 0 and 0 in js:
                    pe.wait_ge(v_ready, b + 1)
                if 0 in js and not (isinstance(b, int) and b == 0 and pr == 0):
                    pe.wait_ge(attT_ready, b * PAIRS + pr)
                pe.wait_ge(turned_taken, (b * H + 2 * pr + 1) * T + js[-1] + 1)
                for j in js:
                    for hh in range(2):
                        h = 2 * pr + hh
                        last = nc.tensor.matmul(PS[hh * DH:(hh + 1) * DH, 6, :], v[:, j, h, :], probT[:, h % 4, j, :],
                                                start=(j == 0), stop=(j == T - 1), skip_group_check=True)
                if T - 1 in js:
                    last.then_inc(in_att, 1)

            def run_use(name, b, k):
                if not (isinstance(k, int) and k == 0):
                    pe.wait_ge(misc_taken, k)
                if name == "xnT":
                    pe.wait_ge(ln_done, b + 1)
                    for i in range(T):
                        last = nc.tensor.transpose(misc[:, i * P:(i + 1) * P], xn[:, i, :], ident[:, :])
                elif name[0] == "v":
                    i = int(name[1])
                    last = nc.tensor.matmul(misc[:, 0:VC + 2 * GC], xnT_next[:, i * P:(i + 1) * P], wvg[:, :],
                                            start=True, stop=True)
                elif name[0] in "qk":
                    pr = int(name[1])
                    pe.wait_ge(xnT_moved, b + 1)
                    wt = wq if name[0] == "q" else wk
                    last = nc.tensor.matmul(misc, wt[:, pr * P:(pr + 1) * P], xnT[:, :], start=True, stop=True)
                elif name[:4] == "back":
                    pe.wait_ge(attT_ready, b * PAIRS + int(name[4]) + 1)
                    for i in range(T):
                        last = nc.tensor.transpose(misc[:, i * P:(i + 1) * P], attT[:, i * P:(i + 1) * P], ident[:, :])
                elif name[0] == "y":
                    c = int(name[1])
                    if c == 0:
                        pe.wait_ge(y_ready, b + 1)
                    for i in range(T):
                        last = nc.tensor.transpose(misc[:, i * P:(i + 1) * P], y[:, i, c * P:(c + 1) * P], ident[:, :])
                elif name == "out":
                    for i in range(T):
                        for c in range(CH):
                            last = nc.tensor.matmul(misc[:, i * P:(i + 1) * P], yT[:, c, i * P:(i + 1) * P], wo[:, c, :],
                                                    start=(c == 0), stop=(c == CH - 1))
                last.then_inc(in_misc, 1)

            def batch(b, kind):
                k_use = None
                for h in range(H):
                    nb, nh = (b, h + 1) if h + 1 < H else (b + 1, 0)
                    for i, at in enumerate(QUARTERS):
                        if h + 1 < H or kind != "last":
                            scores(nb, nh, i, k_use)
                        turn(b, h, i)
                        name, k = use_at(h, at, kind, b)
                        if name:
                            run_use(name, batch_of(name, b), k)
                            if name[0] == "k":
                                k_use = k
                    if h % 2:
                        half_product(b, h // 2, (0, 1))
                    elif h:
                        half_product(b, h // 2 - 1, (2, 3))
                    elif kind != "first":
                        half_product(b - 1, PAIRS - 1, (2, 3))
                    name, k = use_at(h, "E", kind, b)
                    if name:
                        run_use(name, batch_of(name, b), k)

            pe.wait_ge(w_loaded, 16 * N_LOADS)
            for k, name in enumerate(PROLOGUE):
                run_use(name, 0, k)
            for i in range(T):
                scores(0, 0, i, len(PROLOGUE) - 1)
            batch(0, "first")
            with pe.Fori(1, B - 1) as b:
                batch(b, "middle")
            batch(B - 1, "last")
            half_product(B - 1, PAIRS - 1, (2, 3))
            for n, name in enumerate(EPILOGUE):
                run_use(name, B - 1, misc_base("last", B - 1) + count("last") + n)

        @block.vector
        def _(dve):
            def head_max(b, h, i):
                dve.wait_ge(in_scores, (b * H + h) * T + i + 1)
                nc.vector.tensor_reduce(nmax[:, h % 2, i:i + 1], PS[:, i, :], AX.X, ALU.max,
                                        negate=True).then_inc(max_ready, 1)

            def beats(own, i, taken):
                dve.wait_ge(misc_taken, taken)
                logit = xvg[:, i, VC:VC + 2 * GC].rearrange("p (h e) -> p h e", e=E)
                for d in range(1, E):
                    own.ran(nc.vector.tensor_tensor(wins[:, d - 1, i, :, 0:E - d], logit[:, :, 0:E - d],
                                                    logit[:, :, d:E], ALU.is_ge))
                if i == T - 1:
                    own.ran(nc.vector.tensor_copy(
                        beaten[:, :, :, :].rearrange("p i h e -> p (i h) e"),
                        later[:, :].rearrange("p (a e) -> p a e", a=1).to_broadcast([P, T * 2 * H, E])))

            def count_beaten(own, d):
                if d == 1:
                    own.sync()
                flat = beaten[:, :, :, :].rearrange("p i h e -> p (i h) e")
                won = wins[:, d - 1].rearrange("p i h e -> p (i h) e")[:, :, 0:E - d]
                own.only(nc.vector.tensor_tensor(flat[:, :, d:E], flat[:, :, d:E], won, ALU.add))
                own.only(nc.vector.tensor_tensor(flat[:, :, 0:E - d], flat[:, :, 0:E - d], won, ALU.subtract))

            def keep_mo(own):
                own.only(nc.vector.tensor_copy(mo[:, :, :, :], picked[:, :, H:2 * H, :]))

            def pick(own, b):
                own.ran(nc.vector.tensor_scalar(picked[:, :, :, :], beaten[:, :, :, :], 2.0, None, ALU.is_lt))
                dve.wait_ge(esig_ready, b + 1)
                own.only(nc.vector.tensor_scalar(sig[:, :, :], esig[:, :, :], 1.0, None, ALU.add))
                own.only(nc.vector.reciprocal(sig[:, :, :], sig[:, :, :]))
                nc.vector.tensor_tensor(wv[:, :, :].rearrange("p i (h e) -> p i h e", e=E), picked[:, :, 0:H, :],
                                        sig[:, :, :].rearrange("p i (h e) -> p i h e", e=E),
                                        ALU.mult).then_inc(gates_ready, 1)

            def take_v(b):
                if not (isinstance(b, int) and b == 0):
                    dve.wait_ge(in_att, b * PAIRS)
                dve.wait_ge(v_next_ready, b * T + T - FEWER)
                if isinstance(b, int) and b == 0:
                    dve.wait_ge(first_v_ready, len(DVE_TILES))
                nc.vector.tensor_copy(v[:, :, :, :], v_next[:, :, :, :]).then_inc(v_ready, 1)

            def weights(own, b, pr):
                h0 = 2 * pr
                dve.wait_ge(exp_done, (b * H + h0 + 2) * T)
                own.only(nc.vector.reciprocal(rden[:, :, :], den[:, h0:h0 + 2, :]))
                for hh in range(2):
                    own.ran(nc.vector.tensor_tensor(
                        w[:, hh], mo[:, :, h0 + hh, :],
                        rden[:, hh, :].rearrange("p (i a) -> p i a", a=1).to_broadcast([P, T, E]), ALU.mult))

            def products(own, pr, k):
                own.sync()
                dve.wait_ge(in_misc, k + 1)
                att = misc.rearrange("p (i a h k) -> p i a h k", i=T, a=1, h=2)
                for hh in range(2):
                    dst = y[:, :, 0:VC] if pr == 0 and hh == 0 else yprod[:, hh]
                    ins = nc.vector.tensor_tensor(
                        dst.rearrange("p i (e k) -> p i e k", e=E),
                        att[:, :, :, hh, :].to_broadcast([P, T, E, DH]),
                        w[:, hh].rearrange("p i (e a) -> p i e a", a=1).to_broadcast([P, T, E, DH]), ALU.mult)
                    if hh == 0:
                        own.ran(ins)
                    else:
                        ins.then_inc(misc_taken, 1)

            def first_sum(own):
                own.sync()
                own.only(nc.vector.tensor_tensor(y[:, :, 0:VC], y[:, :, 0:VC], yprod[:, 0], ALU.add))

            def second_sum(own, pr, k):
                own.sync()
                dve.wait_ge(misc_taken, k + 1)
                ins = nc.vector.tensor_tensor(y[:, :, 0:VC], y[:, :, 0:VC], yprod[:, 1], ALU.add)
                if pr == PAIRS - 1:
                    ins.then_inc(y_ready, 1)
                else:
                    own.only(ins)

            def add_out(own, b, k):
                dve.wait_ge(in_misc, k + 1)
                nc.vector.tensor_tensor(X[:, b, :, :], misc.rearrange("p (i n) -> p i n", i=T), X[:, b, :, :],
                                        ALU.add).then_inc(misc_taken, 1)

            def front_stats(own, b):
                layernorm_stats(nc, own, X[:, b], stats, mv, var_eps).then_inc(ln_var, 1)

            def front_xn(own, b):
                dve.wait_ge(ln_rstd, b + 1)
                layernorm_apply(nc, X[:, b], xn, mv, rstd).then_inc(ln_done, 1)

            def first_values(own, i):
                prods = yprod[:, :, :, :].rearrange("p a i n -> p (a i n)").rearrange("p (h e k) -> p h e k", h=H, e=E)
                part = yT[:, 0:2, :].rearrange("p a (h k) -> p a h k", h=H)
                if i > DVE_TILES[0]:
                    dve.wait_ge(first_v_ready, i - DVE_TILES[0])
                own.only(nc.vector.tensor_tensor(
                    prods, xvg[:, i, 0:VC].rearrange("p (a e k) -> p a e k", a=1, e=E).to_broadcast([P, H, E, DH]),
                    wv[:, i, :].rearrange("p (h e a) -> p h e a", h=H, a=1).to_broadcast([P, H, E, DH]), ALU.mult))
                own.ran(nc.vector.tensor_tensor(part[:, 0], prods[:, :, 0, :], prods[:, :, 1, :], ALU.add))
                own.ran(nc.vector.tensor_tensor(part[:, 1], prods[:, :, 2, :], prods[:, :, 3, :], ALU.add))
                own.sync()
                own.only(nc.vector.tensor_tensor(part[:, 0], part[:, 0], part[:, 1], ALU.add))
                nc.vector.tensor_tensor(v_next[:, i], part[:, 0], prods[:, :, 4, :], ALU.add).then_inc(first_v_ready, 1)

            def piece(own, name, b, kind):
                what, n = name.rstrip("01234"), int(name[-1]) if name[-1].isdigit() else None
                at = batch_of(name, b)
                if name == "stats":
                    front_stats(own, at)
                elif name == "xn":
                    front_xn(own, at)
                elif name == "take_v":
                    take_v(at)
                elif name == "out":
                    add_out(own, at, number("out", kind, b))
                elif name == "pick":
                    keep_mo(own)
                    if kind != "last":
                        pick(own, b + 1)
                elif what == "beats":
                    beats(own, n, number("v%d" % n, kind, b) + 1)
                elif what == "count":
                    count_beaten(own, n)
                elif what == "weights":
                    weights(own, at, n)
                elif what == "products":
                    products(own, n, number("back%d" % n, kind, b))
                elif what == "first_sum":
                    first_sum(own)
                elif what == "second_sum":
                    second_sum(own, n, number("back%d" % n, kind, b))

            def batch(b, kind, base):
                own = Chain(dve, dve_steps, base)
                for h in range(H):
                    nb, nh = (b, h + 1) if h + 1 < H else (b + 1, 0)
                    for i, at in enumerate("ABCDE"):
                        if at != "E" and (h + 1 < H or kind != "last"):
                            head_max(nb, nh, i)
                        if kind == "first" and (h, at) in ((0, "B"), (1, "A")):
                            first_values(own, DVE_TILES[h])
                        for name in PIECES[h].get(at, []):
                            if not skipped(name, kind):
                                piece(own, name, b, kind)
                assert own.n == own_steps(kind), (kind, own.n, own_steps(kind))

            COUNTED = {"stats": LN_STEPS, "beats": E - 1, "count": 2, "pick": 1 + 3,
                       "weights": 3, "products": 1, "first_sum": 1, "second_sum": 1}

            def own_steps(kind):
                names = [name for h in PIECES for at in PIECES[h] for name in PIECES[h][at] if not skipped(name, kind)]
                n = sum(COUNTED.get(name.rstrip("01234"), 0) for name in names)
                n += "beats3" in names
                n -= "second_sum3" in names
                n += 4 * len(DVE_TILES) * (kind == "first")
                return n - (3 if kind == "last" else 0)

            dve.wait_ge(consts_ready, 2 + E)
            own = Chain(dve, dve_steps, 0)
            front_stats(own, 0)
            front_xn(own, 0)
            front_stats(own, 1)
            for i in range(T):
                beats(own, i, PROLOGUE.index("v%d" % i) + 1)
            for d in range(1, E):
                count_beaten(own, d)
            pick(own, 0)
            for i in range(T):
                head_max(0, 0, i)
            n_start = own.n
            batch(0, "first", n_start)
            n_start += own_steps("first")
            n = own_steps("middle")
            with dve.Fori(1, B - 1) as b:
                batch(b, "middle", b * n + (n_start - n))
            n_start += (B - 2) * n
            batch(B - 1, "last", n_start)
            own = Chain(dve, dve_steps, n_start + own_steps("last"))
            base = misc_base("last", B - 1) + count("last")
            weights(own, B - 1, PAIRS - 1)
            products(own, PAIRS - 1, base)
            first_sum(own)
            second_sum(own, PAIRS - 1, base)
            add_out(own, B - 1, base + EPILOGUE.index("out"))


def phase_geometric_attention(nc, X, PS, ident, Wq, Wk, Wv, Wo, head_dirs, scale):
    H, D, HD = 16, 4, C // 16
    TERMS = ((0, 0), (0, 1), (0, 2), (1, 0), (1, 1), (2, 0))
    ROWS = len(TERMS) * D
    GR = 32
    NG = P // GR
    HALF = H // 2
    SL = NG
    VW = 32
    EX = T * (T + 1) // 2 * P
    NEG = -1e30
    S1A, S1B, S1C, S2A, OUTB, MISC = 0, 1, 2, 3, 6, 7
    BF16 = mybir.dt.bfloat16

    def plan(n):
        us = {h: [] for h in range(H)}

        def put(**slots):
            for name, h in slots.items():
                us[h].append(name)
        if 0 <= n < B:
            put(c1=0, back0=10, back1=14)
        if 1 <= n <= B:
            put(back2=1, back3=5, turn=6, out=7)
        if n + 1 < B:
            put(c0=9)
        if n + 2 < B:
            put(xnT=2, proj=3, v0=11, v1=12, v2=13, v3=15)
        return us

    START = ["xnT", "proj", "v0", "v1", "v2", "v3"]

    def n_uses(n):
        return sum(len(u) for u in plan(n).values())

    def place_of(k, name):
        return [u for us in plan(k).values() for u in us].index(name)

    def misc_base(n, k):
        if isinstance(n, int):
            return len(START) + sum(n_uses(m) for m in range(-1, n))
        return (n - 1) * n_uses(1) + misc_base(1, 1)

    with ExitStack() as ctx:
        def sb(name, shape, dt=F32):
            return ctx.enter_context(nc.sbuf_tensor("c_" + name, shape, dt))

        def sem(name):
            return ctx.enter_context(nc.semaphore("c_" + name))

        stack = nc.dram_tensor("c_stack", [B, 2, H, ROWS, S], BF16).ap()
        shifts = nc.dram_tensor("c_shifts", [B, 2, 3, HALF, S], BF16).ap()

        wq3, wk3 = sb("wq3", [P, H, 3]), sb("wk3", [P, H, 3])
        dirs, scale_sb = sb("dirs", [P, H, 3]), sb("scale", [P, 1])
        wdir = sb("wdir", [P, 2, H, 3])
        w4 = sb("w4", [P, 2, H, D])
        wv, wo = sb("wv", [P, C]), sb("wo", [P, C])
        half = sb("half", [P, 2])
        ident_bf = sb("ident_bf", [P, P], BF16)
        mask_ts = sb("mask_ts", [P, P], BF16)
        stats, mv = sb("stats", [P, T, 6]), sb("mv", [P, T, 2])
        var_eps, rstd = sb("var_eps", [P, T]), sb("rstd", [P, T])
        xn, xnT = sb("xn", [P, T, C]), sb("xnT", [P, S])
        parts, rest = sb("parts", [P, 3, S], BF16), sb("rest", [P, S])
        qx, k1, k2 = sb("qx", [P, 2, H, S], BF16), sb("k1", [P, 2, SL, S], BF16), sb("k2", [P, 2, SL, S], BF16)
        v_next, v = sb("v_next", [P, T, H, HD]), sb("v", [P, 2, T, H, VW])
        nmax = sb("nmax", [P, 2, T, HALF])
        cparts, crest = sb("cparts", [P, 3, S], BF16), sb("crest", [P, S])
        ex = sb("ex", [P, HALF, EX])
        oT = sb("oT", [P, S])
        rz = sb("rz", [P, T, NG])
        att, attT = sb("att", [P, T, C]), sb("attT", [P, S])

        w_loaded, w4_ready, consts_ready = sem("w_loaded"), sem("w4_ready"), sem("consts_ready")
        pool_consts, dve_steps = sem("pool_consts"), sem("dve_steps")
        ln_var, ln_rstd, ln_done = sem("ln_var"), sem("ln_rstd"), sem("ln_done")
        in_misc, misc_taken = sem("in_misc"), sem("misc_taken")
        part1_ready, part2_ready, part3_ready = sem("part1_ready"), sem("part2_ready"), sem("part3_ready")
        odd_q_zeroed, keys_filled = sem("odd_q_zeroed"), sem("keys_filled")
        stack_written, stack_passed = sem("stack_written"), sem("stack_passed")
        pool_passed = sem("pool_passed")
        k1_loaded = sem("k1_loaded")
        qk_loaded = [sem("qk_loaded0"), sem("qk_loaded1")]
        c_part1, c_part2, c_part3 = sem("c_part1"), sem("c_part2"), sem("c_part3")
        c_written, c_loaded = sem("c_written"), [sem("c_loaded0"), sem("c_loaded1")]
        v_ready = sem("v_ready")
        in_first, max_done = sem("in_first"), sem("max_done")
        in_second, exp_done, masked = sem("in_second"), sem("exp_done"), sem("masked")
        in_out, oT_ready = sem("in_out"), sem("oT_ready")
        N_LOADS = 6

        block = ctx.enter_context(nc.Block())
        misc = PS[:, MISC, :]

        def steps_of(emit, j_loop):
            emit(-1, -1)
            emit(0, 0)
            with j_loop(0, (B - 4) // 2) as j:
                emit(j * 2 + 1, 1)
                emit(j * 2 + 2, 2)
            for n in range(B - 3, B + 1):
                emit(n, n)

        def batch_of(name, n):
            if name in ("xnT", "proj", "v0", "v1", "v2", "v3"):
                return n + 2
            if name == "c0":
                return n + 1
            if name in ("back2", "back3", "turn", "out"):
                return n - 1
            return n

        @block.sync
        def _(sp):
            def write_stack(b):
                sp.wait_ge(part2_ready, b + 1)
                sp.wait_ge(part3_ready, b + 1)
                for qk in range(2):
                    for t, term in enumerate(TERMS):
                        sp.dma_start(stack[b, qk, :, t * D:(t + 1) * D, :],
                                     parts[qk * H * D:(qk + 1) * H * D, term[qk], :]).then_inc(stack_written, 16)
                sp.wait_ge(stack_written, b * (2 * len(TERMS) * 16) + 2 * len(TERMS) * 16).then_inc(stack_passed, 1)

            def load_k1(b, par):
                if not (isinstance(b, int) and b < 2):
                    sp.wait_ge(in_first, (b - 1) * (3 * H))
                for g in range(NG):
                    sp.dma_start(k1[g * GR:g * GR + ROWS, par, :, :],
                                 stack[b, 1, g:H:NG].rearrange("s r n -> r s n")).then_inc(k1_loaded, 16)

            def load_qk(b, par, hf):
                if not (isinstance(b, int) and b < 2):
                    sp.wait_ge(in_second, (b - 2) * (2 * H) + (hf + 1) * H)
                s0, s1 = hf * SL // 2, (hf + 1) * SL // 2
                for g in range(NG):
                    rows = slice(g * GR, g * GR + ROWS)
                    sp.dma_start(qx[rows, par, s0 * NG + g:s1 * NG:NG, :],
                                 stack[b, 0, s0 * NG + g:s1 * NG:NG].rearrange("s r n -> r s n")).then_inc(qk_loaded[hf], 16)
                    sp.dma_start(k2[rows, par, s0:s1, :],
                                 stack[b, 1, s0 * NG + g:s1 * NG:NG].rearrange("s r n -> r s n")).then_inc(qk_loaded[hf], 16)

            def move_c(b, par, hf):
                sp.wait_ge(c_part2, b * 2 + hf + 1)
                sp.wait_ge(c_part3, b * 2 + hf + 1)
                sp.dma_start(shifts[b, hf].rearrange("a h n -> h a n"), cparts[0:HALF, :, :]).then_inc(c_written, 16)
                sp.wait_ge(c_written, b * 32 + (hf + 1) * 16)
                for g in range(NG):
                    sp.dma_start(qx[g * GR + ROWS:g * GR + ROWS + 3, par, hf * HALF + g:(hf + 1) * HALF:NG, :],
                                 shifts[b, hf, :, g:HALF:NG, :]).then_inc(c_loaded[hf], 16)

            for dst, src in ((wq3[:, :, :], Wq.rearrange("c (h d) -> c h d", d=3)),
                             (wk3[:, :, :], Wk.rearrange("c (h d) -> c h d", d=3)),
                             (wv[:, :], Wv), (wo[:, :], Wo),
                             (dirs[:, :, :].rearrange("p h d -> p (h d)"),
                              bcast_rows(head_dirs.rearrange("h d -> (h d)"), H * 3)),
                             (scale_sb[:, :], bcast_rows(scale, 1))):
                sp.dma_start(dst, src).then_inc(w_loaded, 16)
            write_stack(0)
            sp.wait_ge(consts_ready, 5)
            sp.wait_ge(keys_filled, 2)
            load_k1(0, 0)
            load_qk(0, 0, 0)
            load_qk(0, 0, 1)
            sp.wait_ge(odd_q_zeroed, 1)

            def step(n, k):
                if 0 <= k < B:
                    move_c(n, k % 2, 1)
                if k + 2 < B:
                    write_stack(n + 2)
                    load_k1(n + 2, k % 2)
                    load_qk(n + 2, k % 2, 0)
                if k + 1 < B:
                    move_c(n + 1, (k + 1) % 2, 0)
                if k + 2 < B:
                    load_qk(n + 2, k % 2, 1)

            steps_of(step, sp.Fori)

        @block.gpsimd
        def _(pool):
            own = Chain(pool, pool_consts, 0)
            own.ran(nc.gpsimd.memset(ident_bf[:, :], 0.0))
            own.ran(nc.gpsimd.memset(mask_ts[:, :], 0.0))
            nc.gpsimd.memset(half[:, :], -0.5).then_inc(consts_ready, 1)
            nc.gpsimd.memset(v[:, :, :, :, :], 0.0).then_inc(pool_consts, 1)
            own.n += 1
            own.sync()
            nc.gpsimd.memset(v[:, :, :, :, HD:HD + 1], 1.0).then_inc(consts_ready, 1)
            nc.gpsimd.affine_select(out=ident_bf[:, :], in_=ident_bf[:, :], compare_op=ALU.not_equal, fill=1.0,
                                    base=0, pattern=[[-1, P]], channel_multiplier=1).then_inc(consts_ready, 1)
            nc.gpsimd.affine_select(out=mask_ts[:, :], in_=mask_ts[:, :], compare_op=ALU.is_ge, fill=NEG,
                                    base=0, pattern=[[-1, P]], channel_multiplier=1).then_inc(consts_ready, 1)

            def ln(b):
                pool.wait_ge(ln_var, b + 1)
                nc.gpsimd.tensor_tensor(rstd[:, :], var_eps[:, :], half[:, 0:1].to_broadcast([P, T]),
                                        ALU.pow).then_inc(ln_rstd, 1)

            def place_v(b, par, v_uses):
                pool.wait_ge(misc_taken, v_uses).then_inc(pool_passed, 1)
                if not (isinstance(b, int) and b < 2):
                    pool.wait_ge(in_out, (b - 1) * NG).then_inc(pool_passed, 1)
                nc.gpsimd.tensor_copy(v[:, par, :, :, 0:HD], v_next[:, :, :, :]).then_inc(v_ready, 1)

            def causal(b, h):
                pool.wait_ge(exp_done, (b * H + h) * 2 + 2).then_inc(pool_passed, 1)
                blocks = ex[:, h % HALF, :].rearrange("p (a n) -> p a n", n=P)
                first_three, last = blocks[:, 0:2 * T + 1:T, :], blocks[:, 2 * T - 1, :]
                nc.gpsimd.affine_select(out=first_three, in_=first_three, compare_op=ALU.is_ge, fill=0.0,
                                        base=0, pattern=[[0, T - 1], [1, P]], channel_multiplier=-1)
                nc.gpsimd.affine_select(out=last, in_=last, compare_op=ALU.is_ge, fill=0.0,
                                        base=0, pattern=[[1, P]], channel_multiplier=-1).then_inc(masked, 1)

            def second_part(b, hf, n, k):
                pool.wait_ge(misc_taken, misc_base(n, k) + place_of(k, "c%d" % hf) + 1).then_inc(pool_passed, 1)
                nc.gpsimd.tensor_copy(cparts[0:HALF, 1, :], crest[0:HALF, :]).then_inc(c_part2, 1)

            def third_part(b, hf):
                pool.wait_ge(c_part2, b * 2 + hf + 1)
                nc.gpsimd.tensor_tensor(cparts[0:HALF, 2, :], crest[0:HALF, :], cparts[0:HALF, 1, :],
                                        ALU.subtract).then_inc(c_part3, 1)

            ln(0)
            nc.gpsimd.memset(k1[:, :, :, :], 0.0).then_inc(keys_filled, 1)
            nc.gpsimd.memset(k2[:, :, :, :], 1.0).then_inc(keys_filled, 1)
            place_v(0, 0, len(START))

            def step(n, k):
                if k + 2 < B:
                    ln(n + 2)
                for h in range(H):
                    if 0 <= k < B:
                        causal(n, h)
                    if h == 1 and 0 <= k < B:
                        second_part(n, 1, n, k)
                    if h == 2 and 0 <= k < B:
                        third_part(n, 1)
                    if h == 4 and 0 <= k and k + 1 < B:
                        place_v(n + 1, (k + 1) % 2, misc_base(n, k))
                    if h == 9 and k + 1 < B:
                        second_part(n + 1, 0, n, k)
                    if h == 10 and k + 1 < B:
                        third_part(n + 1, 0)

            steps_of(step, pool.Fori)

        @block.scalar
        def _(act):
            def exps(b, h):
                if h % NG == 0 and not (isinstance(b, int) and b == 0 and h < HALF):
                    act.wait_ge(in_out, b * NG + h // NG - 1)
                e = h % HALF
                act.wait_ge(in_second, (b * H + h) * 2 + 1)
                nc.scalar.activation(ex[:, e, 0:BANK], PS[:, S2A, :], ACT.Exp).then_inc(exp_done, 1)
                act.wait_ge(in_second, (b * H + h) * 2 + 2)
                nc.scalar.activation(ex[:, e, BANK:EX],
                                     PS[:, S2A + 1:S2A + 3, :].rearrange("p a n -> p (a n)")[:, 0:EX - BANK],
                                     ACT.Exp).then_inc(exp_done, 1)

            def take_out(b, gr):
                act.wait_ge(in_out, b * NG + gr + 1)
                nc.scalar.activation(oT[:, :], PS[:, OUTB, :], ACT.Copy).then_inc(oT_ready, 1)

            def run_use(name, b, k, par):
                if name == "xnT":
                    act.wait_ge(in_misc, k + 1)
                    nc.scalar.activation(xnT[:, :], misc, ACT.Copy).then_inc(misc_taken, 1)
                elif name == "proj":
                    act.wait_ge(in_misc, k + 1)
                    if not (isinstance(b, int) and b == 0):
                        act.wait_ge(stack_written, b * (2 * len(TERMS) * 16))
                    nc.scalar.activation(parts[:, 0, :], misc, ACT.Copy).then_inc(part1_ready, 1)
                elif name[0] == "v":
                    i = int(name[1])
                    act.wait_ge(in_misc, k + 1)
                    if i == 0 and not (isinstance(b, int) and b == 0):
                        act.wait_ge(v_ready, b)
                    nc.scalar.activation(v_next[:, i, :, :].rearrange("p h g -> p (h g)"), misc[:, 0:C],
                                         ACT.Copy).then_inc(misc_taken, 1)
                elif name == "turn":
                    act.wait_ge(in_misc, k + 1)
                    nc.scalar.activation(attT[:, :], misc, ACT.Copy).then_inc(misc_taken, 1)
                elif name in ("c0", "c1"):
                    hf = int(name[1])
                    act.wait_ge(in_misc, k + 1)
                    n = b * 2 + hf
                    if not (isinstance(b, int) and b == 0 and hf == 0):
                        act.wait_ge(c_written, n * 16)
                    nc.scalar.activation(cparts[0:HALF, 0, :], misc[0:HALF, :], ACT.Copy).then_inc(c_part1, 1)

            def second_part(k):
                act.wait_ge(misc_taken, k + 1)
                nc.scalar.activation(parts[:, 1, :], rest[:, :], ACT.Copy).then_inc(part2_ready, 1)

            act.wait_ge(consts_ready, 5)
            for k, name in enumerate(START):
                run_use(name, 0, k, 0)
                if name == "proj":
                    second_part(k)

            def step(n, k):
                m = misc_base(n, k)
                us = plan(k)
                for h in range(H):
                    if 0 <= k < B:
                        exps(n, h)
                    if h % NG == NG - 1:
                        if h >= NG and 0 <= k < B:
                            take_out(n, h // NG - 1)
                        elif h < NG and 1 <= k <= B:
                            take_out(n - 1, NG - 1)
                    if h == 4 and k + 2 < B:
                        second_part(misc_base(n, k) + place_of(k, "proj"))
                    for name in us[h]:
                        run_use(name, batch_of(name, n), m, 0)
                        m = m + 1

            steps_of(step, act.Fori)

        @block.tensor
        def _(pe):
            def first(b, h, par):
                if h == 0:
                    pe.wait_ge(k1_loaded, b * (NG * 16) + NG * 16)
                if h % HALF == 0:
                    pe.wait_ge(qk_loaded[h // HALF], b * (2 * NG * 16) + 2 * NG * 16)
                n4 = (b * H + h) * 4
                started = not (isinstance(b, int) and b == 0 and h == 0)
                q, kk = qx[:, par, h, :], k1[:, par, h // NG, :]

                def tile(bank, c0, i, start, stop):
                    nc.tensor.matmul(PS[:, bank, c0:c0 + (i + 1) * P], q[:, i * P:(i + 1) * P], kk[:, 0:(i + 1) * P],
                                     start=start, stop=False, skip_group_check=True)
                    return nc.tensor.matmul(PS[:, bank, c0 + i * P:c0 + (i + 1) * P], ident_bf[:, :], mask_ts[:, :],
                                            start=False, stop=stop, skip_group_check=True)
                if started:
                    pe.wait_ge(max_done, n4 - 3)
                tile(S1A, 0, 3, True, True).then_inc(in_first, 1)
                if started:
                    pe.wait_ge(max_done, n4 - 1)
                tile(S1B, 0, 2, True, False)
                tile(S1B, 3 * P, 0, False, True).then_inc(in_first, 1)
                if started:
                    pe.wait_ge(max_done, n4)
                tile(S1C, 0, 1, True, True).then_inc(in_first, 1)

            def second(b, h, par):
                if h % HALF == 0:
                    pe.wait_ge(c_loaded[h // HALF], b * (NG * 16) + NG * 16)
                n2 = (b * H + h) * 2
                started = not (isinstance(b, int) and b == 0 and h == 0)
                q, kk = qx[:, par, h, :], k2[:, par, h // NG, :]

                def tile(bank, c0, j, start, stop):
                    return nc.tensor.matmul(PS[:, bank, c0:c0 + S - j * P], kk[:, j * P:(j + 1) * P], q[:, j * P:S],
                                            start=start, stop=stop, skip_group_check=True)
                if started:
                    pe.wait_ge(exp_done, n2 - 1)
                tile(S2A, 0, 0, True, True).then_inc(in_second, 1)
                if started:
                    pe.wait_ge(exp_done, n2)
                tile(S2A + 1, 0, 1, True, False)
                tile(S2A + 1, 3 * P, 3, False, True)
                tile(S2A + 2, 0, 2, True, True).then_inc(in_second, 1)

            EXC = [0, BANK, 2 * BANK, BANK + 3 * P]

            def out_part(b, gr, j, par):
                if j == 0:
                    pe.wait_ge(masked, b * H + (gr + 1) * NG)
                    if gr == 0:
                        pe.wait_ge(v_ready, b + 1)
                    if not (isinstance(b, int) and b == 0 and gr == 0):
                        pe.wait_ge(oT_ready, b * NG + gr)
                for g in range(NG):
                    h = gr * NG + g
                    last = nc.tensor.matmul(PS[g * VW:(g + 1) * VW, OUTB, j * P:S], v[:, par, j, h, :],
                                            ex[:, h % HALF, EXC[j]:EXC[j] + S - j * P],
                                            start=(j == 0), stop=(j == T - 1), skip_group_check=True)
                if j == T - 1:
                    last.then_inc(in_out, 1)

            def run_use(name, b, k):
                if not (isinstance(k, int) and k == 0):
                    pe.wait_ge(misc_taken, k)
                if name == "xnT":
                    pe.wait_ge(ln_done, b + 1)
                    for i in range(T):
                        last = nc.tensor.transpose(misc[:, i * P:(i + 1) * P], xn[:, i, :], ident[:, :])
                elif name == "proj":
                    last = nc.tensor.matmul(misc, w4[:, :, :, :].rearrange("p a h d -> p (a h d)"), xnT[:, :],
                                            start=True, stop=True)
                elif name[0] == "v":
                    i = int(name[1])
                    last = nc.tensor.matmul(misc[:, 0:C], xnT[:, i * P:(i + 1) * P], wv[:, :], start=True, stop=True)
                elif name in ("c0", "c1"):
                    hf = int(name[1])
                    pe.wait_ge(max_done, (b * H + (hf + 1) * HALF) * 4)
                    for i in range(T):
                        last = nc.tensor.transpose(misc[0:HALF, i * P:(i + 1) * P], nmax[:, hf, i, :], ident[:, :])
                elif name[:4] == "back":
                    pe.wait_ge(oT_ready, b * NG + int(name[4]) + 1)
                    for i in range(T):
                        last = nc.tensor.transpose(misc[:, i * P:(i + 1) * P], oT[:, i * P:(i + 1) * P], ident[:, :])
                elif name == "turn":
                    for i in range(T):
                        last = nc.tensor.transpose(misc[:, i * P:(i + 1) * P], att[:, i, :], ident[:, :])
                elif name == "out":
                    for i in range(T):
                        last = nc.tensor.matmul(misc[:, i * P:(i + 1) * P], attT[:, i * P:(i + 1) * P], wo[:, :],
                                                start=True, stop=True)
                last.then_inc(in_misc, 1)

            pe.wait_ge(w4_ready, 1)
            pe.wait_ge(consts_ready, 5)
            for k, name in enumerate(START):
                run_use(name, 0, k)

            def step(n, k):
                m = misc_base(n, k)
                us = plan(k)
                for h in range(H):
                    if k + 1 < B:
                        first(n + 1, h, (k + 1) % 2)
                    if 0 <= k < B:
                        second(n, h, k % 2)
                    if h >= NG and 0 <= k < B:
                        out_part(n, h // NG - 1, h % NG, k % 2)
                    elif h < NG and 1 <= k <= B:
                        out_part(n - 1, NG - 1, h % NG, (k - 1) % 2)
                    for name in us[h]:
                        run_use(name, batch_of(name, n), m)
                        m = m + 1

            steps_of(step, pe.Fori)

        @block.vector
        def _(dve):
            def maxima(b, h):
                n4, n3, hf, hh = (b * H + h) * 4, (b * H + h) * 3, h // HALF, h % HALF

                def reduce(bank, c0, i):
                    nc.vector.tensor_reduce(nmax[:, hf, i, hh:hh + 1], PS[:, bank, c0:c0 + (i + 1) * P], AX.X, ALU.max,
                                            negate=True).then_inc(max_done, 1)
                dve.wait_ge(in_first, n3 + 1)
                reduce(S1A, 0, 3)
                dve.wait_ge(in_first, n3 + 2)
                reduce(S1B, 0, 2)
                reduce(S1B, 3 * P, 0)
                dve.wait_ge(in_first, n3 + 3)
                reduce(S1C, 0, 1)

            def stats_of(own, b):
                layernorm_stats(nc, own, X[:, b], stats, mv, var_eps).then_inc(ln_var, 1)

            def xn_of(b):
                dve.wait_ge(ln_rstd, b + 1)
                layernorm_apply(nc, X[:, b], xn, mv, rstd).then_inc(ln_done, 1)

            def without_first(b):
                dve.wait_ge(part1_ready, b + 1)
                nc.vector.tensor_tensor(rest[:, :], misc, parts[:, 0, :], ALU.subtract).then_inc(misc_taken, 1)

            def third_part(b):
                dve.wait_ge(part2_ready, b + 1)
                nc.vector.tensor_tensor(parts[:, 2, :], rest[:, :], parts[:, 1, :],
                                        ALU.subtract).then_inc(part3_ready, 1)

            def run_use(own, name, b, k):
                if name in ("c0", "c1"):
                    n = b * 2 + int(name[1])
                    dve.wait_ge(c_part1, n + 1)
                    nc.vector.tensor_tensor(crest[0:HALF, :], misc[0:HALF, :], cparts[0:HALF, 0, :],
                                            ALU.subtract).then_inc(misc_taken, 1)
                elif name[:4] == "back":
                    gr = int(name[4])
                    dve.wait_ge(in_misc, k + 1)
                    o = misc.rearrange("p (i g w) -> p i g w", i=T, g=NG)
                    own.only(nc.vector.reciprocal(rz[:, :, :], o[:, :, :, HD]))
                    ins = nc.vector.tensor_tensor(
                        att[:, :, gr * NG * HD:(gr + 1) * NG * HD].rearrange("p i (g w) -> p i g w", g=NG),
                        o[:, :, :, 0:HD],
                        rz[:, :, :].rearrange("p i (g a) -> p i g a", a=1).to_broadcast([P, T, NG, HD]), ALU.mult)
                    ins.then_inc(misc_taken, 1)
                elif name == "out":
                    dve.wait_ge(in_misc, k + 1)
                    nc.vector.tensor_tensor(X[:, b, :, :], misc.rearrange("p (i n) -> p i n", i=T), X[:, b, :, :],
                                            ALU.add).then_inc(misc_taken, 1)

            def n_steps(k):
                names = [u for us in plan(k).values() for u in us]
                return sum(u[:4] == "back" for u in names) + (LN_STEPS if k + 2 < B else 0)

            own = Chain(dve, dve_steps, 0)
            stats_of(own, 0)
            nc.vector.memset(qx[:, 0, :, :], 0.0).then_inc(consts_ready, 1)
            xn_of(0)
            dve.wait_ge(w_loaded, 16 * N_LOADS)
            for a, w3 in enumerate((wq3, wk3)):
                own.ran(nc.vector.tensor_tensor(wdir[:, a], w3[:, :, :], dirs[:, :, :], ALU.mult))
            own.ran(nc.vector.tensor_scalar(w4[:, 0, :, 0:3], wq3[:, :, :], scale_sb[:, 0:1], None, ALU.mult))
            own.ran(nc.vector.tensor_copy(w4[:, 1, :, 0:3], wk3[:, :, :]))
            own.sync()
            nc.vector.tensor_reduce(w4[:, :, :, 3], wdir[:, :, :, :], AX.X, ALU.add).then_inc(w4_ready, 1)
            without_first(0)
            third_part(0)
            nc.vector.memset(qx[:, 1, :, :], 0.0).then_inc(odd_q_zeroed, 1)
            n_start = own.n

            def step(n, k):
                if isinstance(n, int):
                    base = n_start + sum(n_steps(m) for m in range(-1, n))
                else:
                    base = (n - 1) * n_steps(1) + n_start + sum(n_steps(m) for m in range(-1, 1))
                own = Chain(dve, dve_steps, base)
                m = misc_base(n, k)
                us = plan(k)
                for h in range(H):
                    if k + 1 < B:
                        maxima(n + 1, h)
                    if k + 2 < B:
                        if h == 0:
                            stats_of(own, n + 2)
                        if h == 1:
                            xn_of(n + 2)
                        if h == 4:
                            without_first(n + 2)
                        if h == 5:
                            third_part(n + 2)
                    for name in us[h]:
                        run_use(own, name, batch_of(name, n), m)
                        m = m + 1
                assert own.n == n_steps(k), (k, own.n, n_steps(k))

            steps_of(step, dve.Fori)


def phase_expert_choice(nc, X, PS, ident, gate_w, gate_b, w1, w2, out):
    E, HID, TOP = 32, w1.shape[2], 8
    GB = P // E
    NGR = B // GB
    EG = E // GB
    BW = 32
    CH = HID // P
    HALF_S = -0.5
    with ExitStack() as ctx:
        def sb(name, shape):
            return ctx.enter_context(nc.sbuf_tensor("d_" + name, shape, F32))

        def sem(name):
            return ctx.enter_context(nc.semaphore("d_" + name))

        w1_sb, w2_sb = sb("w1", [P, E, HID]), sb("w2", [P, E, CH * C])
        b1, b2 = sb("b1", [P, HID]), sb("b2", [P, C])
        gw, gwT, gb = sb("gw", [E, C]), sb("gwT", [P, E]), sb("gb", [P, 1])
        half = sb("half", [P, 1])
        NT = GB * T
        stats, mv = sb("stats", [P, NT, 6]), sb("mv", [P, NT, 2])
        var_eps, rstd = sb("var_eps", [P, NT]), sb("rstd", [P, NT])
        xn_even, xnT = sb("xn_even", [P, NT, C]), sb("xnT", [P, GB, S])
        xn_odd = w2_sb[:, E - GB:E, :].rearrange("p e (i c) -> p (e i) c", c=C)
        xn = (xn_even, xn_odd)
        logit, nmax, total = sb("logit", [P, S]), sb("nmax", [P, 1]), sb("total", [P, 1])
        expo, rtotal, top = sb("expo", [P, S]), sb("rtotal", [P, 1]), sb("top", [P, TOP])
        picked, chosen = sb("picked", [P, S]), sb("chosen", [P, NGR, S])
        chosenT, merged = sb("chosenT", [P, T, P]), sb("merged", [P, C])
        mT = sb("mT", [P, E, BW])
        hid, hidT = sb("hid", [P, HID]), sb("hidT", [P, CH, P])
        res = sb("res", [P, 2, C])
        resT = logit[:, :].rearrange("p (b e) -> p b e", b=B)
        spread = xn_even[:, :, :].rearrange("p (g b) c -> p g b c", g=NGR)

        small_loaded, gw_turned, gwT_ready = sem("small_loaded"), sem("gw_turned"), sem("gwT_ready")
        w1_loaded = [sem("w1_loaded%d" % g) for g in range(EG)]
        w2_loaded = [sem("w2_loaded%d" % g) for g in range(EG)]
        zeroed, dve_steps = sem("zeroed"), sem("dve_steps")
        ln_var, ln_rstd, ln_done = sem("ln_var"), sem("ln_rstd"), sem("ln_done")
        in_xnT, xnT_ready = sem("in_xnT"), sem("xnT_ready")
        in_gate, nmax_ready, exp_ready, picked_ready = (
            sem("in_gate"), sem("nmax_ready"), sem("exp_ready"), sem("picked_ready"))
        chosen_kept = sem("chosen_kept")
        in_turned, turned_ready, in_merged, merged_ready = (
            sem("in_turned"), sem("turned_ready"), sem("in_merged"), sem("merged_ready"))
        in_mT, mT_ready = sem("in_mT"), sem("mT_ready")
        in_hid, hid_ready, in_hidT, hidT_ready = sem("in_hid"), sem("hid_ready"), sem("in_hidT"), sem("hidT_ready")
        in_res, res_ready, in_resT, resT_ready = sem("in_res"), sem("res_ready"), sem("in_resT"), sem("resT_ready")
        in_placed, spread_ready = sem("in_placed"), sem("spread_ready")
        in_back, added, stored = sem("in_back"), sem("added"), sem("stored")
        N_SMALL = 3 + GB

        block = ctx.enter_context(nc.Block())

        @block.sync
        def _(sp):
            sp.dma_start(gw[:, :], gate_w).then_inc(small_loaded, 16)
            for g in range(GB):
                sp.dma_start(gb[g * E:(g + 1) * E, :], gate_b.rearrange("(e a) -> e a", a=1)).then_inc(small_loaded, 16)
            sp.wait_ge(zeroed, 2)
            sp.dma_start(b1[0:E, :], w1[:, C, :]).then_inc(small_loaded, 16)
            sp.dma_start(b2[0:E, :], w2[:, HID, :]).then_inc(small_loaded, 16)
            for g in range(EG):
                e = slice(g * GB, (g + 1) * GB)
                sp.dma_start(w1_sb[:, e, :], w1[e, 0:C, :].rearrange("e d h -> d e h")).then_inc(w1_loaded[g], 16)
                if g == EG - 1:
                    sp.wait_ge(in_merged, NGR)
                sp.dma_start(w2_sb[:, e, :], w2[e, 0:HID, :].rearrange("e (p c) o -> p e (c o)", c=CH)).then_inc(w2_loaded[g], 16)
            with sp.Fori(0, NGR) as g:
                sp.wait_ge(added, g * T + T)
                for b in range(GB):
                    sp.dma_start(out[g * GB + b].rearrange("(i p) c -> p i c", p=P), X[:, g * GB + b, :, :]).then_inc(stored, 16)
            sp.wait_ge(stored, 16 * B)

        @block.gpsimd
        def _(pool):
            nc.gpsimd.memset(b1[:, :], 0.0).then_inc(zeroed, 1)
            nc.gpsimd.memset(b2[:, :], 0.0).then_inc(zeroed, 1)
            nc.gpsimd.memset(half[:, :], HALF_S).then_inc(zeroed, 1)
            nc.gpsimd.memset(mT[:, :, :], 0.0).then_inc(zeroed, 1)
            pool.wait_ge(zeroed, 4)
            def rstd_of(g):
                pool.wait_ge(ln_var, g + 1)
                if g:
                    pool.wait_ge(ln_done, g * GB)
                nc.gpsimd.tensor_tensor(rstd[:, :], var_eps[:, :], half[:, 0:1].to_broadcast([P, NT]),
                                        ALU.pow).then_inc(ln_rstd, 1)

            rstd_of(0)
            rstd_of(1)
            for g in range(NGR):
                if g == NGR - 1:
                    pool.wait_ge(in_merged, NGR - 1)
                    nc.gpsimd.memset(xn_even[:, :, :], 0.0).then_inc(zeroed, 1)
                pool.wait_ge(picked_ready, g + 1)
                nc.gpsimd.tensor_copy(chosen[:, g, :], picked[:, :]).then_inc(chosen_kept, 1)
                if g + 2 < NGR:
                    rstd_of(g + 2)

        @block.scalar
        def _(act):
            act.wait_ge(gw_turned, 1)
            nc.scalar.activation(gwT[:, :], PS[:, 7, 0:E], ACT.Copy).then_inc(gwT_ready, 1)
            for g in range(NGR):
                for b in range(GB):
                    act.wait_ge(in_xnT, g * GB + b + 1)
                    nc.scalar.activation(xnT[:, b, :], PS[:, b, :], ACT.Copy).then_inc(xnT_ready, 1)
                act.wait_ge(nmax_ready, g + 1)
                nc.scalar.activation(expo[:, :], logit[:, :], ACT.Exp, bias=nmax[:, 0:1],
                                     accum_out=total[:, 0:1]).then_inc(exp_ready, 1)
                act.wait_ge(in_turned, g + 1)
                nc.scalar.activation(chosenT[:, :, :].rearrange("p i n -> p (i n)"), PS[:, 5, :], ACT.Copy).then_inc(turned_ready, 1)
                act.wait_ge(in_merged, g + 1)
                nc.scalar.activation(merged[:, :], PS[:, 6, 0:C], ACT.Copy).then_inc(merged_ready, 1)
            def take_resT(g):
                act.wait_ge(in_resT, g + 1)
                nc.scalar.activation(resT[:, :, g * GB:(g + 1) * GB].rearrange("p b e -> p e b"),
                                     PS[:, 4, 0:P].rearrange("p (e b) -> p e b", b=BW)[:, :, 0:B], ACT.Copy).then_inc(resT_ready, 1)

            for g in range(EG):
                act.wait_ge(in_hid, g + 1)
                if g:
                    act.wait_ge(in_hidT, g)
                nc.scalar.activation(hid[:, :], PS[:, g % 2, :], ACT.Gelu).then_inc(hid_ready, 1)
                if g:
                    take_resT(g - 1)
            take_resT(EG - 1)
            for g in range(NGR):
                act.wait_ge(in_placed, g + 1)
                if g == 0:
                    act.wait_ge(zeroed, 5)
                for b in range(GB):
                    rows = slice(b * E, (b + 1) * E)
                    last = nc.scalar.activation(spread[rows, g, b, :], PS[rows, 4 + g, 0:C], ACT.Copy)
                last.then_inc(spread_ready, 1)

        @block.tensor
        def _(pe):
            pe.wait_ge(small_loaded, 16 * N_SMALL)
            nc.tensor.transpose(PS[:, 7, 0:E], gw[:, :], ident[0:E, 0:E]).then_inc(gw_turned, 1)
            pe.wait_ge(gwT_ready, 1)
            for g in range(NGR):
                for b in range(GB):
                    pe.wait_ge(ln_done, g * GB + b + 1)
                    for i in range(T):
                        last = nc.tensor.transpose(PS[:, b, i * P:(i + 1) * P], xn[g % 2][:, b * T + i, :], ident[:, :])
                    last.then_inc(in_xnT, 1)
                pe.wait_ge(xnT_ready, g * GB + GB)
                for b in range(GB):
                    last = nc.tensor.matmul(PS[b * E:(b + 1) * E, 4, :], gwT[:, :], xnT[:, b, :], start=True, stop=True)
                last.then_inc(in_gate, 1)
                pe.wait_ge(picked_ready, g + 1)
                for i in range(T):
                    last = nc.tensor.transpose(PS[:, 5, i * P:(i + 1) * P], picked[:, i * P:(i + 1) * P], ident[:, :])
                last.then_inc(in_turned, 1)
                pe.wait_ge(turned_ready, g + 1)
                for i in range(T):
                    for b in range(GB):
                        last = nc.tensor.matmul(PS[b * E:(b + 1) * E, 6, 0:C], chosenT[:, i, b * E:(b + 1) * E],
                                                xn[g % 2][:, b * T + i, :], start=(i == 0), stop=(i == T - 1), skip_group_check=True)
                last.then_inc(in_merged, 1)
                pe.wait_ge(merged_ready, g + 1)
                nc.tensor.transpose(PS[:, 7, 0:P], merged[:, :], ident[:, :]).then_inc(in_mT, 1)

            def hidden(g):
                if g == 0:
                    pe.wait_ge(mT_ready, NGR)
                pe.wait_ge(w1_loaded[g], 16)
                if g >= 2:
                    pe.wait_ge(hid_ready, g - 1)
                for e4 in range(GB):
                    nc.tensor.matmul(PS[e4 * BW:(e4 + 1) * BW, g % 2, :], mT[:, g * GB + e4, :], w1_sb[:, g * GB + e4, :],
                                     start=True, stop=False, skip_group_check=True)
                for e4 in range(GB):
                    e = g * GB + e4
                    last = nc.tensor.matmul(PS[e4 * BW:(e4 + 1) * BW, g % 2, :], ident[:, e:e + 1].to_broadcast([P, BW]),
                                            b1[:, :], start=False, stop=True, skip_group_check=True)
                last.then_inc(in_hid, 1)

            def turn_hidden(g):
                pe.wait_ge(hid_ready, g + 1)
                if g:
                    pe.wait_ge(hidT_ready, g)
                for c in range(CH):
                    last = nc.tensor.transpose(PS[:, 2, c * P:(c + 1) * P], hid[:, c:HID:CH], ident[:, :])
                last.then_inc(in_hidT, 1)

            def result(g):
                pe.wait_ge(hidT_ready, g + 1)
                pe.wait_ge(w2_loaded[g], 16)
                if g:
                    pe.wait_ge(res_ready, g)
                for c in range(CH):
                    for e4 in range(GB):
                        nc.tensor.matmul(PS[e4 * BW:(e4 + 1) * BW, 3, 0:C], hidT[:, c, e4 * BW:(e4 + 1) * BW],
                                         w2_sb[:, g * GB + e4, c * C:(c + 1) * C],
                                         start=(c == 0), stop=False, skip_group_check=True)
                for e4 in range(GB):
                    e = g * GB + e4
                    last = nc.tensor.matmul(PS[e4 * BW:(e4 + 1) * BW, 3, 0:C], ident[:, e:e + 1].to_broadcast([P, BW]),
                                            b2[:, :], start=False, stop=True, skip_group_check=True)
                last.then_inc(in_res, 1)

            hidden(0)
            def turn_result(g):
                pe.wait_ge(res_ready, g + 1)
                if g:
                    pe.wait_ge(resT_ready, g)
                nc.tensor.transpose(PS[:, 4, 0:P], res[:, g % 2, :], ident[:, :]).then_inc(in_resT, 1)

            for g in range(EG):
                turn_hidden(g)
                if g + 1 < EG:
                    hidden(g + 1)
                if g:
                    turn_result(g - 1)
                result(g)
            turn_result(EG - 1)
            pe.wait_ge(resT_ready, EG)
            for g in range(NGR):
                nc.tensor.transpose(PS[:, 4 + g, 0:C], resT[:, g * GB:(g + 1) * GB, :].rearrange("p b e -> p (b e)"),
                                    ident[:, :]).then_inc(in_placed, 1)

            pe.wait_ge(chosen_kept, NGR)
            for g in range(NGR):
                pe.wait_ge(spread_ready, g + 1)
                for i in range(T):
                    n = g * T + i
                    if n >= 4:
                        pe.wait_ge(added, n - 3)
                    nc.tensor.matmul(PS[:, n % 4, :], chosen[:, g, i * P:(i + 1) * P],
                                     spread[:, g, :, :].rearrange("p b c -> p (b c)"),
                                     start=True, stop=True).then_inc(in_back, 1)

        @block.vector
        def _(dve):
            own = Chain(dve, dve_steps, 0)

            def token_stats(g):
                for n in range(NT):
                    own.ran(nc.vector.bn_stats(stats[:, n, :], X[:, g * GB + n // T, n % T, :]))
                own.sync()
                for n in range(NT):
                    own.ran(nc.vector.bn_aggr(mv[:, n, :], stats[:, n, :]))
                own.sync()
                nc.vector.tensor_scalar(var_eps[:, :], mv[:, :, 1], LN_EPS, None, ALU.add).then_inc(ln_var, 1)

            def normalise(g):
                dve.wait_ge(ln_rstd, g + 1)
                if g >= 2:
                    dve.wait_ge(in_merged, g - 1)
                for n in range(NT):
                    last = nc.vector.tensor_scalar(xn[g % 2][:, n, :], X[:, g * GB + n // T, n % T, :], mv[:, n, 0:1],
                                                   rstd[:, n:n + 1], ALU.subtract, ALU.mult)
                    if n % T == T - 1:
                        last.then_inc(ln_done, 1)

            def choose(g):
                dve.wait_ge(in_gate, g + 1)
                own.only(nc.vector.tensor_scalar(logit[:, :], PS[:, 4, :], gb[:, 0:1], None, ALU.add))
                nc.vector.tensor_reduce(nmax[:, 0:1], logit[:, :], AX.X, ALU.max, negate=True).then_inc(nmax_ready, 1)
                dve.wait_ge(exp_ready, g + 1)
                own.only(nc.vector.reciprocal(rtotal[:, :], total[:, :]))
                own.only(nc.vector.tensor_scalar(expo[:, :], expo[:, :], rtotal[:, 0:1], None, ALU.mult))
                own.only(nc.vector.max(top[:, :], expo[:, :]))
                if g:
                    dve.wait_ge(chosen_kept, g)
                own.only(nc.vector.match_replace(picked[:, :], top[:, :], expo[:, :], 0.0))
                nc.vector.tensor_tensor(picked[:, :], expo[:, :], picked[:, :], ALU.subtract).then_inc(picked_ready, 1)

            def take_mT(g):
                dve.wait_ge(in_mT, g + 1)
                for b in range(GB):
                    last = nc.vector.tensor_copy(mT[:, :, g * GB + b], PS[:, 7, b * E:(b + 1) * E])
                last.then_inc(mT_ready, 1)

            token_stats(0)
            normalise(0)
            dve.wait_ge(small_loaded, 16 * N_SMALL)
            dve.wait_ge(zeroed, 4)
            token_stats(1)
            for g in range(NGR):
                choose(g)
                if g + 1 < NGR:
                    normalise(g + 1)
                take_mT(g)
                if g + 2 < NGR:
                    token_stats(g + 2)
            for g in range(EG):
                dve.wait_ge(in_hidT, g + 1)
                if g:
                    dve.wait_ge(in_res, g)
                nc.vector.tensor_copy(hidT[:, :, :].rearrange("p c n -> p (c n)"), PS[:, 2, :]).then_inc(hidT_ready, 1)
                dve.wait_ge(in_res, g + 1)
                if g >= 2:
                    dve.wait_ge(in_resT, g - 1)
                nc.vector.tensor_copy(res[:, g % 2, :], PS[:, 3, 0:C]).then_inc(res_ready, 1)
            for g in range(NGR):
                for i in range(T):
                    n = g * T + i
                    dve.wait_ge(in_back, n + 1)
                    xs = X[:, g * GB:(g + 1) * GB, i, :]
                    nc.vector.tensor_tensor(xs, PS[:, n % 4, :].rearrange("p (b c) -> p b c", b=GB), xs,
                                            ALU.add).then_inc(added, 1)


def program(nc, x, Wqkv, bqkv, gamma_q, beta_q, gamma_k, beta_k, Wo0, Wq, Wk, Ws, Wd, Wv, Wo1,
            wq, wk, wv, wo, head_dirs, scale, gate_w, gate_b, w1, w2, bo, out):
    with (nc.sbuf_tensor("x", [P, B, T, C], F32) as X, nc.sbuf_tensor("ident", [P, P], F32) as ident,
          nc.psum_tensor("banks", [P, 8, BANK], F32) as PS):
        phase_linear_attention(nc, X, PS, ident, x, Wqkv, bqkv, gamma_q, beta_q, gamma_k, beta_k, Wo0, bo)
        phase_head_mixture(nc, X, PS, ident, Wq, Wk, Ws, Wd, Wv, Wo1)
        phase_geometric_attention(nc, X, PS, ident, wq, wk, wv, wo, head_dirs, scale)
        phase_expert_choice(nc, X, PS, ident, gate_w, gate_b, w1, w2, out)


_INS = ["L0_attn_x", "L0_attn_Wqkv", "L0_attn_bqkv", "L0_attn_gamma_q", "L0_attn_beta_q", "L0_attn_gamma_k",
        "L0_attn_beta_k", "L0_attn_Wo", "L0_ffn_Wq", "L0_ffn_Wk", "L0_ffn_Ws", "L0_ffn_Wd", "L0_ffn_Wv",
        "L0_ffn_Wo", "L1_attn_wq", "L1_attn_wk", "L1_attn_wv", "L1_attn_wo", "L1_attn_head_dirs",
        "L1_attn_scale", "L1_ffn_gate_w", "L1_ffn_gate_b", "L1_ffn_w1", "L1_ffn_w2", "L0_attn_bo"]


def kernel(**inputs):
    import numpy as np
    import concourse.bacc as bacc
    from concourse.bass_utils import run_bass_kernel_spmd

    nc = bacc.Bacc("TRN2", target_bir_lowering=False, num_devices=1)
    arrays, args = {}, []
    for name in _INS:
        a = np.ascontiguousarray(inputs[name])
        arrays["in_" + name] = a
        args.append(nc.dram_tensor("in_" + name, a.shape, mybir.dt.from_np(a.dtype), kind="ExternalInput").ap())
    out = nc.dram_tensor("out", (B, S, C), F32, kind="ExternalOutput").ap()
    program(nc, *args, out)
    r = run_bass_kernel_spmd(nc, [arrays], core_ids=[0])
    return r.results[0]["out"]
```
